# Optimizing a Trainium2 kernel written in Bass

```python
import numpy as np
import jax
import jax.numpy as jnp

def _softmax(x, axis=-1):
    return jax.nn.softmax(x, axis=axis)

def _gelu(x):
    return jax.nn.gelu(x, approximate=True)

def _silu(x):
    return jax.nn.silu(x)

def _sigmoid(x):
    return jax.nn.sigmoid(x)

def _layernorm(x, axis=-1, eps=1e-05):
    m = jnp.mean(x, axis=axis, keepdims=True)
    v = jnp.var(x, axis=axis, keepdims=True)
    return (x - m) / jnp.sqrt(v + eps)

def _scatter_add(tgt, idx, src, axis=0):
    return tgt.at[idx].add(src)

def _segment_sum(src, seg, n):
    return jax.ops.segment_sum(src, seg, n)
kernel_name = 'mk_adaln_d1_jaxref_r4_7f7c75'

def setup_inputs(seed: int=0):
    np.random.seed(seed)
    _w = jnp.asarray

    def _L0_attn_setup():
        import jax, jax.numpy as jnp
        import numpy as np
        LN_EPS = 1e-05

        def _forward(x, Wk, Wv, Wo, Wts, gate, time_decay, time_first, ln_w, ln_b):
            B, T, D = x.shape
            shift_len = max(1, int(T * 0.5))
            x_cat = jnp.roll(x, -shift_len, axis=1)
            g = jax.nn.sigmoid(gate)
            x_shift = jnp.einsum('btd,ed->bte', x_cat, Wts) * g + x * (1.0 - g)
            mu = x_shift.mean(-1, keepdims=True)
            var = jnp.mean((x_shift - mu) ** 2, -1, keepdims=True)
            xn = (x_shift - mu) * jax.lax.rsqrt(var + LN_EPS) * ln_w + ln_b
            k = jnp.einsum('btd,sd->bts', xn, Wk)
            v = jnp.einsum('btd,sd->bts', xn, Wv)
            w = jnp.exp(time_decay)
            wkv = jnp.exp(-jnp.exp(time_first) * jax.nn.sigmoid(k)) * v

            def step(s, wkv_t):
                s = s * w + wkv_t
                return (s, s)
            init = jnp.zeros((B, wkv.shape[-1]), x.dtype)
            last_state, states = jax.lax.scan(step, init, jnp.swapaxes(wkv, 0, 1))
            states = jnp.swapaxes(states, 0, 1)
            out = jnp.einsum('bts,ds->btd', states, Wo)
            return (out, last_state)

        def _reference_tuple_inner(x, Wk, Wv, Wo, Wts, gate, time_decay, time_first, ln_w, ln_b):
            out, last_state = _forward(x, Wk, Wv, Wo, Wts, gate, time_decay, time_first, ln_w, ln_b)
            return (out, jax.lax.stop_gradient(last_state))
        key = jax.random.key(seed)
        ks = jax.random.split(key, 8)
        B, T, D, S = (8, 1024, 512, 64)
        x = jax.random.normal(ks[0], (B, T, D), jnp.float32)
        Wk = jax.random.normal(ks[1], (S, D), jnp.float32) * 0.02
        Wv = jax.random.normal(ks[2], (S, D), jnp.float32) * 0.02
        Wo = jax.random.normal(ks[3], (D, S), jnp.float32) * 0.02
        Wts = jax.random.normal(ks[4], (D, D), jnp.float32) * 0.02
        gate = jax.random.normal(ks[5], (D,), jnp.float32) * 0.1 + 1.0
        time_decay = jax.random.normal(ks[6], (S,), jnp.float32) * 0.1 - 0.5
        time_first = jax.random.normal(ks[7], (S,), jnp.float32) * 0.1
        ln_w = jnp.ones((D,), jnp.float32)
        ln_b = jnp.zeros((D,), jnp.float32)
        return dict(x=x, Wk=Wk, Wv=Wv, Wo=Wo, Wts=Wts, gate=gate, time_decay=time_decay, time_first=time_first, ln_w=ln_w, ln_b=ln_b)
    _L0_attn_in = _L0_attn_setup()

    def _L0_ffn_setup():
        import jax, jax.numpy as jnp
        import numpy as np
        B, S, H = (1, 256, 512)
        E, K = (32, 4)
        F, FS = (352, 1408)
        CAP = 64

        def silu(x):
            return x * jax.nn.sigmoid(x)
        key = jax.random.key(seed)
        ks = jax.random.split(key, 9)
        sc = 0.02
        return {'hidden_states': jax.random.normal(ks[0], (B, S, H), jnp.float32), 'Wr': jax.random.normal(ks[1], (H, E), jnp.float32) * sc, 'Wg': jax.random.normal(ks[2], (E, H, F), jnp.float32) * sc, 'Wu': jax.random.normal(ks[3], (E, H, F), jnp.float32) * sc, 'Wd': jax.random.normal(ks[4], (E, F, H), jnp.float32) * sc, 'Wsg': jax.random.normal(ks[5], (H, FS), jnp.float32) * sc, 'Wsu': jax.random.normal(ks[6], (H, FS), jnp.float32) * sc, 'Wsd': jax.random.normal(ks[7], (FS, H), jnp.float32) * sc, 'Wse': jax.random.normal(ks[8], (H, 1), jnp.float32) * sc}
    _L0_ffn_in = _L0_ffn_setup()
    _L0_c = _w((lambda *s: np.random.randn(*s).astype(np.float32) * 0.05)(2, 512))
    _L0_wmod = _w((lambda *s: np.random.randn(*s).astype(np.float32) * 0.05)(512, 6 * 512) * 512 ** (-0.5))
    _d = {'L0_attn_x': _L0_attn_in['x'], 'L0_attn_Wk': _L0_attn_in['Wk'], 'L0_attn_Wv': _L0_attn_in['Wv'], 'L0_attn_Wo': _L0_attn_in['Wo'], 'L0_attn_Wts': _L0_attn_in['Wts'], 'L0_attn_gate': _L0_attn_in['gate'], 'L0_attn_time_decay': _L0_attn_in['time_decay'], 'L0_attn_time_first': _L0_attn_in['time_first'], 'L0_attn_ln_w': _L0_attn_in['ln_w'], 'L0_attn_ln_b': _L0_attn_in['ln_b'], 'L0_ffn_Wr': _L0_ffn_in['Wr'], 'L0_ffn_Wg': _L0_ffn_in['Wg'], 'L0_ffn_Wu': _L0_ffn_in['Wu'], 'L0_ffn_Wd': _L0_ffn_in['Wd'], 'L0_ffn_Wsg': _L0_ffn_in['Wsg'], 'L0_ffn_Wsu': _L0_ffn_in['Wsu'], 'L0_ffn_Wsd': _L0_ffn_in['Wsd'], 'L0_ffn_Wse': _L0_ffn_in['Wse'], 'L0_c': _L0_c, 'L0_wmod': _L0_wmod}
    _x0 = _d['L0_attn_x']
    _d['L0_attn_x'] = jax.random.normal(jax.random.fold_in(jax.random.key(seed), 1), (2, 1024, 512), dtype=_x0.dtype)
    del _x0
    return _d

def reference(L0_attn_x, L0_attn_Wk, L0_attn_Wv, L0_attn_Wo, L0_attn_Wts, L0_attn_gate, L0_attn_time_decay, L0_attn_time_first, L0_attn_ln_w, L0_attn_ln_b, L0_ffn_Wr, L0_ffn_Wg, L0_ffn_Wu, L0_ffn_Wd, L0_ffn_Wsg, L0_ffn_Wsu, L0_ffn_Wsd, L0_ffn_Wse, L0_c, L0_wmod):

    def _L0_attn_ref(x, Wk, Wv, Wo, Wts, gate, time_decay, time_first, ln_w, ln_b):
        import jax, jax.numpy as jnp
        import numpy as np
        LN_EPS = 1e-05

        def _forward(x, Wk, Wv, Wo, Wts, gate, time_decay, time_first, ln_w, ln_b):
            B, T, D = x.shape
            shift_len = max(1, int(T * 0.5))
            x_cat = jnp.roll(x, -shift_len, axis=1)
            g = jax.nn.sigmoid(gate)
            x_shift = jnp.einsum('btd,ed->bte', x_cat, Wts) * g + x * (1.0 - g)
            mu = x_shift.mean(-1, keepdims=True)
            var = jnp.mean((x_shift - mu) ** 2, -1, keepdims=True)
            xn = (x_shift - mu) * jax.lax.rsqrt(var + LN_EPS) * ln_w + ln_b
            k = jnp.einsum('btd,sd->bts', xn, Wk)
            v = jnp.einsum('btd,sd->bts', xn, Wv)
            w = jnp.exp(time_decay)
            wkv = jnp.exp(-jnp.exp(time_first) * jax.nn.sigmoid(k)) * v

            def step(s, wkv_t):
                s = s * w + wkv_t
                return (s, s)
            init = jnp.zeros((B, wkv.shape[-1]), x.dtype)
            last_state, states = jax.lax.scan(step, init, jnp.swapaxes(wkv, 0, 1))
            states = jnp.swapaxes(states, 0, 1)
            out = jnp.einsum('bts,ds->btd', states, Wo)
            return (out, last_state)

        def _reference_tuple_inner(x, Wk, Wv, Wo, Wts, gate, time_decay, time_first, ln_w, ln_b):
            out, last_state = _forward(x, Wk, Wv, Wo, Wts, gate, time_decay, time_first, ln_w, ln_b)
            return (out, jax.lax.stop_gradient(last_state))
        return _reference_tuple_inner(x, Wk, Wv, Wo, Wts, gate, time_decay, time_first, ln_w, ln_b)[0]

    def _L0_ffn_ref(hidden_states, Wr, Wg, Wu, Wd, Wsg, Wsu, Wsd, Wse):
        import jax, jax.numpy as jnp
        import numpy as np
        B, S, H = (1, 256, 512)
        E, K = (32, 4)
        F, FS = (352, 1408)
        CAP = 64

        def silu(x):
            return x * jax.nn.sigmoid(x)
        b, s_len, h = hidden_states.shape
        x = hidden_states.reshape(-1, h)
        T = x.shape[0]
        probs = jax.nn.softmax(x @ Wr, axis=-1)
        topw, topi = jax.lax.top_k(probs, K)
        topw = topw / jnp.sum(topw, axis=-1, keepdims=True)
        shared = silu(x @ Wsg) * (x @ Wsu) @ Wsd
        shared = shared * jax.nn.sigmoid(x @ Wse)
        sel = topi.reshape(-1)
        w = topw.reshape(-1)
        tok = jnp.repeat(jnp.arange(T), K)
        oh = jax.nn.one_hot(sel, E, dtype=jnp.int32)
        pos = (jnp.cumsum(oh, axis=0) * oh).sum(-1) - 1
        valid = (pos < CAP).astype(x.dtype)
        posc = jnp.clip(pos, 0, CAP - 1)
        xe = jnp.zeros((E, CAP, h), x.dtype).at[sel, posc].add(x[tok] * valid[:, None])
        g = silu(jnp.einsum('ech,ehf->ecf', xe, Wg))
        u = jnp.einsum('ech,ehf->ecf', xe, Wu)
        ye = jnp.einsum('ecf,efh->ech', g * u, Wd)
        y_pair = ye[sel, posc] * (w * valid)[:, None]
        out = shared.at[tok].add(y_pair)
        return out.reshape(b, s_len, h)
    x = L0_attn_x
    mod = (_silu(L0_c) @ L0_wmod).reshape(L0_c.shape[0], 6, 1, -1)
    sa, ca, ga, sb, cb, gb = (mod[:, 0], mod[:, 1], mod[:, 2], mod[:, 3], mod[:, 4], mod[:, 5])
    ga = (2 * (ga >= 0) - 1) * jnp.maximum(jnp.abs(ga), 0.25)
    gb = (2 * (gb >= 0) - 1) * jnp.maximum(jnp.abs(gb), 0.25)
    h = _layernorm(x, axis=-1) * (1 + ca) + sa
    x = x + ga * _L0_attn_ref(h, L0_attn_Wk, L0_attn_Wv, L0_attn_Wo, L0_attn_Wts, L0_attn_gate, L0_attn_time_decay, L0_attn_time_first, L0_attn_ln_w, L0_attn_ln_b)
    h = _layernorm(x, axis=-1) * (1 + cb) + sb
    x = x + gb * _L0_ffn_ref(h, L0_ffn_Wr, L0_ffn_Wg, L0_ffn_Wu, L0_ffn_Wd, L0_ffn_Wsg, L0_ffn_Wsu, L0_ffn_Wsd, L0_ffn_Wse)
    return x

_drawn_inputs = setup_inputs


def setup_inputs(seed=0):
    import zlib

    import numpy as np

    out = dict(_drawn_inputs(seed))
    spreads = {'L0_attn_ln_w': (1.0, 0.6), 'L0_attn_ln_b': (0.0, 0.8)}
    factors = {'L0_attn_Wk': 8.0,
     'L0_attn_Wv': 3.708,
     'L0_attn_Wo': 3.675,
     'L0_attn_Wts': 4.872,
     'L0_attn_gate': 64.0,
     'L0_attn_time_decay': 8.0,
     'L0_attn_time_first': 8.0,
     'L0_ffn_Wr': 8.0,
     'L0_ffn_Wg': 8.0,
     'L0_ffn_Wu': 8.0,
     'L0_ffn_Wd': 8.0,
     'L0_ffn_Wsg': 5.52,
     'L0_ffn_Wsu': 5.401,
     'L0_ffn_Wsd': 5.399,
     'L0_ffn_Wse': 8.0,
     'L0_c': 2.992,
     'L0_wmod': 3.046}
    for name, (base, spread) in spreads.items():
        noise = np.random.default_rng([zlib.crc32(name.encode()), seed]).standard_normal(out[name].shape)
        drawn = base * np.exp(spread * noise) if base else spread * noise
        out[name] = jnp.asarray(drawn.astype(out[name].dtype))
    for name, factor in factors.items():
        out[name] = (out[name] * factor).astype(out[name].dtype)
    return out
```

```python
from contextlib import ExitStack

import concourse.bass as bass
from concourse import mybir

F32 = mybir.dt.float32
F32R = mybir.dt.float32r
U32 = mybir.dt.uint32
ALU = mybir.AluOpType
ACT = mybir.ActivationFunctionType
AX = mybir.AxisListType

P = 128
LN_EPS = 1e-5
GATE_FLOOR = 0.25
TOP_K = 4
CAP = 64
FAR = 1 << 16


class Tally:

    def __init__(self, sem, start=0):
        self.sem, self.at, self.n = sem, start, 0

    def loop(self, var, per):
        self.start, self.per = self.at + self.n, per
        self.at, self.n = self.start + var * per, 0

    def end(self, times):
        assert self.n == self.per, (self.sem, self.n, self.per)
        self.at, self.n = self.start + self.per * times, 0

    def tick(self, k=1):
        self.n += k
        return self.at + self.n

    def last(self):
        return self.at + self.n


def row(ap):
    return ap.rearrange("p a n -> p (a n)")


def build(nc, x, Wk, Wv, Wo, Wts, gate, time_decay, time_first, ln_w, ln_b,
          Wr, Wg, Wu, Wd, Wsg, Wsu, Wsd, Wse, c_in, wmod, out):
    B, T, H = x.shape
    S = Wk.shape[0]
    E, _, F = Wg.shape
    FS = Wsg.shape[1]
    C = H // P
    NT = B * T // P
    BT = T // P
    HB = BT // 2
    GT = 4
    GW = GT * P
    NG = NT // GT
    BG = BT // GT
    NP = E // 2
    FC = [(0, P), (P, P), (2 * P, F - 2 * P)]
    PC = 3
    PARTS = [PC, PC, PC, FS // P - 3 * PC]
    PAIR_PARTS = (1, 2)
    R = E + 2
    assert (H, S, C, CAP * 2, BT, NP, FS % P) == (512, 64, 4, P, 8, 16, 0)
    assert len(PAIR_PARTS) * NG * 2 == NP

    h2_dram = nc.dram_tensor("h2_rows", (B * T, H), F32, kind="Internal").ap()
    ye_dram = nc.dram_tensor("expert_rows", (E * CAP, H), F32, kind="Internal").ap()
    tok_dram = nc.dram_tensor("slot_tokens", (E * CAP, 1), U32, kind="Internal").ap()

    x_rows = x.rearrange("b (i p) h -> p (b i) h", p=P)
    out_rows = out.rearrange("b (i p) h -> p (b i) h", p=P)
    wmod_v = wmod.rearrange("(k p) n -> p k n", p=P)

    with ExitStack() as ctx:
        def sb(name, shape, dt=F32, scope=ctx):
            return scope.enter_context(nc.sbuf_tensor(name, shape, dt))

        def sems(names):
            return [ctx.enter_context(nc.semaphore(n)) for n in names.split()]

        xres = sb("xres", [P, NT, H])
        h2T = sb("h2T", [P, C, B * T])
        gate_b = sb("gate_b", [P, B, H])
        ident = sb("ident", [P, P])
        wrN = sb("wrN", [P, C, R])

        bank = [ctx.enter_context(nc.psum_tensor(f"bank{i}", [P, 512], F32)) for i in range(8)]

        with ExitStack() as pa:
            hTH = sb("hTH", [P, C, T], F32R, pa)
            hTL = sb("hTL", [P, C, T], F32R, pa)
            stage = sb("stage", [P, 2, C, 512], F32, pa)
            bc = sb("bc", [P, 4, B, H], F32, pa)
            wtsH = sb("wtsH", [P, C, H], F32R, pa)
            wtsL = sb("wtsL", [P, C, H], F32R, pa)
            xnTH = sb("xnTH", [P, C, GW], F32R, pa)
            xnTL = sb("xnTL", [P, C, GW], F32R, pa)
            xhat = stage[:, :, :, :].rearrange("p a c h -> p (a c) h")
            fT = sb("fT", [P, C, P], F32, pa)
            mix = sb("mix", [P, 2, H], F32, pa)
            h2r = sb("h2r", [P, 2, H], F32, pa)
            xs = sb("xs", [P, H], F32, pa)
            xn = sb("xn", [P, 2, H], F32, pa)
            kE = sb("kE", [S, GW], F32, pa)
            vV = sb("vV", [S, GW], F32, pa)
            states = sb("states", [S, T], F32, pa)
            woT = sb("woT", [S, B, H], F32, pa)
            woS = sb("woS", [P, C, B, S], F32, pa)
            woN = sb("woN", [P, C, S], F32, pa)
            kvH = sb("kvH", [P, C, P], F32R, pa)
            kvL = sb("kvL", [P, C, P], F32R, pa)
            rows = sb("rows", [24, P], F32, pa)
            cols = sb("cols", [P, 24], F32, pa)
            cT = sb("cT", [P, C, B], F32, pa)
            gcol = sb("gcol", [P, 2, C], F32, pa)
            ecol = sb("ecol", [P, 12], F32, pa)
            wcol = sb("wcol", [S, 4], F32, pa)
            modc = sb("modc", [P, 6, C, B], F32, pa)
            dcol = sb("dcol", [P, B, 8, C], F32, pa)
            tmpc = sb("tmpc", [P, 3, C, B], F32, pa)
            st6 = sb("st6", [P, 6], F32, pa)
            mv1 = sb("mv1", [P, BT, 2], F32, pa)
            mv2 = sb("mv2", [P, 2, 2], F32, pa)
            ve = sb("ve", [P, BT], F32, pa)
            ve2 = sb("ve2", [P, 2], F32, pa)
            neg_half = sb("neg_half", [P, BT], F32, pa)
            rs = sb("rs", [P, BT], F32, pa)
            rs2 = sb("rs2", [P, 2], F32, pa)

            (rows_zero, const_ok, cols_in, kv_in, wo_in, wr_in, x_in0, x_in1, stage_in0, stage_in1,
             col_full, col_ok, exp_ok, silu_c_ok, wts_scaled, wo_scaled, split_hi, mod_done,
             t_full0, t_full1, t_taken0, t_taken1, xhat_ok, hT_hi, xnT_hi, lo_done,
             s_full0, s_full1, s_taken0, s_taken1, mix_ok, xn_ok, xhat2_ok, h2_ok, h2_sent, h2_free,
             kv_full, kv_read, e_neg, e_sig, e_fac, st_ok, ve_ok, rs_ok, dve_self, pool_self) = sems(
                 "rows_zero const_ok cols_in kv_in wo_in wr_in x_in0 x_in1 stage_in0 stage_in1 "
                 "col_full col_ok exp_ok silu_c_ok wts_scaled wo_scaled split_hi mod_done "
                 "t_full0 t_full1 t_taken0 t_taken1 xhat_ok hT_hi xnT_hi lo_done "
                 "s_full0 s_full1 s_taken0 s_taken1 mix_ok xn_ok xhat2_ok h2_ok h2_sent h2_free "
                 "kv_full kv_read e_neg e_sig e_fac st_ok ve_ok rs_ok dve_self pool_self")
            x_in, stage_in = (x_in0, x_in1), (stage_in0, stage_in1)

            tb, sbk, kvb, modb = bank[0:2], bank[2:4], bank[4], bank[5]
            GATE, LNW, LNB, CC, TD, TF = 0, 4, 8, 12, 20, 21
            M_SA, M_CA, M_GA, M_SB, M_CB, M_GB = range(6)
            K_1CA, K_SA, K_A, K_B, K_1CB, K_SB, K_GB, K_GA = range(8)
            SPREAD = [(K_A, 0), (K_B, 1), (K_1CB, 2), (K_SB, 3), (K_GB, None)]
            Q_KV = C
            Q_WO = Q_KV + 1
            Q_SPREAD = Q_WO + B
            Q_LOOP = Q_SPREAD + len(SPREAD) * B
            Q_H, Q_XN, Q_H2 = Q_LOOP, Q_LOOP + BT, Q_LOOP + 2 * BT
            PER_RS = 1 + 2 * BT
            t_full, t_taken = (t_full0, t_full1), (t_taken0, t_taken1)
            s_full, s_taken = (s_full0, s_full1), (s_taken0, s_taken1)

            def t_use(q, b=0):
                return b * (3 * BT // 2) + (q // 2 + 1)

            def s_use(n, b):
                return b * BT + (n // 2 + 1)

            with nc.Block() as block:

                @block.sync
                def _(sp):
                    sp.wait_ge(rows_zero, 1)
                    for src, r in ((gate, GATE), (ln_w, LNW), (ln_b, LNB)):
                        sp.dma_start(rows[r:r + C, :], src.rearrange("(c p) -> c p", p=P)).then_inc(cols_in, 16)
                    sp.dma_start(rows[CC:CC + B * C, :], c_in.rearrange("b (c p) -> (b c) p", p=P)).then_inc(cols_in, 16)
                    for src, r in ((time_decay, TD), (time_first, TF)):
                        sp.dma_start(rows[r:r + 1, 0:S], src.rearrange("(a s) -> a s", a=1)).then_inc(cols_in, 16)
                    sp.dma_start(stage[:, 0, :, :], Wts.rearrange("(c p) d -> p c d", p=P)).then_inc(stage_in0, 16)
                    sp.dma_start(stage[:, 1, :, :], wmod_v[:, :, 0:512]).then_inc(stage_in1, 16)
                    sp.dma_start(xn[0:S, 0, :], Wk).then_inc(kv_in, 16)
                    sp.dma_start(xn[S:2 * S, 0, :], Wv).then_inc(kv_in, 16)
                    sp.dma_start(woN[:, :, :], Wo.rearrange("(c p) s -> p c s", p=P)).then_inc(wo_in, 16)
                    sp.dma_start(wrN[:, :, 0:E], Wr.rearrange("(c p) e -> p c e", p=P)).then_inc(wr_in, 16)
                    with nc.allow_non_contiguous_dma(reason="one column"):
                        sp.dma_start(wrN[:, :, E:E + 1], Wse.rearrange("(c p) e -> p c e", p=P)).then_inc(wr_in, 16)
                    for j in range(1, 6):
                        half = (j + 1) % 2
                        if j == 1:
                            sp.wait_ge(t_full[(C - 1) % 2], t_use(C - 1))
                        else:
                            sp.wait_ge(mod_done, j - 1)
                        sp.dma_start(stage[:, half, :, :], wmod_v[:, :, j * 512:(j + 1) * 512]).then_inc(stage_in[half], 16)
                    sp.sem_inc(h2_free, 2)
                    for b in range(B):
                        for i in range(BT):
                            sp.wait_ge(h2_ok, b * BT + (i + 2))
                            sp.dma_start(h2_dram[bass.ds((b * BT + i) * P, P), :], h2r[:, i % 2, :]).then_inc(h2_sent, 16)
                            sp.wait_ge(h2_sent, b * (BT * 16) + (i + 1) * 16)
                            sp.sem_inc(h2_free, 1)
                    sp.wait_ge(wr_in, 32)

                @block.gpsimd
                def _(pool):
                    g = nc.gpsimd
                    own = Tally(pool_self)
                    g.memset(rows[:, :], 0.0).then_inc(rows_zero, 1)
                    g.memset(ident[:, :], 0.0).then_inc(pool_self, 1)
                    g.memset(neg_half[:, :], -0.5).then_inc(pool_self, 1)
                    own.tick()
                    pool.wait_ge(pool_self, own.tick())
                    g.affine_select(out=ident[:, :], in_=ident[:, :], compare_op=ALU.not_equal, fill=1.0,
                                    base=0, pattern=[[-1, P]], channel_multiplier=1).then_inc(const_ok, 1)
                    q = Q_LOOP - 1
                    pool.wait_ge(t_taken[q % 2], t_use(q))
                    pool.wait_ge(t_taken[(q - 1) % 2], t_use(q - 1))
                    for b in range(B):
                        this = bass.ds(b, 1)

                        def lo_part(i, hi_ready, hi, lo, at):
                            pool.wait_ge(hi_ready, b * BT + (i + 1))
                            g.tensor_tensor(lo[:, :, at:at + P], fT[:, :, :], hi[:, :, at:at + P].bitcast(F32),
                                            ALU.subtract).then_inc(lo_done, 1)

                        def mix_rows(i):
                            pool.wait_ge(s_taken[i % 2], b * BT + (i // 2 + 1))
                            pool.wait_ge(xhat_ok, b * BT + (i + 1))
                            g.tensor_tensor(mix[:, i % 2, :], xhat[:, i, :], row(bc[:, 0, this, :]), ALU.mult).then_inc(pool_self, 1)
                            pool.wait_ge(pool_self, own.tick())
                            g.tensor_tensor(mix[:, i % 2, :], mix[:, i % 2, :], row(bc[:, 1, this, :]), ALU.add).then_inc(mix_ok, 1)

                        def rstd(n):
                            pool.wait_ge(ve_ok, b * PER_RS + (n + 2))
                            g.tensor_tensor(rs2[:, n % 2:n % 2 + 1], ve2[:, n % 2:n % 2 + 1], neg_half[:, 0:1], ALU.pow).then_inc(rs_ok, 1)

                        pool.wait_ge(ve_ok, b * PER_RS + 1)
                        g.tensor_tensor(rs[:, :], ve[:, :], neg_half[:, :], ALU.pow).then_inc(rs_ok, 1)
                        for i in range(BT):
                            lo_part(i, hT_hi, hTH, hTL, i * P)
                        mix_rows(0)
                        for i in range(BT):
                            if i + 1 < BT:
                                mix_rows(i + 1)
                            rstd(i)
                            if i:
                                lo_part(i - 1, xnT_hi, xnTH, xnTL, ((i - 1) % GT) * P)
                        lo_part(BT - 1, xnT_hi, xnTH, xnTL, (GT - 1) * P)
                        rstd(BT)
                        for i in range(BT):
                            if i + 1 < BT:
                                rstd(BT + i + 1)
                            pool.wait_ge(xhat2_ok, b * BT + (i + 1))
                            pool.wait_ge(h2_free, b * BT + (i + 1))
                            q = Q_H2 + i - 2
                            pool.wait_ge(t_full[q % 2], t_use(q, b))
                            g.tensor_tensor(h2r[:, i % 2, :], xn[:, i % 2, :], row(bc[:, 2, this, :]), ALU.mult).then_inc(pool_self, 1)
                            pool.wait_ge(pool_self, own.tick())
                            g.tensor_tensor(h2r[:, i % 2, :], h2r[:, i % 2, :], row(bc[:, 3, this, :]), ALU.add).then_inc(h2_ok, 1)

                @block.scalar
                def _(act):
                    a = nc.scalar
                    act.sem_inc(lo_done, 1)
                    act.sem_inc(st_ok, 1)
                    for b in range(B):
                        for h in range(2):
                            if b:
                                act.wait_ge(x_in[h], 16 * b)
                            lo = b * BT + h * HB
                            act.dma_start(xres[:, lo:lo + HB, :], x_rows[:, lo:lo + HB, :]).then_inc(x_in[h], 16)
                    act.wait_ge(col_ok, 1)
                    a.activation(ecol[:, 0:C], cols[:, GATE:GATE + C], ACT.Exp, scale=-1.0).then_inc(exp_ok, 1)
                    a.activation(ecol[:, C:C + B * C], cols[:, CC:CC + B * C], ACT.Exp, scale=-1.0).then_inc(exp_ok, 1)
                    a.activation(wcol[:, 0:2], cols[0:S, TD:TD + 2], ACT.Exp).then_inc(exp_ok, 1)

                    def filled(q, b=0):
                        act.wait_ge(t_full[q % 2], t_use(q, b))

                    for q in range(C):
                        filled(q)
                        a.activation(wtsH[:, q, :], tb[q % 2][:, :], ACT.Copy).then_inc(split_hi, 1)
                    filled(Q_KV)
                    a.activation(kvH[:, :, :], tb[Q_KV % 2][:, :].rearrange("p (c m) -> p c m", c=C), ACT.Copy).then_inc(split_hi, 1)
                    for b in range(B):
                        q = Q_WO + b
                        filled(q)
                        a.activation(woT[:, b, :], tb[q % 2][0:S, :], ACT.Copy).then_inc(t_taken[q % 2], 1)
                    for b in range(B):
                        for n, (kind, place) in enumerate(SPREAD):
                            q = Q_SPREAD + b * len(SPREAD) + n
                            filled(q)
                            dst = gate_b[:, b, :] if place is None else bc[:, place, b, :]
                            a.activation(dst, tb[q % 2][:, :], ACT.Copy).then_inc(t_taken[q % 2], 1)

                    for b in range(B):
                        this = bass.ds(b, 1)

                        def turned(q, n_lo, scale, bias):
                            filled(q, b)
                            act.wait_ge(lo_done, b * (2 * BT) + (n_lo + 1))
                            for c in range(C):
                                ins = a.activation(fT[:, c, :], tb[q % 2][:, c * P:(c + 1) * P], ACT.Identity,
                                                   scale=scale(c), bias=bias(c))
                            ins.then_inc(t_taken[q % 2], 1)

                        for i in range(BT):
                            turned(Q_H + i, i, lambda c: row(dcol[:, this, K_1CA, c:c + 1]), lambda c: row(dcol[:, this, K_SA, c:c + 1]))

                        def kv_front(n):
                            act.wait_ge(kv_full, b * BG + (n + 2))
                            act.wait_ge(st_ok, b * BG + (n + 1))
                            a.activation(kE[:, :], kvb[0:S, :], ACT.Exp, scale=-1.0).then_inc(e_neg, 1)
                            a.activation(vV[:, :], kvb[S:2 * S, :], ACT.Copy).then_inc(kv_read, 1)

                        def kv_back(n):
                            act.wait_ge(e_sig, b * BG + (n + 1))
                            a.activation(kE[:, :], kE[:, :], ACT.Exp, scale=wcol[:, 2:3]).then_inc(e_fac, 1)

                        for i in range(BT):
                            turned(Q_XN + i, BT + i, lambda c: cols[:, LNW + c:LNW + c + 1], lambda c: cols[:, LNB + c:LNB + c + 1])
                            if i == GT - 1:
                                kv_front(0)
                            if i == GT:
                                kv_back(0)
                        kv_front(1)
                        kv_back(1)
                        for i in range(BT):
                            q = Q_H2 + i
                            filled(q, b)
                            a.activation(h2T[:, :, bass.ds((b * BT + i) * P, P)],
                                         tb[q % 2][:, :].rearrange("p (c m) -> p c m", c=C), ACT.Copy).then_inc(t_taken[q % 2], 1)

                @block.vector
                def _(dve):
                    v = nc.vector
                    own = Tally(dve_self)
                    dve.sem_inc(kv_full, 1)
                    dve.sem_inc(h2_ok, 1)

                    def link(ins):
                        ins.then_inc(dve_self, 1)
                        dve.wait_ge(dve_self, own.tick())

                    link(v.memset(wrN[:, :, E + 1:R], 0.0))
                    dve.wait_ge(col_full, 1)
                    v.tensor_copy(cols[:, :], modb[:, 0:24]).then_inc(col_ok, 1)
                    dve.wait_ge(col_ok, 1)
                    dve.wait_ge(exp_ok, 3)
                    link(v.tensor_scalar(ecol[:, :], ecol[:, :], 1.0, None, ALU.add))
                    link(v.reciprocal(ecol[:, :], ecol[:, :]))
                    link(v.tensor_copy(gcol[:, 0, :], ecol[:, 0:C]))
                    link(v.tensor_scalar(gcol[:, 1, :], ecol[:, 0:C], -1.0, 1.0, ALU.mult, ALU.add))
                    link(v.tensor_scalar(wcol[:, 2:3], wcol[:, 1:2], -1.0, None, ALU.mult))
                    v.tensor_tensor(cT[:, :, :], cols[:, CC:CC + B * C].rearrange("p (b c) -> p c b", b=B),
                                    ecol[:, C:C + B * C].rearrange("p (b c) -> p c b", b=B), ALU.mult).then_inc(silu_c_ok, 1)
                    dve.wait_ge(stage_in0, 16)
                    for c in range(C):
                        v.tensor_scalar(stage[:, 0, c, :], stage[:, 0, c, :], gcol[:, 0, c:c + 1], None, ALU.mult).then_inc(wts_scaled, 1)
                    for q in range(C):
                        dve.wait_ge(split_hi, q + 1)
                        v.tensor_tensor(wtsL[:, q, :], tb[q % 2][:, :], wtsH[:, q, :].bitcast(F32), ALU.subtract).then_inc(t_taken[q % 2], 1)
                    dve.wait_ge(split_hi, C + 1)
                    v.tensor_tensor(kvL[:, :, :], tb[Q_KV % 2][:, :].rearrange("p (c m) -> p c m", c=C),
                                    kvH[:, :, :].bitcast(F32), ALU.subtract).then_inc(t_taken[Q_KV % 2], 1)
                    dve.wait_ge(mod_done, 6)
                    link(v.tensor_copy(modc[:, :, :, :].rearrange("p j c b -> p (j c b)"), modb[:, 0:6 * C * B]))
                    dk = lambda kind: dcol[:, :, kind, :].rearrange("p b c -> p c b")
                    g1 = gcol[:, 1, :].rearrange("p (c a) -> p c a", a=1).to_broadcast([P, C, B])
                    link(v.tensor_scalar(dk(K_1CA), modc[:, M_CA, :, :], 1.0, None, ALU.add))
                    link(v.tensor_scalar(dk(K_1CB), modc[:, M_CB, :, :], 1.0, None, ALU.add))
                    link(v.tensor_copy(dk(K_SA), modc[:, M_SA, :, :]))
                    link(v.tensor_copy(dk(K_SB), modc[:, M_SB, :, :]))
                    link(v.tensor_tensor(dk(K_A), dk(K_1CA), g1, ALU.mult))
                    link(v.tensor_tensor(dk(K_B), modc[:, M_SA, :, :], g1, ALU.mult))
                    for src, kind in ((M_GA, K_GA), (M_GB, K_GB)):
                        link(v.tensor_scalar(tmpc[:, 0, :, :], modc[:, src, :, :], 0.0, 2.0, ALU.is_ge, ALU.mult))
                        link(v.tensor_scalar(tmpc[:, 1, :, :], tmpc[:, 0, :, :], -1.0, None, ALU.add))
                        link(v.tensor_scalar(tmpc[:, 2, :, :], modc[:, src, :, :], -1.0, GATE_FLOOR, ALU.mult, ALU.max))
                        link(v.tensor_tensor(tmpc[:, 2, :, :], tmpc[:, 2, :, :], modc[:, src, :, :], ALU.max))
                        link(v.tensor_tensor(dk(kind), tmpc[:, 1, :, :], tmpc[:, 2, :, :], ALU.mult))
                    dve.wait_ge(wo_in, 16)
                    for b in range(B):
                        for c in range(C):
                            v.tensor_scalar(woS[:, c, b, :], woN[:, c, :], dcol[:, b, K_GA, c:c + 1], None, ALU.mult).then_inc(wo_scaled, 1)

                    for b in range(B):

                        def xrow(i):
                            return row(xres[:, bass.ds(b * BT + i, 1), :])

                        if b:
                            dve.wait_ge(xhat_ok, b * BT)
                        for i in range(BT):
                            if i % HB == 0:
                                dve.wait_ge(x_in[i // HB], b * 16 + 16)
                            link(v.bn_stats(st6[:, :], xrow(i)))
                            link(v.bn_aggr(mv1[:, i, :], st6[:, :]))
                        v.tensor_scalar(ve[:, :], mv1[:, :, 1], LN_EPS, None, ALU.add).then_inc(ve_ok, 1)
                        dve.wait_ge(rs_ok, b * PER_RS + 1)

                        def hi_part(q, i, dst, at, done):
                            dve.wait_ge(t_taken[q % 2], t_use(q, b))
                            v.tensor_copy(dst[:, :, at:at + P], fT[:, :, :]).then_inc(done, 1)

                        for i in range(BT):
                            v.tensor_scalar(xhat[:, i, :], xrow(i), mv1[:, i, 0:1], rs[:, i:i + 1], ALU.subtract, ALU.mult).then_inc(xhat_ok, 1)
                            if i:
                                hi_part(Q_H + i - 1, i - 1, hTH, (i - 1) * P, hT_hi)
                        hi_part(Q_H + BT - 1, BT - 1, hTH, (BT - 1) * P, hT_hi)

                        def stats(n, src):
                            link(v.bn_stats(st6[:, :], src))
                            link(v.bn_aggr(mv2[:, n % 2, :], st6[:, :]))
                            v.tensor_scalar(ve2[:, n % 2:n % 2 + 1], mv2[:, n % 2, 1:2], LN_EPS, None, ALU.add).then_inc(ve_ok, 1)

                        def apply(n, src, dst, done):
                            dve.wait_ge(rs_ok, b * PER_RS + (n + 2))
                            v.tensor_scalar(dst, src, mv2[:, n % 2, 0:1], rs2[:, n % 2:n % 2 + 1], ALU.subtract, ALU.mult).then_inc(done, 1)

                        def mix_front(i):
                            dve.wait_ge(s_full[i % 2], s_use(i, b))
                            dve.wait_ge(mix_ok, b * BT + (i + 1))
                            if b or i:
                                dve.wait_ge(xn_ok, b * BT + i)
                            if b and i == 0:
                                dve.wait_ge(xhat2_ok, b * BT)
                            v.tensor_tensor(xs[:, :], sbk[i % 2][:, :], mix[:, i % 2, :], ALU.add).then_inc(s_taken[i % 2], 1)
                            dve.wait_ge(s_taken[i % 2], s_use(i, b) + 1)
                            stats(i, xs[:, :])

                        def mix_apply(i):
                            if i < 2:
                                dve.wait_ge(h2_ok, b * BT + 1)
                            apply(i, xs[:, :], xn[:, i % 2, :], xn_ok)

                        def mix_back(i):
                            if i % GT == 0:
                                dve.wait_ge(kv_full, b * BG + (i // GT + 1))
                            hi_part(Q_XN + i, i, xnTH, (i % GT) * P, xnT_hi)

                        def kv_mid(n):
                            dve.wait_ge(e_neg, b * BG + (n + 1))
                            link(v.tensor_scalar(kE[:, :], kE[:, :], 1.0, None, ALU.add))
                            v.reciprocal(kE[:, :], kE[:, :]).then_inc(e_sig, 1)

                        def kv_scan(n):
                            dve.wait_ge(e_fac, b * BG + (n + 1))
                            dve.wait_ge(kv_read, b * BG + (n + 2))
                            link(v.tensor_tensor(kE[:, :], kE[:, :], vV[:, :], ALU.mult))
                            if n:
                                dve.wait_ge(st_ok, b * BG + (n + 1))
                            v.tensor_tensor_scan(states[:, n * GW:(n + 1) * GW], wcol[:, 0:1].to_broadcast([S, GW]), kE[:, :],
                                                 states[:, n * GW - 1:n * GW] if n else 0.0, ALU.mult, ALU.add).then_inc(st_ok, 1)

                        for i in range(BT):
                            mix_front(i)
                            if i == GT + 1:
                                kv_mid(0)
                            if i:
                                mix_back(i - 1)
                            mix_apply(i)
                            if i == GT + 2:
                                kv_scan(0)
                        mix_back(BT - 1)
                        kv_mid(1)
                        kv_scan(1)

                        def residual(i):
                            if i == 0:
                                dve.wait_ge(xn_ok, (b + 1) * BT)
                            elif i > 1:
                                dve.wait_ge(xhat2_ok, b * BT + i - 1)
                            dve.wait_ge(s_full[i % 2], s_use(BT + i, b))
                            v.tensor_tensor(xrow(i), sbk[i % 2][:, :], xrow(i), ALU.add).then_inc(s_taken[i % 2], 1)
                            dve.wait_ge(s_taken[i % 2], s_use(BT + i, b) + 1)
                            stats(BT + i, xrow(i))

                        residual(0)
                        for i in range(BT):
                            if i + 1 < BT:
                                residual(i + 1)
                            if i > 1:
                                dve.wait_ge(h2_ok, b * BT + i)
                            apply(BT + i, xrow(i), xn[:, i % 2, :], xhat2_ok)

                @block.tensor
                def _(pe):
                    m = nc.tensor
                    for s_ in (s_taken0, s_taken1, kv_read):
                        pe.sem_inc(s_, 1)
                    pe.wait_ge(const_ok, 1)
                    pe.wait_ge(cols_in, 96)
                    m.transpose(modb[:, 0:24], rows[:, :], ident[0:24, 0:24]).then_inc(col_full, 1)

                    def vacant(q, b=0):
                        if q >= 2:
                            pe.wait_ge(t_taken[q % 2], t_use(q - 2, b))

                    pe.wait_ge(wts_scaled, C)
                    for q in range(C):
                        vacant(q)
                        for ec in range(C):
                            ins = m.transpose(tb[q % 2][:, ec * P:(ec + 1) * P], stage[:, 0, ec, q * P:(q + 1) * P], ident[:, :])
                        ins.then_inc(t_full[q % 2], 1)
                    vacant(Q_KV)
                    pe.wait_ge(kv_in, 32)
                    for c in range(C):
                        ins = m.transpose(tb[Q_KV % 2][:, c * P:(c + 1) * P], xn[:, 0, c * P:(c + 1) * P], ident[:, :])
                    ins.then_inc(t_full[Q_KV % 2], 1)
                    pe.wait_ge(silu_c_ok, 1)
                    for j in range(6):
                        half = (j + 1) % 2
                        pe.wait_ge(stage_in[half], 16 * ((j + 1) // 2 + 1))
                        for cc in range(C):
                            at = (j * C + cc) * B
                            for k in range(C):
                                ins = m.matmul(modb[:, at:at + B], stage[:, half, k, cc * P:(cc + 1) * P], cT[:, k, :],
                                               start=(k == 0), stop=(k == C - 1))
                        ins.then_inc(mod_done, 1)
                    for b in range(B):
                        q = Q_WO + b
                        vacant(q)
                        pe.wait_ge(wo_scaled, (b + 1) * C)
                        for c in range(C):
                            ins = m.transpose(tb[q % 2][0:S, c * P:(c + 1) * P], woS[:, c, b, :], ident[:, :])
                        ins.then_inc(t_full[q % 2], 1)
                    for b in range(B):
                        for n, (kind, _place) in enumerate(SPREAD):
                            q = Q_SPREAD + b * len(SPREAD) + n
                            vacant(q)
                            for c in range(C):
                                ins = m.matmul(tb[q % 2][:, c * P:(c + 1) * P], dcol[:, b, kind, c:c + 1].to_broadcast([P, P]),
                                               ident[:, :], start=True, stop=True)
                            ins.then_inc(t_full[q % 2], 1)

                    for b in range(B):

                        def turn(q, src, ready, n):
                            vacant(q, b)
                            pe.wait_ge(ready, n)
                            for c in range(C):
                                ins = m.transpose(tb[q % 2][:, c * P:(c + 1) * P], src[:, c * P:(c + 1) * P], ident[:, :])
                            ins.then_inc(t_full[q % 2], 1)

                        for i in range(BT):
                            turn(Q_H + i, xhat[:, i, :], xhat_ok, b * BT + (i + 1))

                        def mixer(i):
                            s = (i + HB) % BT
                            pe.wait_ge(s_taken[i % 2], s_use(i, b))
                            pe.wait_ge(lo_done, b * (2 * BT) + (s + 2))
                            k = 0
                            for c in range(C):
                                for l, r in ((hTH, wtsH), (hTH, wtsL), (hTL, wtsH)):
                                    ins = m.matmul(sbk[i % 2][:, :], l[:, c, s * P:(s + 1) * P], r[:, c, :],
                                                   start=(k == 0), stop=(k == 3 * C - 1))
                                    k += 1
                            ins.then_inc(s_full[i % 2], 1)

                        def keys_values(n):
                            pe.wait_ge(lo_done, b * (2 * BT) + (BT + (n + 1) * GT + 1))
                            pe.wait_ge(kv_read, b * BG + (n + 1))
                            k = 0
                            for c in range(C):
                                for l, r in ((kvH, xnTH), (kvH, xnTL), (kvL, xnTH)):
                                    ins = m.matmul(kvb[:, :], l[:, c, :], r[:, c, :], start=(k == 0), stop=(k == 3 * C - 1))
                                    k += 1
                            ins.then_inc(kv_full, 1)

                        for i in range(BT):
                            mixer(i)
                            if i == GT + 1:
                                keys_values(0)
                            if i:
                                turn(Q_XN + i - 1, xn[:, (i - 1) % 2, :], xn_ok, b * BT + i)
                        turn(Q_XN + BT - 1, xn[:, (BT - 1) % 2, :], xn_ok, b * BT + BT)
                        keys_values(1)

                        def project(i):
                            pe.wait_ge(s_taken[i % 2], s_use(BT + i, b))
                            pe.wait_ge(st_ok, b * BG + (i // GT + 2))
                            m.matmul(sbk[i % 2][:, :], states[:, i * P:(i + 1) * P], woT[:, bass.ds(b, 1), :].rearrange("s a h -> s (a h)"),
                                     start=True, stop=True).then_inc(s_full[i % 2], 1)

                        for i in range(BT):
                            project(i)
                            if i:
                                turn(Q_H2 + i - 1, h2r[:, (i - 1) % 2, :], h2_ok, b * BT + (i + 1))
                        turn(Q_H2 + BT - 1, h2r[:, (BT - 1) % 2, :], h2_ok, b * BT + (BT + 1))

        with ExitStack() as pb:
            xsH = sb("xsH", [P, C, GW], F32R, pb)
            xsL = sb("xsL", [P, C, GW], F32R, pb)
            wguN = sb("wguN", [P, 2, C, PC * P], F32, pb)
            wdN = sb("wdN", [P, PC, H], F32, pb)
            wguH = sb("wguH", [P, 2, C, PC * P], F32R, pb)
            wguL = sb("wguL", [P, 2, C, PC * P], F32R, pb)
            wdH = sb("wdH", [P, PC, H], F32R, pb)
            wdL = sb("wdL", [P, PC, H], F32R, pb)
            silu = sb("silu", [P, GW], F32, pb)
            prod = sb("prod", [P, GW], F32, pb)
            prodH = sb("prodH", [P, PC, GW], F32R, pb)
            prodL = sb("prodL", [P, PC, GW], F32R, pb)
            ytmp = sb("ytmp", [P, 2, H], F32, pb)
            egu = sb("egu", [P, 2, 2, C, F], F32, pb)
            ed = sb("ed", [P, 2, len(FC), H], F32, pb)
            xg = sb("xg", [P, H], F32, pb)
            xeT = sb("xeT", [P, C, P], F32, pb)
            esilu = sb("esilu", [P, F], F32, pb)
            eprod = sb("eprod", [P, F], F32, pb)
            epT = sb("epT", [P, len(FC), P], F32, pb)
            ye = sb("ye", [P, H], F32, pb)
            tri = sb("tri", [P, P], F32, pb)
            ones = sb("ones", [P, P], F32, pb)
            iota_e = sb("iota_e", [P, E], F32, pb)
            iota_i = sb("iota_i", [P, E], U32, pb)
            tok_id = sb("tok_id", [P, NT], U32, pb)
            zero_u = sb("zero_u", [P, NP], U32, pb)
            slotw = sb("slotw", [P, NT, TOP_K], F32, pb)
            sigma = sb("sigma", [P, NT], F32, pb)
            y_idx = sb("y_idx", [P, NT, TOP_K], U32, pb)
            t_idx = sb("t_idx", [P, NT, TOP_K], U32, pb)
            slot_tok = sb("slot_tok", [P, NP], U32, pb)
            rmax = sb("rmax", [P, NT], F32, pb)
            top8 = sb("top8", [P, NT, 8], F32, pb)
            top_i = sb("top_i", [P, NT, 8], U32, pb)
            top_e = sb("top_e", [P, NT, TOP_K], F32, pb)
            odd = sb("odd", [P, NT, TOP_K], F32, pb)
            pos = sb("pos", [P, NT, TOP_K], F32, pb)
            over = sb("over", [P, NT, TOP_K], F32, pb)
            idx_f = sb("idx_f", [P, NT, TOP_K], F32, pb)

            scr = egu[:, :, :, :, :].rearrange("p a w c f -> p (a w c f)")
            scd = ed[:, :, :, :].rearrange("p a c h -> p (a c h)")
            logits = scr[:, 0:NT * R].rearrange("p (i r) -> p i r", r=R)
            probs = scr[:, 544:544 + NT * E].rearrange("p (i e) -> p i e", e=E)
            onehot = scr[:, 1056:1056 + NT * TOP_K * E].rearrange("p (i k e) -> p i k e", k=TOP_K, e=E)
            picked = scr[:, 3104:3104 + NT * TOP_K * E].rearrange("p (i k e) -> p i k e", k=TOP_K, e=E)
            logT = scd[0:R, 0:NG * GW]
            mask = scd[:, 2048:2048 + NT * E].rearrange("p (i e) -> p i e", e=E)
            before = scd[:, 2560:2560 + NT * E].rearrange("p (i e) -> p i e", e=E)
            yg = scr[:, 0:2 * TOP_K * H].rearrange("p (n k h) -> p n k h", n=2, k=TOP_K)

            (rb_ok, rconst, lt_full, lt_ok, lg_full, shift_ok, ex_ok, pos_full, mask_ok, route_ok,
             tab_zero, scat, tab_in, w_in, whi_ok, wlo_ok, xhi_ok, xlo_ok, g_full, silu_ok, u_full,
             prod_ok, phi_ok, plo_ok, d_full0, d_full1, d_used0, d_used1, x_acc,
             xg_in, et_full, et_taken, eg_full, esilu_ok, eprod_ok, ey_full, ye_ok, ye_sent, ye_free,
             gu_in, dn_in, yg_zero, y_in0, y_in1, y_used, final_ok, out_done, dve_b, pool_b) = sems(
                 "rb_ok rconst lt_full lt_ok lg_full shift_ok ex_ok pos_full mask_ok route_ok "
                 "tab_zero scat tab_in w_in whi_ok wlo_ok xhi_ok xlo_ok g_full silu_ok u_full "
                 "prod_ok phi_ok plo_ok d_full0 d_full1 d_used0 d_used1 x_acc "
                 "xg_in et_full et_taken eg_full esilu_ok eprod_ok ey_full ye_ok ye_sent ye_free "
                 "gu_in dn_in yg_zero y_in0 y_in1 y_used final_ok out_done dve_b pool_b")
            d_full, d_used, y_in = (d_full0, d_full1), (d_used0, d_used1), (y_in0, y_in1)
            gB, uB, dB = bank[0], bank[1], bank[2:4]
            egB, euB, etB, eyB = bank[4:8]

            def chunk(p, g, f):
                return NG * sum(PARTS[:p]) + (g * PARTS[p] + f)

            def tile(p, g, m):
                return p * NG * GT + (g * GT + m)

            def pair(p, g, h):
                return (p - PAIR_PARTS[0]) * 2 * NG + (2 * g + h)

            wsg_v = Wsg.rearrange("(c p) f -> p c f", p=P)
            wsu_v = Wsu.rearrange("(c p) f -> p c f", p=P)

            with nc.Block() as block:

                @block.sync
                def _(sp):
                    def load_part(p):
                        lo, n = P * sum(PARTS[:p]), PARTS[p]
                        if p:
                            sp.wait_ge(wlo_ok, 3 * p)
                        sp.dma_start(wguN[:, 0, :, 0:n * P], wsg_v[:, :, lo:lo + n * P]).then_inc(w_in, 16)
                        sp.dma_start(wguN[:, 1, :, 0:n * P], wsu_v[:, :, lo:lo + n * P]).then_inc(w_in, 16)
                        sp.dma_start(wdN[:, 0:n, :], Wsd[lo:lo + n * P, :].rearrange("(f p) h -> p f h", p=P)).then_inc(w_in, 16)

                    def load_gate_up(j):
                        for e in range(2):
                            for w, src in enumerate((Wg, Wu)):
                                sp.dma_start(egu[:, e, w, :, :], src[2 * j + e, :, :].rearrange("(p c) f -> p c f", c=C)).then_inc(gu_in, 16)

                    def load_down(j):
                        for e in range(2):
                            sp.dma_start(ed[:, e, 0:2, :], Wd[2 * j + e, 0:2 * P, :].rearrange("(c p) h -> p c h", p=P)).then_inc(dn_in, 16)
                            sp.dma_start(ed[0:F - 2 * P, e, 2, :], Wd[2 * j + e, 2 * P:F, :]).then_inc(dn_in, 16)

                    load_part(0)
                    sp.wait_ge(rconst, 1)
                    sp.dma_start(tok_dram.rearrange("(p j) a -> p (j a)", p=P), zero_u[:, :]).then_inc(tab_zero, 16)
                    sp.wait_ge(route_ok, 1)
                    load_gate_up(0)
                    load_down(0)
                    load_part(1)
                    sp.wait_ge(scat, 16 * NT * TOP_K)
                    sp.dma_start(slot_tok[:, :], tok_dram.rearrange("(p j) a -> p (j a)", p=P)).then_inc(tab_in, 16)
                    sp.sem_inc(ye_free, 1)
                    for p in PAIR_PARTS:
                        for g in range(NG):
                            for h in range(2):
                                j = pair(p, g, h)
                                if j + 1 < NP:
                                    sp.wait_ge(eg_full, j + 1)
                                    load_gate_up(j + 1)
                                    sp.wait_ge(ey_full, j + 1)
                                    load_down(j + 1)
                                sp.wait_ge(ye_ok, j + 1)
                                sp.dma_start(ye_dram[j * P:(j + 1) * P, :], ye[:, :]).then_inc(ye_sent, 16)
                                sp.wait_ge(ye_sent, 16 * (j + 1))
                                sp.sem_inc(ye_free, 1)
                        load_part(p + 1)
                    for g in range(NG):
                        for m in range(GT):
                            i = g * GT + m
                            sp.wait_ge(final_ok, i + 1)
                            sp.dma_start(out_rows[:, i, :], xres[:, i, :]).then_inc(out_done, 16)
                    sp.wait_ge(out_done, 16 * NT)

                @block.gpsimd
                def _(pool):
                    gp = nc.gpsimd
                    own = Tally(pool_b)

                    def link(ins):
                        ins.then_inc(pool_b, 1)
                        pool.wait_ge(pool_b, own.tick())

                    gp.memset(zero_u[:, :], 0).then_inc(rconst, 1)
                    link(gp.memset(ones[:, :], 1.0))
                    link(gp.iota(iota_i[:, :], [[1, E]], base=0, channel_multiplier=0))
                    link(gp.tensor_copy(iota_e[:, :], iota_i[:, :]))
                    link(gp.iota(tok_id[:, :], [[P, NT]], base=0, channel_multiplier=1))
                    gp.affine_select(out=tri[:, :], in_=ones[:, :], compare_op=ALU.is_gt, fill=0.0, base=0,
                                     pattern=[[1, P]], channel_multiplier=-1).then_inc(rb_ok, 1)
                    pool.wait_ge(route_ok, 1)
                    pool.wait_ge(tab_zero, 16)
                    for i in range(NT):
                        for k in range(TOP_K):
                            gp.indirect_dma_start(tok_dram[:, :], bass.IndirectOffsetOnAxis(t_idx[:, i, k:k + 1], axis=0),
                                                  tok_id[:, i:i + 1], None,
                                                  bounds_check=E * CAP - 1, oob_is_err=False).then_inc(scat, 16)
                    pool.wait_ge(tab_in, 16)
                    for j in range(NP):
                        if j:
                            pool.wait_ge(et_full, 2 * j - 1)
                        gp.indirect_dma_start(xg[:, :], None, h2_dram[:, :],
                                              bass.IndirectOffsetOnAxis(slot_tok[:, j:j + 1], axis=0)).then_inc(xg_in, 16)
                    pool.wait_ge(eg_full, NP)
                    link(gp.memset(scr[:, 0:2 * TOP_K * H], 0.0))
                    pool.wait_ge(ye_free, NP + 1)
                    for i in range(NT):
                        if i > 1:
                            pool.wait_ge(y_used, i - 1)
                        for k in range(TOP_K):
                            gp.indirect_dma_start(yg[:, i % 2, k, :], None, ye_dram[:, :],
                                                  bass.IndirectOffsetOnAxis(y_idx[:, i, k:k + 1], axis=0),
                                                  bounds_check=E * CAP - 1, oob_is_err=False).then_inc(y_in[i % 2], 16)

                @block.scalar
                def _(act):
                    a = nc.scalar
                    act.sem_inc(u_full, 1)
                    act.sem_inc(prod_ok, 1)
                    for g in range(NG):
                        act.wait_ge(lt_full, g + 1)
                        a.activation(logT[:, g * GW:(g + 1) * GW], bank[4 + g][0:R, :], ACT.Copy).then_inc(lt_ok, 1)
                    act.wait_ge(shift_ok, 1)
                    a.activation(probs, probs, ACT.Exp).then_inc(ex_ok, 1)
                    a.activation(sigma[:, :], logits[:, :, E], ACT.Exp, scale=-1.0).then_inc(ex_ok, 1)

                    def split_weights(p):
                        n = PARTS[p]
                        act.wait_ge(w_in, 48 * (p + 1))
                        act.wait_ge(u_full, chunk(p, 0, 0) + 1)
                        for w in range(2):
                            a.activation(wguH[:, w, :, 0:n * P], wguN[:, w, :, 0:n * P], ACT.Copy).then_inc(whi_ok, 1)

                    def split_down(p):
                        n = PARTS[p]
                        if p:
                            for q in range(2):
                                act.wait_ge(d_full[q], p * NG * GT // 2)
                        a.activation(wdH[:, 0:n, :], wdN[:, 0:n, :], ACT.Copy).then_inc(whi_ok, 1)

                    def split_group(p, g):
                        act.wait_ge(u_full, chunk(p, g, 0) + 1)
                        for c in range(C):
                            a.activation(xsH[:, c, :], h2T[:, c, g * GW:(g + 1) * GW], ACT.Copy).then_inc(xhi_ok, 1)

                    def gate_up(p, g, f):
                        n = chunk(p, g, f)
                        act.wait_ge(g_full, n + 1)
                        act.wait_ge(prod_ok, n + 1)
                        a.activation(silu[:, :], gB[:, :], ACT.Silu).then_inc(silu_ok, 1)
                        act.wait_ge(prod_ok, n + 2)
                        a.activation(prodH[:, f, :], prod[:, :], ACT.Copy).then_inc(phi_ok, 1)

                    def pair_rows(j):
                        act.wait_ge(et_full, 2 * j + 1)
                        a.activation(xeT[:, :, :], etB[:, :].rearrange("p (c m) -> p c m", c=C), ACT.Copy).then_inc(et_taken, 1)

                    def pair_silu(j):
                        act.wait_ge(eg_full, j + 1)
                        if j:
                            act.wait_ge(eprod_ok, j)
                        a.activation(esilu[:, :], egB[:, 0:F], ACT.Silu).then_inc(esilu_ok, 1)

                    def pair_turned(j):
                        act.wait_ge(et_full, 2 * j + 2)
                        for c, (lo, n) in enumerate(FC):
                            ins = a.activation(epT[0:n, c, :], etB[0:n, c * P:(c + 1) * P], ACT.Copy)
                        ins.then_inc(et_taken, 1)

                    def pair_out(j):
                        act.wait_ge(ey_full, j + 1)
                        act.wait_ge(ye_free, j + 1)
                        a.activation(ye[:, :], eyB[:, :], ACT.Copy).then_inc(ye_ok, 1)

                    for p, n in enumerate(PARTS):
                        split_weights(p)
                        for g in range(NG):
                            split_group(p, g)
                            if g == 0:
                                split_down(p)
                            pairs = [pair(p, g, h) for h in range(2)] if p in PAIR_PARTS else None
                            gate_up(p, g, 0)
                            if pairs:
                                pair_rows(pairs[0])
                            gate_up(p, g, 1)
                            if pairs:
                                pair_silu(pairs[0])
                            if n > 2:
                                gate_up(p, g, 2)
                            if pairs:
                                pair_turned(pairs[0])
                                pair_out(pairs[0])
                                pair_rows(pairs[1])
                                pair_silu(pairs[1])
                                pair_turned(pairs[1])
                                pair_out(pairs[1])

                @block.vector
                def _(dve):
                    v = nc.vector
                    own = Tally(dve_b)
                    dve.sem_inc(silu_ok, 1)
                    dve.sem_inc(plo_ok, 1)
                    dve.sem_inc(x_acc, 2)

                    def link(ins):
                        ins.then_inc(dve_b, 1)
                        dve.wait_ge(dve_b, own.tick())

                    def over_e(ap):
                        return ap.rearrange("p (i a) -> p i a", a=1).to_broadcast([P, NT, E])

                    def over_k(ap):
                        return ap.rearrange("p i (a e) -> p i a e", a=1).to_broadcast([P, NT, TOP_K, E])

                    for n in range(2):
                        dve.wait_ge(lg_full, n + 1)
                        link(v.tensor_copy(logits[:, n * BT:(n + 1) * BT, :].rearrange("p i r -> p (i r)"), bank[4 + n][:, 0:BT * R]))
                    link(v.tensor_reduce(rmax[:, :], logits[:, :, 0:E], AX.X, ALU.max))
                    v.tensor_tensor(probs, logits[:, :, 0:E], over_e(rmax[:, :]), ALU.subtract).then_inc(shift_ok, 1)
                    dve.wait_ge(ex_ok, 2)
                    link(v.tensor_reduce(rmax[:, :], probs, AX.X, ALU.add))
                    link(v.reciprocal(rmax[:, :], rmax[:, :]))
                    link(v.tensor_tensor(probs, probs, over_e(rmax[:, :]), ALU.mult))
                    link(v.tensor_scalar(sigma[:, :], sigma[:, :], 1.0, None, ALU.add))
                    link(v.reciprocal(sigma[:, :], sigma[:, :]))
                    for i in range(NT):
                        v.max(top8[:, i, :], probs[:, i, :]).then_inc(dve_b, 1)
                        own.tick()
                    dve.wait_ge(dve_b, own.last())
                    for i in range(NT):
                        v.max_index(top_i[:, i, :], top8[:, i, :], probs[:, i, :]).then_inc(dve_b, 1)
                        own.tick()
                    dve.wait_ge(dve_b, own.last())
                    link(v.tensor_copy(top_e[:, :, :], top_i[:, :, 0:TOP_K]))
                    dve.wait_ge(rb_ok, 1)
                    for k in range(TOP_K):
                        v.tensor_tensor(onehot[:, :, k, :], top_e[:, :, k:k + 1].to_broadcast([P, NT, E]),
                                        iota_e[:, :].rearrange("p (a e) -> p a e", a=1).to_broadcast([P, NT, E]), ALU.is_equal).then_inc(dve_b, 1)
                        own.tick()
                    dve.wait_ge(dve_b, own.last())
                    link(v.tensor_reduce(mask, onehot.rearrange("p i k e -> p i e k"), AX.X, ALU.add))
                    link(v.memset(before[:, 0, :], 0.0))
                    for i in range(1, NT):
                        ins = v.tensor_tensor(before[:, i, :], before[:, i - 1, :], mask[:, i - 1, :], ALU.add)
                        if i < NT - 1:
                            link(ins)
                        else:
                            ins.then_inc(mask_ok, 1)
                    dve.wait_ge(pos_full, 1)
                    for k in range(TOP_K):
                        v.tensor_tensor(picked[:, :, k, :], bank[6][:, :].rearrange("p (i e) -> p i e", e=E), onehot[:, :, k, :], ALU.mult).then_inc(dve_b, 1)
                        own.tick()
                    dve.wait_ge(dve_b, own.last())
                    link(v.tensor_reduce(pos[:, :, :], picked, AX.X, ALU.add))
                    link(v.tensor_scalar(over[:, :, :], pos[:, :, :], float(CAP), None, ALU.is_ge))
                    link(v.scalar_tensor_tensor(idx_f[:, :, :], top_e[:, :, :], float(CAP), pos[:, :, :], ALU.mult, ALU.add))
                    link(v.scalar_tensor_tensor(idx_f[:, :, :], over[:, :, :], float(FAR), idx_f[:, :, :], ALU.mult, ALU.add))
                    link(v.tensor_copy(y_idx[:, :, :], idx_f[:, :, :]))
                    link(v.tensor_scalar(t_idx[:, :, :], top_i[:, :, 0:TOP_K], 1, None, ALU.bitwise_and))
                    link(v.tensor_copy(odd[:, :, :], t_idx[:, :, :]))
                    link(v.tensor_tensor(top_e[:, :, :], top_e[:, :, :], odd[:, :, :], ALU.subtract))
                    link(v.scalar_tensor_tensor(pos[:, :, :], odd[:, :, :], float(CAP), pos[:, :, :], ALU.mult, ALU.add))
                    link(v.tensor_scalar(pos[:, :, :], pos[:, :, :], float(NP), None, ALU.mult))
                    link(v.scalar_tensor_tensor(pos[:, :, :], top_e[:, :, :], 0.5, pos[:, :, :], ALU.mult, ALU.add))
                    link(v.scalar_tensor_tensor(pos[:, :, :], over[:, :, :], float(FAR), pos[:, :, :], ALU.mult, ALU.add))
                    link(v.tensor_copy(t_idx[:, :, :], pos[:, :, :]))
                    link(v.tensor_reduce(rmax[:, :], top8[:, :, 0:TOP_K], AX.X, ALU.add))
                    link(v.reciprocal(rmax[:, :], rmax[:, :]))
                    link(v.tensor_tensor(slotw[:, :, :], top8[:, :, 0:TOP_K],
                                         rmax[:, :].rearrange("p (i a) -> p i a", a=1).to_broadcast([P, NT, TOP_K]), ALU.mult))
                    link(v.tensor_scalar(over[:, :, :], over[:, :, :], -1.0, 1.0, ALU.mult, ALU.add))
                    v.tensor_tensor(slotw[:, :, :], slotw[:, :, :], over[:, :, :], ALU.mult).then_inc(route_ok, 1)

                    def lo_weights(p, w):
                        n = PARTS[p]
                        dve.wait_ge(whi_ok, 3 * p + w + 1)
                        if w < 2:
                            v.tensor_tensor(wguL[:, w, :, 0:n * P], wguN[:, w, :, 0:n * P],
                                            wguH[:, w, :, 0:n * P].bitcast(F32), ALU.subtract).then_inc(wlo_ok, 1)
                        else:
                            v.tensor_tensor(wdL[:, 0:n, :], wdN[:, 0:n, :], wdH[:, 0:n, :].bitcast(F32), ALU.subtract).then_inc(wlo_ok, 1)

                    def lo_group(p, g):
                        for c in range(C):
                            dve.wait_ge(xhi_ok, (p * NG + g) * C + c + 1)
                            v.tensor_tensor(xsL[:, c, :], h2T[:, c, g * GW:(g + 1) * GW], xsH[:, c, :].bitcast(F32), ALU.subtract).then_inc(xlo_ok, 1)

                    def gate_up(p, g, f):
                        n = chunk(p, g, f)
                        dve.wait_ge(silu_ok, n + 2)
                        dve.wait_ge(u_full, n + 2)
                        dve.wait_ge(plo_ok, n + 1)
                        v.tensor_tensor(prod[:, :], uB[:, :], silu[:, :], ALU.mult).then_inc(prod_ok, 1)
                        dve.wait_ge(phi_ok, n + 1)
                        v.tensor_tensor(prodL[:, f, :], prod[:, :], prodH[:, f, :].bitcast(F32), ALU.subtract).then_inc(plo_ok, 1)

                    def down(p, g, m):
                        n, i = tile(p, g, m), g * GT + m
                        dve.wait_ge(d_full[m % 2], n // 2 + 1)
                        dve.wait_ge(x_acc, n + 1)
                        v.scalar_tensor_tensor(ytmp[:, m % 2, :], dB[m % 2][:, :], sigma[:, i:i + 1], gate_b[:, i // BT, :],
                                               ALU.mult, ALU.mult).then_inc(d_used[m % 2], 1)
                        dve.wait_ge(d_used[m % 2], n // 2 + 2)
                        v.tensor_tensor(xres[:, i, :], xres[:, i, :], ytmp[:, m % 2, :], ALU.add).then_inc(x_acc, 1)

                    def pair_prod(j):
                        dve.wait_ge(esilu_ok, j + 1)
                        if j:
                            dve.wait_ge(et_full, 2 * j)
                        v.tensor_tensor(eprod[:, :], euB[:, 0:F], esilu[:, :], ALU.mult).then_inc(eprod_ok, 1)

                    def combine(g, m):
                        i = g * GT + m
                        dve.wait_ge(y_in[i % 2], 16 * TOP_K * (i // 2 + 1))
                        y = lambda k: yg[:, i % 2, k, :]
                        dve.wait_ge(x_acc, tile(len(PARTS) - 1, g, GT - 1) + 3)
                        link(v.tensor_scalar(ytmp[:, 0, :], y(0), slotw[:, i, 0:1], None, ALU.mult))
                        for k in range(1, TOP_K):
                            link(v.scalar_tensor_tensor(ytmp[:, 0, :], y(k), slotw[:, i, k:k + 1], ytmp[:, 0, :], ALU.mult, ALU.add))
                        v.tensor_tensor(ytmp[:, 0, :], ytmp[:, 0, :], gate_b[:, i // BT, :], ALU.mult).then_inc(y_used, 1)
                        dve.wait_ge(y_used, i + 1)
                        v.tensor_tensor(xres[:, i, :], xres[:, i, :], ytmp[:, 0, :], ALU.add).then_inc(final_ok, 1)
                        dve.wait_ge(final_ok, i + 1)

                    for p, n in enumerate(PARTS):
                        lo_weights(p, 0)
                        lo_weights(p, 1)
                        for g in range(NG):
                            lo_group(p, g)
                            if g == 0:
                                lo_weights(p, 2)
                            pairs = [pair(p, g, h) for h in range(2)] if p in PAIR_PARTS else None
                            gate_up(p, g, 0)
                            gate_up(p, g, 1)
                            if pairs:
                                pair_prod(pairs[0])
                            if n > 2:
                                gate_up(p, g, 2)
                            down(p, g, 0)
                            down(p, g, 1)
                            if pairs:
                                pair_prod(pairs[1])
                            down(p, g, 2)
                            down(p, g, 3)
                            if p == len(PARTS) - 1:
                                for m in range(GT):
                                    combine(g, m)

                @block.tensor
                def _(pe):
                    mm = nc.tensor
                    for s_ in (d_used0, d_used1):
                        pe.sem_inc(s_, 1)
                    for g in range(NG):
                        for c in range(C):
                            ins = mm.matmul(bank[4 + g][0:R, :], wrN[:, c, :], h2T[:, c, g * GW:(g + 1) * GW], start=(c == 0), stop=(c == C - 1))
                        ins.then_inc(lt_full, 1)
                    pe.wait_ge(lt_ok, NG)
                    for n in range(2):
                        for i in range(BT):
                            t = n * BT + i
                            ins = mm.transpose(bank[4 + n][:, i * R:(i + 1) * R], logT[:, t * P:(t + 1) * P], ident[0:R, 0:R])
                        ins.then_inc(lg_full, 1)
                    pe.wait_ge(mask_ok, 1)
                    mm.matmul(bank[6][:, :], tri[:, :], mask.rearrange("p i e -> p (i e)"), start=True, stop=False)
                    mm.matmul(bank[6][:, :], ones[:, :], before.rearrange("p i e -> p (i e)"), start=False, stop=True).then_inc(pos_full, 1)

                    def gate_up(p, g, f):
                        n = chunk(p, g, f)
                        for w, (bk, free, full) in enumerate(((gB, silu_ok, g_full), (uB, prod_ok, u_full))):
                            pe.wait_ge(free, n + 1)
                            k = 0
                            for c in range(C):
                                if f == 0 and w == 0:
                                    pe.wait_ge(xlo_ok, (p * NG + g) * C + c + 1)
                                at = slice(f * P, (f + 1) * P)
                                for l, r in ((wguH, xsH), (wguL, xsH), (wguH, xsL)):
                                    ins = mm.matmul(bk[:, :], l[:, w, c, at], r[:, c, :], start=(k == 0), stop=(k == 3 * C - 1))
                                    k += 1
                            ins.then_inc(full, 1)

                    def down(p, g, m):
                        n, nf = tile(p, g, m), PARTS[p]
                        pe.wait_ge(d_used[m % 2], n // 2 + 1)
                        if m == 0:
                            pe.wait_ge(plo_ok, chunk(p, g, nf) + 1)
                        k = 0
                        for f in range(nf):
                            for l, r in ((prodH, wdH), (prodH, wdL), (prodL, wdH)):
                                ins = mm.matmul(dB[m % 2][:, :], l[:, f, m * P:(m + 1) * P], r[:, f, :], start=(k == 0), stop=(k == 3 * nf - 1))
                                k += 1
                        ins.then_inc(d_full[m % 2], 1)

                    def pair_rows(j):
                        pe.wait_ge(xg_in, 16 * (j + 1))
                        if j:
                            pe.wait_ge(et_taken, 2 * j)
                        rows_v = xg[:, :].rearrange("s (p c) -> s c p", c=C)
                        for c in range(C):
                            ins = mm.transpose(etB[:, c * P:(c + 1) * P], rows_v[:, c, :], ident[:, :])
                        ins.then_inc(et_full, 1)

                    def pair_gate_up(j):
                        pe.wait_ge(gu_in, 64 * (j + 1))
                        pe.wait_ge(et_taken, 2 * j + 1)
                        if j:
                            pe.wait_ge(eprod_ok, j)
                        for c in range(C):
                            for w, bk in enumerate((egB, euB)):
                                for e in range(2):
                                    half = slice(e * CAP, (e + 1) * CAP)
                                    ins = mm.matmul(bk[half, 0:F], xeT[:, c, half], egu[:, e, w, c, :], start=(c == 0), stop=(c == C - 1))
                        ins.then_inc(eg_full, 1)

                    def pair_turned(j):
                        pe.wait_ge(eprod_ok, j + 1)
                        for c, (lo, n) in enumerate(FC):
                            ins = mm.transpose(etB[0:n, c * P:(c + 1) * P], eprod[:, lo:lo + n], ident[:, :])
                        ins.then_inc(et_full, 1)

                    def pair_down(j):
                        pe.wait_ge(dn_in, 64 * (j + 1))
                        pe.wait_ge(et_taken, 2 * j + 2)
                        if j:
                            pe.wait_ge(ye_ok, j)
                        for c, (lo, n) in enumerate(FC):
                            for e in range(2):
                                half = slice(e * CAP, (e + 1) * CAP)
                                ins = mm.matmul(eyB[half, :], epT[0:n, c, half], ed[0:n, e, c, :], start=(c == 0), stop=(c == len(FC) - 1))
                        ins.then_inc(ey_full, 1)

                    for p, n in enumerate(PARTS):
                        pe.wait_ge(wlo_ok, 3 * p + 2)
                        for g in range(NG):
                            pairs = [pair(p, g, h) for h in range(2)] if p in PAIR_PARTS else None
                            gate_up(p, g, 0)
                            if pairs:
                                pair_rows(pairs[0])
                            gate_up(p, g, 1)
                            if pairs:
                                pair_gate_up(pairs[0])
                            if n > 2:
                                gate_up(p, g, 2)
                            if pairs:
                                pair_turned(pairs[0])
                            if g == 0:
                                pe.wait_ge(wlo_ok, 3 * p + 3)
                            down(p, g, 0)
                            if pairs:
                                pair_down(pairs[0])
                                pair_rows(pairs[1])
                            down(p, g, 1)
                            if pairs:
                                pair_gate_up(pairs[1])
                            down(p, g, 2)
                            if pairs:
                                pair_turned(pairs[1])
                                pair_down(pairs[1])
                            down(p, g, 3)


_INS = ['L0_attn_x', 'L0_attn_Wk', 'L0_attn_Wv', 'L0_attn_Wo', 'L0_attn_Wts', 'L0_attn_gate', 'L0_attn_time_decay',
        'L0_attn_time_first', 'L0_attn_ln_w', 'L0_attn_ln_b', 'L0_ffn_Wr', 'L0_ffn_Wg', 'L0_ffn_Wu', 'L0_ffn_Wd',
        'L0_ffn_Wsg', 'L0_ffn_Wsu', 'L0_ffn_Wsd', 'L0_ffn_Wse', 'L0_c', 'L0_wmod']
_OUTS = [((2, 1024, 512), 'float32')]


def kernel(**inputs):
    import numpy as _np
    import concourse.bacc as _bacc
    from concourse import mybir as _mybir
    from concourse.bass_utils import run_bass_kernel_spmd as _run

    nc = _bacc.Bacc("TRN2", target_bir_lowering=False, num_devices=1)
    arrays, args = {}, []
    for name in _INS:
        a = _np.ascontiguousarray(inputs[name])
        arrays[f"in_{name}_dram"] = a
        args.append(nc.dram_tensor(f"in_{name}_dram", a.shape, _mybir.dt.from_np(a.dtype), kind="ExternalInput").ap())
    for i, (shape, dtype) in enumerate(_OUTS):
        dt = _mybir.dt.from_np(_np.dtype(dtype))
        args.append(nc.dram_tensor(f"out_{i}_dram", shape, dt, kind="ExternalOutput").ap())
    build(nc, *args)
    r = _run(nc, [arrays], core_ids=[0])
    got = tuple(r.results[0][f"out_{i}_dram"] for i in range(len(_OUTS)))
    return got[0]
```

```python
from contextlib import ExitStack

import concourse.bass as bass
from concourse import mybir

F32 = mybir.dt.float32
F32R = mybir.dt.float32r
U32 = mybir.dt.uint32
ALU = mybir.AluOpType
ACT = mybir.ActivationFunctionType
AX = mybir.AxisListType

P = 128
LN_EPS = 1e-5
GATE_FLOOR = 0.25
TOP_K = 4
CAP = 64
FAR = 1 << 16


class Tally:

    def __init__(self, sem, start=0):
        self.sem, self.at, self.n = sem, start, 0

    def loop(self, var, per):
        self.start, self.per = self.at + self.n, per
        self.at, self.n = self.start + var * per, 0

    def end(self, times):
        assert self.n == self.per, (self.sem, self.n, self.per)
        self.at, self.n = self.start + self.per * times, 0

    def tick(self, k=1):
        self.n += k
        return self.at + self.n

    def last(self):
        return self.at + self.n


def row(ap):
    return ap.rearrange("p a n -> p (a n)")


def build(nc, x, Wk, Wv, Wo, Wts, gate, time_decay, time_first, ln_w, ln_b,
          Wr, Wg, Wu, Wd, Wsg, Wsu, Wsd, Wse, c_in, wmod, out):
    B, T, H = x.shape
    S = Wk.shape[0]
    E, _, F = Wg.shape
    FS = Wsg.shape[1]
    C = H // P
    NT = B * T // P
    BT = T // P
    HB = BT // 2
    GT = 4
    GW = GT * P
    NG = NT // GT
    BG = BT // GT
    NP = E // 2
    FC = [(0, P), (P, P), (2 * P, F - 2 * P)]
    PC = 3
    PARTS = [PC, PC, PC, FS // P - 3 * PC]
    PAIR_PARTS = (1, 2)
    R = E + 2
    assert (H, S, C, CAP * 2, BT, NP, FS % P) == (512, 64, 4, P, 8, 16, 0)
    assert len(PAIR_PARTS) * NG * 2 == NP

    h2_dram = nc.dram_tensor("h2_rows", (B * T, H), F32, kind="Internal").ap()
    ye_dram = nc.dram_tensor("expert_rows", (E * CAP, H), F32, kind="Internal").ap()
    tok_dram = nc.dram_tensor("slot_tokens", (E * CAP, 1), U32, kind="Internal").ap()

    x_rows = x.rearrange("b (i p) h -> p (b i) h", p=P)
    out_rows = out.rearrange("b (i p) h -> p (b i) h", p=P)
    wmod_v = wmod.rearrange("(k p) n -> p k n", p=P)

    with ExitStack() as ctx:
        def sb(name, shape, dt=F32, scope=ctx):
            return scope.enter_context(nc.sbuf_tensor(name, shape, dt))

        def sems(names):
            return [ctx.enter_context(nc.semaphore(n)) for n in names.split()]

        xres = sb("xres", [P, NT, H])
        h2T = sb("h2T", [P, C, B * T])
        gate_b = sb("gate_b", [P, B, H])
        ident = sb("ident", [P, P])
        wrN = sb("wrN", [P, C, R])

        with ExitStack() as first_use:
            hT = sb("hT", [P, 2, C, T], F32R, first_use)
        wguN = sb("wguN", [P, 2, C, PC * P])
        wdN = sb("wdN", [P, PC, H])
        prodH = sb("prodH", [P, PC, GW], F32R)
        prodL = sb("prodL", [P, PC, GW], F32R)
        silu = sb("silu", [P, GW])
        assert 2 * C * T == 2 * C * PC * P + PC * H + 2 * PC * GW + GW
        w_in = sems("w_in")[0]
        wsg_v = Wsg.rearrange("(c p) f -> p c f", p=P)
        wsu_v = Wsu.rearrange("(c p) f -> p c f", p=P)

        def load_shared(sp, p):
            lo, n = P * sum(PARTS[:p]), PARTS[p]
            sp.dma_start(wguN[:, 0, :, 0:n * P], wsg_v[:, :, lo:lo + n * P]).then_inc(w_in, 16)
            sp.dma_start(wguN[:, 1, :, 0:n * P], wsu_v[:, :, lo:lo + n * P]).then_inc(w_in, 16)
            sp.dma_start(wdN[:, 0:n, :], Wsd[lo:lo + n * P, :].rearrange("(f p) h -> p f h", p=P)).then_inc(w_in, 16)

        bank = [ctx.enter_context(nc.psum_tensor(f"bank{i}", [P, 512], F32)) for i in range(8)]

        with ExitStack() as pa:
            hTH, hTL = hT[:, 0, :, :], hT[:, 1, :, :]
            xhat = sb("xhat", [P, BT, H], F32, pa)
            bc = sb("bc", [P, 4, B, H], F32, pa)
            wtsH = sb("wtsH", [P, C, H], F32R, pa)
            wtsL = sb("wtsL", [P, C, H], F32R, pa)
            xnTH = sb("xnTH", [P, C, GW], F32R, pa)
            xnTL = sb("xnTL", [P, C, GW], F32R, pa)
            mix = sb("mix", [P, 2, H], F32, pa)
            h2r = sb("h2r", [P, 2, H], F32, pa)
            xs = sb("xs", [P, 2, H], F32, pa)
            xn = sb("xn", [P, 2, H], F32, pa)
            kE = sb("kE", [S, GW], F32, pa)
            vV = sb("vV", [S, GW], F32, pa)
            states = sb("states", [S, T], F32, pa)
            woT = sb("woT", [S, B, H], F32, pa)
            kvH = sb("kvH", [P, C, P], F32R, pa)
            kvL = sb("kvL", [P, C, P], F32R, pa)
            rows = sb("rows", [24, P], F32, pa)
            cols = sb("cols", [P, 24], F32, pa)
            cT = sb("cT", [P, C, B], F32, pa)
            gcol = sb("gcol", [P, 2, C], F32, pa)
            ecol = sb("ecol", [P, 12], F32, pa)
            wcol = sb("wcol", [S, 4], F32, pa)
            kvbias = sb("kvbias", [S, 2], F32, pa)
            modc = sb("modc", [P, 6, C, B], F32, pa)
            dcol = sb("dcol", [P, B, 8, C], F32, pa)
            tmpc = sb("tmpc", [P, 3, C, B], F32, pa)
            st6 = sb("st6", [P, 6], F32, pa)
            mv1 = sb("mv1", [P, BT, 2], F32, pa)
            mv2 = sb("mv2", [P, 2, 2], F32, pa)
            ve = sb("ve", [P, BT], F32, pa)
            ve2 = sb("ve2", [P, 2], F32, pa)
            neg_half = sb("neg_half", [P, BT], F32, pa)
            rs = sb("rs", [P, BT], F32, pa)
            rs2 = sb("rs2", [P, 2], F32, pa)
            stage = [h2T[:, :, k * H:(k + 1) * H] for k in range(3)]
            wtsT = h2T[:, :, 3 * H:4 * H]
            woN = h2r[:, 0, 0:C * S].rearrange("p (c s) -> p c s", c=C)
            woS = h2r[:, 1, 0:C * B * S].rearrange("p (c b s) -> p c b s", c=C, b=B)
            kvN = xn[:, 0, :]
            kvT = xs[:, 1, :].rearrange("p (c m) -> p c m", c=C)

            (rows_zero, const_ok, cols_in, kv_in, wo_in, wr_in, stage_in0, stage_in1, stage_in2,
             col_full, col_ok, exp_ok, silu_c_ok, wts_scaled, wtsT_ok, kvT_ok, kvH_ok, kvL_ok, bias_full, kvb_ok,
             sa_ok, spread_ok, mod_ok, wo_scaled, wts_hi, wts_lo, mod_done,
             xhat_ok, hi_ok, s_full0, s_full1, s_taken0, s_taken1, mix_ok, normed, h2_ok,
             h2_sent0, h2_sent1, h2_free, kv_full, kv_read, e_neg, e_sig, e_fac, st_ok, ve_ok, rs_ok, dve_self, pool_self) = sems(
                 "rows_zero const_ok cols_in kv_in wo_in wr_in stage_in0 stage_in1 stage_in2 "
                 "col_full col_ok exp_ok silu_c_ok wts_scaled wtsT_ok kvT_ok kvH_ok kvL_ok bias_full kvb_ok "
                 "sa_ok spread_ok mod_ok wo_scaled wts_hi wts_lo mod_done "
                 "xhat_ok hi_ok s_full0 s_full1 s_taken0 s_taken1 mix_ok normed h2_ok "
                 "h2_sent0 h2_sent1 h2_free kv_full kv_read e_neg e_sig e_fac st_ok ve_ok rs_ok dve_self pool_self")
            x_in = [sems(f"x_in{b}{h}")[0] for b in range(B) for h in range(2)]
            stage_in = (stage_in0, stage_in1, stage_in2)
            h2_sent = (h2_sent0, h2_sent1)
            NTB = 3
            t_full = [sems(f"t_full{k}")[0] for k in range(NTB)]
            t_taken = [sems(f"t_taken{k}")[0] for k in range(NTB)]
            s_full, s_taken = (s_full0, s_full1), (s_taken0, s_taken1)

            tb, sbk, kvb, modb, biasb = [bank[0], bank[1], bank[6]], bank[2:4], bank[4], bank[5], bank[7]
            GATE, LNW, LNB, CC, TD, TF = 0, 4, 8, 12, 20, 21
            M_CA, M_SA, M_GA, M_SB, M_CB, M_GB = range(6)
            BLOCK = [1, 0, 2, 3, 4, 5]
            STAGE = [1, 2, 0, 1, 2, 0]
            MOD_AT, WSA_AT, KVB_AT = 32, 0, 16
            K_1CA, K_A, K_B, K_1CB, K_SB, K_GB, K_GA = range(7)
            PLACE = {K_A: 0, K_B: 1, K_1CB: 2, K_SB: 3}
            FIRST = [(i + HB) % BT for i in range(BT)]

            TURNS = [("wts", q) for q in range(C)] + [("kv",)] + [("h", 0, i) for i in FIRST]
            TURNS += [("spread", 0, K_A), ("spread", 0, K_B)]
            LAG, LAG2 = 2, 3

            def mixer_turns(b, i):
                t = []
                if b and i < LAG2:
                    t.append(("h2", b - 1, BT - LAG2 + i))
                if i >= LAG:
                    t.append(("xn", b, i - LAG))
                if b == 0 and i == BT - 2:
                    t += [("wo", 0), ("wo", 1)]
                if b == 0 and i == BT - 1:
                    t += [("spread", 0, K_1CB), ("spread", 0, K_SB), ("spread", 1, K_A), ("spread", 1, K_B)]
                return t

            def last_turns(b):
                before = [("xn", b, i) for i in range(BT - LAG, BT)]
                after = []
                if b + 1 < B:
                    before += [("h", b + 1, i) for i in FIRST[0:2]]
                    after += [("h", b + 1, i) for i in FIRST[2:HB]]
                    after += [("spread", 0, K_GB)] + [("spread", 1, k) for k in (K_1CB, K_SB, K_GB)]
                return before, after

            def out_turns(b, i):
                t = []
                if b + 1 < B and i < HB:
                    t.append(("h", b + 1, FIRST[HB + i]))
                if i >= LAG2:
                    t.append(("h2", b, i - LAG2))
                return t

            for b in range(B):
                for i in range(BT):
                    TURNS += mixer_turns(b, i)
                TURNS += last_turns(b)[0] + last_turns(b)[1]
                for i in range(BT):
                    TURNS += out_turns(b, i)
            TURNS += [("h2", B - 1, i) for i in range(BT - LAG2, BT)]
            SPLITS = [t for t in TURNS if t[0] in ("h", "xn")]
            NORMS = [(k, b, i) for b in range(B) for k in ("xn", "h2") for i in range(BT)]
            RSTDS = [("h", 0, 1), ("h", 0, 0)]
            for b in range(B):
                RSTDS += [("xn", b, i) for i in range(BT)]
                if b + 1 < B:
                    RSTDS += [("h", b + 1, 1), ("h", b + 1, 0)]
                RSTDS += [("h2", b, i) for i in range(BT)]

            def turn_full(eng, t):
                q = TURNS.index(t)
                eng.wait_ge(t_full[q % NTB], q // NTB + 1)

            def turn_taken(eng, t):
                q = TURNS.index(t)
                eng.wait_ge(t_taken[q % NTB], q // NTB + 1)

            def s_use(n, b):
                return b * BT + (n // 2 + 1)

            def mixers_done(eng, b):
                for i in (BT - 2, BT - 1):
                    eng.wait_ge(s_full[i % 2], s_use(i, b))

            with nc.Block() as block:

                @block.sync
                def _(sp):
                    sp.wait_ge(rows_zero, 1)
                    for src, r in ((gate, GATE), (ln_w, LNW), (ln_b, LNB)):
                        sp.dma_start(rows[r:r + C, :], src.rearrange("(c p) -> c p", p=P)).then_inc(cols_in, 16)
                    sp.dma_start(rows[CC:CC + B * C, :], c_in.rearrange("b (c p) -> (b c) p", p=P)).then_inc(cols_in, 16)
                    for src, r in ((time_decay, TD), (time_first, TF)):
                        sp.dma_start(rows[r:r + 1, 0:S], src.rearrange("(a s) -> a s", a=1)).then_inc(cols_in, 16)
                    sp.dma_start(stage[0], Wts.rearrange("(c p) d -> p c d", p=P)).then_inc(stage_in0, 16)
                    sp.dma_start(kvN[0:S, :], Wk).then_inc(kv_in, 16)
                    sp.dma_start(kvN[S:2 * S, :], Wv).then_inc(kv_in, 16)
                    for j in range(6):
                        if j == 2:
                            turn_full(sp, ("wts", C - 1))
                        elif j > 2:
                            sp.wait_ge(mod_done, j - 2)
                        sp.dma_start(stage[STAGE[j]], wmod_v[:, :, BLOCK[j] * 512:(BLOCK[j] + 1) * 512]).then_inc(stage_in[STAGE[j]], 16)
                        if j == 1:
                            sp.dma_start(woN, Wo.rearrange("(c p) s -> p c s", p=P)).then_inc(wo_in, 16)
                            sp.dma_start(wrN[:, :, 0:E], Wr.rearrange("(c p) e -> p c e", p=P)).then_inc(wr_in, 16)
                            with nc.allow_non_contiguous_dma(reason="one column"):
                                sp.dma_start(wrN[:, :, E:E + 1], Wse.rearrange("(c p) e -> p c e", p=P)).then_inc(wr_in, 16)
                    sp.wait_ge(wr_in, 32)
                    for b in range(B):
                        if b == B - 1:
                            mixers_done(sp, b)
                            load_shared(sp, 0)
                        for i in range(BT):
                            n = b * BT + i
                            sp.wait_ge(h2_ok, n + 1)
                            sp.dma_start(h2_dram[n * P:(n + 1) * P, :], h2r[:, i % 2, :]).then_inc(h2_sent[i % 2], 16)
                            if n:
                                sp.wait_ge(h2_sent[(n - 1) % 2], 16 * ((n - 1) // 2 + 1))
                                sp.sem_inc(h2_free, 1)
                    sp.wait_ge(h2_sent[(B * BT - 1) % 2], 16 * (B * BT // 2))

                @block.gpsimd
                def _(pool):
                    g = nc.gpsimd
                    own = Tally(pool_self)
                    g.memset(rows[:, :], 0.0).then_inc(rows_zero, 1)
                    g.memset(ident[:, :], 0.0).then_inc(pool_self, 1)
                    g.memset(neg_half[:, :], -0.5).then_inc(pool_self, 1)
                    own.tick()
                    pool.wait_ge(pool_self, own.tick())
                    g.affine_select(out=ident[:, :], in_=ident[:, :], compare_op=ALU.not_equal, fill=1.0,
                                    base=0, pattern=[[-1, P]], channel_multiplier=1).then_inc(const_ok, 1)

                    def rstd(kind, b, i):
                        pool.wait_ge(ve_ok, RSTDS.index((kind, b, i)) + 1)
                        if kind == "h":
                            at = slice(i * HB, (i + 1) * HB)
                            g.tensor_tensor(rs[:, at], ve[:, at], neg_half[:, at], ALU.pow).then_inc(rs_ok, 1)
                        else:
                            at = slice(i % 2, i % 2 + 1)
                            g.tensor_tensor(rs2[:, at], ve2[:, at], neg_half[:, 0:1], ALU.pow).then_inc(rs_ok, 1)

                    def mix_rows(b, i):
                        if i > 1:
                            pool.wait_ge(s_taken[i % 2], s_use(i - 2, b) + 1)
                        if i == 0:
                            turn_taken(pool, ("spread", b, K_A))
                        pool.wait_ge(xhat_ok, b * BT + FIRST.index(i) + 1)
                        g.tensor_tensor(mix[:, i % 2, :], xhat[:, i, :], bc[:, PLACE[K_A], b, :], ALU.mult).then_inc(pool_self, 1)
                        if i == 0:
                            turn_taken(pool, ("spread", b, K_B))
                        pool.wait_ge(pool_self, own.tick())
                        g.tensor_tensor(mix[:, i % 2, :], mix[:, i % 2, :], bc[:, PLACE[K_B], b, :], ALU.add).then_inc(mix_ok, 1)

                    def h2_rows(b, i):
                        n = b * BT + i
                        pool.wait_ge(normed, NORMS.index(("h2", b, i)) + 1)
                        if n > 1:
                            pool.wait_ge(h2_free, n - 1)
                            turn_full(pool, ("h2", (n - 2) // BT, (n - 2) % BT))
                        if i == 0:
                            turn_taken(pool, ("spread", b, K_1CB))
                            turn_taken(pool, ("spread", b, K_SB))
                        if n == 0:
                            turn_full(pool, ("wo", 1))
                        g.tensor_tensor(h2r[:, i % 2, :], xn[:, i % 2, :], bc[:, PLACE[K_1CB], b, :], ALU.mult).then_inc(pool_self, 1)
                        pool.wait_ge(pool_self, own.tick())
                        g.tensor_tensor(h2r[:, i % 2, :], h2r[:, i % 2, :], bc[:, PLACE[K_SB], b, :], ALU.add).then_inc(h2_ok, 1)

                    rstd("h", 0, 1)
                    rstd("h", 0, 0)
                    for b in range(B):
                        mix_rows(b, 0)
                        if b:
                            h2_rows(b - 1, BT - 1)
                        for i in range(BT):
                            if i + 1 < BT:
                                mix_rows(b, i + 1)
                            rstd("xn", b, i)
                        if b + 1 < B:
                            rstd("h", b + 1, 1)
                            rstd("h", b + 1, 0)
                        for i in range(BT):
                            rstd("h2", b, i)
                            if i:
                                h2_rows(b, i - 1)
                        if b == B - 1:
                            h2_rows(b, BT - 1)

                @block.scalar
                def _(act):
                    a = nc.scalar

                    def load_x(b, h):
                        lo = b * BT + h * HB
                        act.dma_start(xres[:, lo:lo + HB, :], x_rows[:, lo:lo + HB, :]).then_inc(x_in[b * 2 + h], 16)

                    def take(t):
                        q, kind = TURNS.index(t), t[0]
                        src = tb[q % NTB]
                        wide = src[:, :].rearrange("p (c m) -> p c m", c=C)
                        turn_full(act, t)
                        if kind == "wts":
                            a.activation(wtsT[:, t[1], :], src[:, :], ACT.Copy).then_inc(t_taken[q % NTB], 1)
                        elif kind == "kv":
                            a.activation(kvT, wide, ACT.Copy).then_inc(t_taken[q % NTB], 1)
                        elif kind == "wo":
                            a.activation(woT[:, t[1], :], src[0:S, :], ACT.Copy).then_inc(t_taken[q % NTB], 1)
                        elif kind == "spread":
                            dst = gate_b[:, t[1], :] if t[2] == K_GB else bc[:, PLACE[t[2]], t[1], :]
                            a.activation(dst, src[:, :], ACT.Copy).then_inc(t_taken[q % NTB], 1)
                        elif kind == "h":
                            _, b, i = t
                            if b and i == FIRST[0]:
                                mixers_done(act, b - 1)
                            a.activation(hTH[:, :, i * P:(i + 1) * P], wide, ACT.Copy).then_inc(hi_ok, 1)
                        elif kind == "xn":
                            _, b, i = t
                            k = b * BG + i // GT
                            if k and i % GT == 0:
                                act.wait_ge(kv_full, k)
                            at = (i % GT) * P
                            a.activation(xnTH[:, :, at:at + P], wide, ACT.Copy).then_inc(hi_ok, 1)
                        else:
                            n = t[1] * BT + t[2]
                            a.activation(h2T[:, :, n * P:(n + 1) * P], wide, ACT.Copy).then_inc(t_taken[q % NTB], 1)

                    def scale_weights(b):
                        if b:
                            mixers_done(act, b - 1)
                        act.wait_ge(sa_ok, 1)
                        for c in range(C):
                            a.activation(wtsH[:, c, :], wtsT[:, c, :], ACT.Copy, scale=dcol[:, b, K_1CA, c:c + 1]).then_inc(wts_hi, 1)

                    def kv_front(b, n):
                        k = b * BG + n
                        act.wait_ge(kv_full, k + 1)
                        act.wait_ge(st_ok, k + 1)
                        a.activation(kE[:, :], kvb[0:S, :], ACT.Exp, scale=-1.0, bias=kvbias[:, 0:1]).then_inc(e_neg, 1)
                        a.activation(vV[:, :], kvb[S:2 * S, :], ACT.Copy).then_inc(kv_read, 1)

                    def kv_back(b, n):
                        act.wait_ge(e_sig, b * BG + n + 1)
                        a.activation(kE[:, :], kE[:, :], ACT.Exp, scale=wcol[:, 2:3]).then_inc(e_fac, 1)

                    act.sem_inc(st_ok, 1)
                    load_x(0, 1)
                    load_x(0, 0)
                    act.wait_ge(col_ok, 1)
                    a.activation(ecol[:, 0:C], cols[:, GATE:GATE + C], ACT.Exp, scale=-1.0).then_inc(exp_ok, 1)
                    a.activation(ecol[:, C:C + B * C], cols[:, CC:CC + B * C], ACT.Exp, scale=-1.0).then_inc(exp_ok, 1)
                    a.activation(wcol[:, 0:2], cols[0:S, TD:TD + 2], ACT.Exp).then_inc(exp_ok, 1)
                    for q in range(C):
                        take(("wts", q))
                    take(("kv",))
                    turn_taken(act, ("kv",))
                    for c in range(C):
                        a.activation(kvH[:, c, :], kvT[:, c, :], ACT.Copy, scale=cols[:, LNW + c:LNW + c + 1]).then_inc(kvH_ok, 1)
                    for i in FIRST[0:HB]:
                        take(("h", 0, i))
                    load_x(1, 1)
                    load_x(1, 0)
                    for q in range(C):
                        turn_taken(act, ("wts", q))
                    scale_weights(0)
                    for i in FIRST[HB:BT]:
                        take(("h", 0, i))
                    take(("spread", 0, K_A))
                    take(("spread", 0, K_B))
                    act.wait_ge(kvb_ok, 1)

                    for b in range(B):
                        for i in range(BT):
                            for t in mixer_turns(b, i):
                                take(t)
                            if i == BT - 2:
                                kv_front(b, 0)
                            if i == BT - 1:
                                kv_back(b, 0)
                        before, after = last_turns(b)
                        for t in before:
                            take(t)
                        kv_front(b, 1)
                        for t in after:
                            take(t)
                            if t == after[1]:
                                kv_back(b, 1)
                        if not after:
                            kv_back(b, 1)
                        if b + 1 < B:
                            scale_weights(b + 1)
                        for i in range(BT):
                            for t in out_turns(b, i):
                                take(t)
                    for i in range(BT - LAG2, BT):
                        take(("h2", B - 1, i))

                @block.vector
                def _(dve):
                    v = nc.vector
                    own = Tally(dve_self)

                    def link(ins):
                        ins.then_inc(dve_self, 1)
                        dve.wait_ge(dve_self, own.tick())

                    def xrow(b, i):
                        return xres[:, b * BT + i, :]

                    def first_stats(b, i):
                        dve.wait_ge(x_in[b * 2 + i // HB], 16)
                        link(v.bn_stats(st6[:, :], xrow(b, i)))
                        link(v.bn_aggr(mv1[:, i, :], st6[:, :]))

                    def first_var(b, h):
                        at = slice(h * HB, (h + 1) * HB)
                        v.tensor_scalar(ve[:, at], mv1[:, at, 1], LN_EPS, None, ALU.add).then_inc(ve_ok, 1)

                    def first_rows(b, i):
                        dve.wait_ge(rs_ok, RSTDS.index(("h", b, i // HB)) + 1)
                        if b:
                            dve.wait_ge(mix_ok, b * BT)
                        v.tensor_scalar(xhat[:, i, :], xrow(b, i), mv1[:, i, 0:1], rs[:, i:i + 1], ALU.subtract, ALU.mult).then_inc(xhat_ok, 1)

                    def lo(t):
                        (kind, b, i), q = t, TURNS.index(t)
                        dve.wait_ge(hi_ok, SPLITS.index(t) + 1)
                        dh, dl = (hTH, hTL) if kind == "h" else (xnTH, xnTL)
                        at = slice(i * P, (i + 1) * P) if kind == "h" else slice((i % GT) * P, (i % GT + 1) * P)
                        v.tensor_tensor(dl[:, :, at], tb[q % NTB][:, :].rearrange("p (c m) -> p c m", c=C),
                                        dh[:, :, at].bitcast(F32), ALU.subtract).then_inc(t_taken[q % NTB], 1)

                    def scale_weights(b):
                        for c in range(C):
                            dve.wait_ge(wts_hi, b * C + c + 1)
                            v.scalar_tensor_tensor(wtsL[:, c, :], wtsT[:, c, :], dcol[:, b, K_1CA, c:c + 1],
                                                   wtsH[:, c, :].bitcast(F32), ALU.mult, ALU.subtract).then_inc(wts_lo, 1)

                    dk = lambda kind: dcol[:, :, kind, :].rearrange("p b c -> p c b")
                    g1 = gcol[:, 1, :].rearrange("p (c a) -> p c a", a=1).to_broadcast([P, C, B])
                    modp = lambda j, n: modb[:, MOD_AT + j * C * B:MOD_AT + (j + n) * C * B]

                    link(v.memset(wrN[:, :, E + 1:R], 0.0))
                    dve.wait_ge(col_full, 1)
                    v.tensor_copy(cols[:, :], modb[:, 0:24]).then_inc(col_ok, 1)
                    dve.wait_ge(col_ok, 1)
                    dve.wait_ge(exp_ok, 3)
                    link(v.tensor_scalar(ecol[:, :], ecol[:, :], 1.0, None, ALU.add))
                    link(v.reciprocal(ecol[:, :], ecol[:, :]))
                    link(v.tensor_copy(gcol[:, 0, :], ecol[:, 0:C]))
                    link(v.tensor_scalar(gcol[:, 1, :], ecol[:, 0:C], -1.0, 1.0, ALU.mult, ALU.add))
                    link(v.tensor_scalar(wcol[:, 2:3], wcol[:, 1:2], -1.0, None, ALU.mult))
                    v.tensor_tensor(cT[:, :, :], cols[:, CC:CC + B * C].rearrange("p (b c) -> p c b", b=B),
                                    ecol[:, C:C + B * C].rearrange("p (b c) -> p c b", b=B), ALU.mult).then_inc(silu_c_ok, 1)
                    dve.wait_ge(stage_in0, 16)
                    for c in range(C):
                        v.tensor_scalar(stage[0][:, c, :], stage[0][:, c, :], gcol[:, 0, c:c + 1], None, ALU.mult).then_inc(wts_scaled, 1)
                    for i in FIRST[0:HB]:
                        first_stats(0, i)
                    first_var(0, 1)
                    for c in range(C):
                        dve.wait_ge(kvH_ok, c + 1)
                        v.scalar_tensor_tensor(kvL[:, c, :], kvT[:, c, :], cols[:, LNW + c:LNW + c + 1],
                                               kvH[:, c, :].bitcast(F32), ALU.mult, ALU.subtract).then_inc(kvL_ok, 1)
                    for i in FIRST[0:HB]:
                        first_rows(0, i)
                    for i in FIRST[HB:BT]:
                        first_stats(0, i)
                    first_var(0, 0)
                    for i in FIRST[0:HB]:
                        lo(("h", 0, i))
                    for i in FIRST[HB:BT]:
                        first_rows(0, i)
                    dve.wait_ge(mod_done, 2)
                    link(v.tensor_copy(modc[:, 0:2, :, :].rearrange("p j c b -> p (j c b)"), modp(0, 2)))
                    v.tensor_scalar(dk(K_1CA), modc[:, M_CA, :, :], 1.0, None, ALU.add).then_inc(sa_ok, 1)
                    dve.wait_ge(sa_ok, 1)
                    link(v.tensor_tensor(dk(K_A), dk(K_1CA), g1, ALU.mult))
                    link(v.tensor_tensor(tmpc[:, 0, :, :], modc[:, M_SA, :, :], g1, ALU.mult))
                    scale_weights(0)
                    dve.wait_ge(bias_full, 1)
                    v.tensor_tensor(dk(K_B), biasb[:, WSA_AT:WSA_AT + C * B].rearrange("p (c b) -> p c b", c=C),
                                    tmpc[:, 0, :, :], ALU.add).then_inc(spread_ok, 1)
                    link(v.tensor_scalar(kvbias[:, 0:1], biasb[0:S, KVB_AT:KVB_AT + 1], -1.0, None, ALU.mult))
                    v.tensor_copy(kvbias[:, 1:2], biasb[0:S, KVB_AT + 1:KVB_AT + 2]).then_inc(kvb_ok, 1)
                    for i in FIRST[HB:BT]:
                        lo(("h", 0, i))

                    def derive():
                        dve.wait_ge(mod_done, 6)
                        link(v.tensor_copy(modc[:, 2:6, :, :].rearrange("p j c b -> p (j c b)"), modp(2, 4)))
                        link(v.tensor_scalar(dk(K_1CB), modc[:, M_CB, :, :], 1.0, None, ALU.add))
                        link(v.tensor_copy(dk(K_SB), modc[:, M_SB, :, :]))
                        for src, kind in ((M_GA, K_GA), (M_GB, K_GB)):
                            link(v.tensor_scalar(tmpc[:, 0, :, :], modc[:, src, :, :], 0.0, 2.0, ALU.is_ge, ALU.mult))
                            link(v.tensor_scalar(tmpc[:, 1, :, :], tmpc[:, 0, :, :], -1.0, None, ALU.add))
                            link(v.tensor_scalar(tmpc[:, 2, :, :], modc[:, src, :, :], -1.0, GATE_FLOOR, ALU.mult, ALU.max))
                            link(v.tensor_tensor(tmpc[:, 2, :, :], tmpc[:, 2, :, :], modc[:, src, :, :], ALU.max))
                            if kind == K_GA:
                                link(v.tensor_tensor(dk(kind), tmpc[:, 1, :, :], tmpc[:, 2, :, :], ALU.mult))
                            else:
                                v.tensor_tensor(dk(kind), tmpc[:, 1, :, :], tmpc[:, 2, :, :], ALU.mult).then_inc(mod_ok, 1)
                        dve.wait_ge(wo_in, 16)
                        for b in range(B):
                            for c in range(C):
                                v.tensor_scalar(woS[:, c, b, :], woN[:, c, :], dcol[:, b, K_GA, c:c + 1], None, ALU.mult).then_inc(wo_scaled, 1)

                    def stats(t, src):
                        link(v.bn_stats(st6[:, :], src))
                        n = NORMS.index(t)
                        if n > 1:
                            dve.wait_ge(normed, n - 1)
                        link(v.bn_aggr(mv2[:, n % 2, :], st6[:, :]))
                        v.tensor_scalar(ve2[:, n % 2:n % 2 + 1], mv2[:, n % 2, 1:2], LN_EPS, None, ALU.add).then_inc(ve_ok, 1)

                    def apply(t, src):
                        n = NORMS.index(t)
                        dve.wait_ge(rs_ok, RSTDS.index(t) + 1)
                        if n > 1:
                            before = NORMS[n - 2]
                            if before[0] == "xn":
                                turn_full(dve, before)
                            else:
                                dve.wait_ge(h2_ok, before[1] * BT + before[2] + 1)
                        else:
                            turn_full(dve, ("kv",))
                        v.tensor_scalar(xn[:, n % 2, :], src, mv2[:, n % 2, 0:1], rs2[:, n % 2:n % 2 + 1],
                                        ALU.subtract, ALU.mult).then_inc(normed, 1)

                    def mix_front(b, i):
                        n = NORMS.index(("xn", b, i))
                        dve.wait_ge(s_full[i % 2], s_use(i, b))
                        dve.wait_ge(mix_ok, b * BT + (i + 1))
                        if n > 1:
                            dve.wait_ge(normed, n - 1)
                        v.tensor_tensor(xs[:, i % 2, :], sbk[i % 2][:, :], mix[:, i % 2, :], ALU.add).then_inc(s_taken[i % 2], 1)
                        dve.wait_ge(s_taken[i % 2], s_use(i, b) + 1)
                        stats(("xn", b, i), xs[:, i % 2, :])

                    def kv_mid(b, n):
                        dve.wait_ge(e_neg, b * BG + n + 1)
                        link(v.tensor_scalar(kE[:, :], kE[:, :], 1.0, None, ALU.add))
                        v.reciprocal(kE[:, :], kE[:, :]).then_inc(e_sig, 1)

                    def kv_scan(b, n):
                        k = b * BG + n
                        dve.wait_ge(e_fac, k + 1)
                        dve.wait_ge(kv_read, k + 2)
                        link(v.scalar_tensor_tensor(kE[:, :], vV[:, :], kvbias[:, 1:2], kE[:, :], ALU.add, ALU.mult))
                        dve.wait_ge(st_ok, k + 1)
                        v.tensor_tensor_scan(states[:, n * GW:(n + 1) * GW], wcol[:, 0:1].to_broadcast([S, GW]), kE[:, :],
                                             states[:, n * GW - 1:n * GW] if n else 0.0, ALU.mult, ALU.add).then_inc(st_ok, 1)

                    def residual(b, i):
                        dve.wait_ge(s_full[i % 2], s_use(BT + i, b))
                        v.tensor_tensor(xrow(b, i), sbk[i % 2][:, :], xrow(b, i), ALU.add).then_inc(s_taken[i % 2], 1)
                        dve.wait_ge(s_taken[i % 2], s_use(BT + i, b) + 1)
                        stats(("h2", b, i), xrow(b, i))

                    for b in range(B):
                        for i in range(BT):
                            mix_front(b, i)
                            if i:
                                apply(("xn", b, i - 1), xs[:, (i - 1) % 2, :])
                            if i == BT - 1:
                                kv_mid(b, 0)
                            if i >= LAG:
                                lo(("xn", b, i - LAG))
                            if b == 0 and i == BT - 3:
                                derive()
                        apply(("xn", b, BT - 1), xs[:, (BT - 1) % 2, :])
                        kv_scan(b, 0)
                        if b + 1 < B:
                            for i in FIRST[0:HB]:
                                first_stats(b + 1, i)
                            first_var(b + 1, 1)
                        lo(("xn", b, BT - 2))
                        lo(("xn", b, BT - 1))
                        if b + 1 < B:
                            for i in FIRST[0:HB]:
                                first_rows(b + 1, i)
                        kv_mid(b, 1)
                        if b + 1 < B:
                            lo(("h", b + 1, FIRST[0]))
                            lo(("h", b + 1, FIRST[1]))
                            for i in FIRST[HB:HB + 2]:
                                first_stats(b + 1, i)
                        kv_scan(b, 1)
                        if b + 1 < B:
                            lo(("h", b + 1, FIRST[2]))
                            lo(("h", b + 1, FIRST[3]))
                            for i in FIRST[HB + 2:BT]:
                                first_stats(b + 1, i)
                            first_var(b + 1, 0)
                            for i in FIRST[HB:BT]:
                                first_rows(b + 1, i)
                        for i in range(BT):
                            residual(b, i)
                            if b + 1 < B and i < HB:
                                lo(("h", b + 1, FIRST[HB + i]))
                            if b + 1 < B and i == HB:
                                scale_weights(b + 1)
                            if i:
                                apply(("h2", b, i - 1), xrow(b, i - 1))
                        apply(("h2", b, BT - 1), xrow(b, BT - 1))

                @block.tensor
                def _(pe):
                    m = nc.tensor
                    for s_ in (s_taken0, s_taken1, kv_read):
                        pe.sem_inc(s_, 1)
                    pe.wait_ge(const_ok, 1)
                    pe.wait_ge(cols_in, 96)
                    m.transpose(modb[:, 0:24], rows[:, :], ident[0:24, 0:24]).then_inc(col_full, 1)

                    def turn(t):
                        q, kind = TURNS.index(t), t[0]
                        if q >= NTB:
                            pe.wait_ge(t_taken[q % NTB], q // NTB)
                        dst = tb[q % NTB]
                        if kind == "spread":
                            if t[2] in (K_A, K_B):
                                pe.wait_ge(spread_ok, 1)
                            else:
                                pe.wait_ge(mod_ok, 1)
                            for c in range(C):
                                ins = m.matmul(dst[:, c * P:(c + 1) * P], dcol[:, t[1], t[2], c:c + 1].to_broadcast([P, P]),
                                               ident[:, :], start=True, stop=True)
                            ins.then_inc(t_full[q % NTB], 1)
                            return
                        if kind == "wts":
                            pe.wait_ge(wts_scaled, C)
                            src = [stage[0][:, c, t[1] * P:(t[1] + 1) * P] for c in range(C)]
                        elif kind == "wo":
                            pe.wait_ge(wo_scaled, (t[1] + 1) * C)
                            src, dst = [woS[:, c, t[1], :] for c in range(C)], dst[0:S, :]
                        else:
                            if kind == "kv":
                                pe.wait_ge(kv_in, 32)
                                r = kvN
                            elif kind == "h":
                                pe.wait_ge(xhat_ok, t[1] * BT + FIRST.index(t[2]) + 1)
                                r = xhat[:, t[2], :]
                            elif kind == "xn":
                                pe.wait_ge(normed, NORMS.index(t) + 1)
                                r = xn[:, t[2] % 2, :]
                            else:
                                pe.wait_ge(h2_ok, t[1] * BT + t[2] + 1)
                                r = h2r[:, t[2] % 2, :]
                            src = [r[:, c * P:(c + 1) * P] for c in range(C)]
                        for c in range(C):
                            ins = m.transpose(dst[:, c * P:(c + 1) * P], src[c], ident[:, :])
                        ins.then_inc(t_full[q % NTB], 1)

                    def modulation(j):
                        if j == 0:
                            pe.wait_ge(silu_c_ok, 1)
                        uses = [k for k in range(j + 1) if STAGE[k] == STAGE[j]]
                        pe.wait_ge(stage_in[STAGE[j]], 16 * (len(uses) + (STAGE[j] == 0)))
                        for cc in range(C):
                            at = MOD_AT + (j * C + cc) * B
                            for k in range(C):
                                ins = m.matmul(modb[:, at:at + B], stage[STAGE[j]][:, k, cc * P:(cc + 1) * P], cT[:, k, :],
                                               start=(k == 0), stop=(k == C - 1))
                        ins.then_inc(mod_done, 1)

                    def mixer(b, i):
                        s = FIRST[i]
                        pe.wait_ge(s_taken[i % 2], s_use(i, b))
                        turn_taken(pe, ("h", b, s))
                        if i == 0:
                            pe.wait_ge(wts_lo, (b + 1) * C)
                        k = 0
                        for c in range(C):
                            for l, r in ((hTH, wtsH), (hTH, wtsL), (hTL, wtsH)):
                                ins = m.matmul(sbk[i % 2][:, :], l[:, c, s * P:(s + 1) * P], r[:, c, :],
                                               start=(k == 0), stop=(k == 3 * C - 1))
                                k += 1
                        ins.then_inc(s_full[i % 2], 1)

                    def keys_values(b, n):
                        for i in range(n * GT, (n + 1) * GT):
                            turn_taken(pe, ("xn", b, i))
                        pe.wait_ge(kv_read, b * BG + (n + 1))
                        if b == 0 and n == 0:
                            pe.wait_ge(kvL_ok, C)
                        k = 0
                        for c in range(C):
                            for l, r in ((kvH, xnTH), (kvH, xnTL), (kvL, xnTH)):
                                ins = m.matmul(kvb[:, :], l[:, c, :], r[:, c, :], start=(k == 0), stop=(k == 3 * C - 1))
                                k += 1
                        ins.then_inc(kv_full, 1)

                    def project(b, i):
                        pe.wait_ge(s_taken[i % 2], s_use(BT + i, b))
                        pe.wait_ge(st_ok, b * BG + (i // GT + 2))
                        if i == 0:
                            turn_taken(pe, ("wo", b))
                        m.matmul(sbk[i % 2][:, :], states[:, i * P:(i + 1) * P], woT[:, b, :],
                                 start=True, stop=True).then_inc(s_full[i % 2], 1)

                    for q in range(C):
                        turn(("wts", q))
                    turn(("kv",))
                    for i in FIRST[0:HB]:
                        turn(("h", 0, i))
                    modulation(0)
                    modulation(1)
                    pe.wait_ge(sa_ok, 1)
                    for cc in range(C):
                        at = WSA_AT + cc * B
                        for k in range(C):
                            ins = m.matmul(biasb[:, at:at + B], wtsT[:, k, cc * P:(cc + 1) * P], modc[:, M_SA, k, :],
                                           start=(k == 0), stop=(k == C - 1))
                    for w in range(2):
                        for c in range(C):
                            ins = m.matmul(biasb[0:S, KVB_AT + w:KVB_AT + w + 1], kvT[:, c, w * S:(w + 1) * S], cols[:, LNB + c:LNB + c + 1],
                                           start=(c == 0), stop=(c == C - 1))
                    ins.then_inc(bias_full, 1)
                    for i in FIRST[HB:BT]:
                        turn(("h", 0, i))
                    turn(("spread", 0, K_A))
                    turn(("spread", 0, K_B))

                    for b in range(B):
                        for i in range(BT):
                            mixer(b, i)
                            if i == GT + LAG:
                                keys_values(b, 0)
                            if b == 0 and 0 < i < 5:
                                modulation(i + 1)
                            for t in mixer_turns(b, i):
                                turn(t)
                        before, after = last_turns(b)
                        for t in before:
                            turn(t)
                        keys_values(b, 1)
                        for t in after:
                            turn(t)
                        for i in range(BT):
                            project(b, i)
                            for t in out_turns(b, i):
                                turn(t)
                    for i in range(BT - LAG2, BT):
                        turn(("h2", B - 1, i))

        with ExitStack() as pb:
            xsH = sb("xsH", [P, C, GW], F32R, pb)
            xsL = sb("xsL", [P, C, GW], F32R, pb)
            wguH = sb("wguH", [P, 2, C, PC * P], F32R, pb)
            wguL = sb("wguL", [P, 2, C, PC * P], F32R, pb)
            wdH = sb("wdH", [P, PC, H], F32R, pb)
            wdL = sb("wdL", [P, PC, H], F32R, pb)
            prod = sb("prod", [P, GW], F32, pb)
            ytmp = sb("ytmp", [P, 2, H], F32, pb)
            egu = sb("egu", [P, 2, 2, C, F], F32, pb)
            ed = sb("ed", [P, 2, len(FC), H], F32, pb)
            xg = sb("xg", [P, H], F32, pb)
            xeT = sb("xeT", [P, C, P], F32, pb)
            esilu = sb("esilu", [P, F], F32, pb)
            eprod = sb("eprod", [P, F], F32, pb)
            epT = sb("epT", [P, len(FC), P], F32, pb)
            ye = sb("ye", [P, H], F32, pb)
            tri = sb("tri", [P, P], F32, pb)
            ones = sb("ones", [P, P], F32, pb)
            iota_e = sb("iota_e", [P, E], F32, pb)
            iota_i = sb("iota_i", [P, E], U32, pb)
            tok_id = sb("tok_id", [P, NT], U32, pb)
            zero_u = sb("zero_u", [P, NP], U32, pb)
            slotw = sb("slotw", [P, NT, TOP_K], F32, pb)
            sigma = sb("sigma", [P, NT], F32, pb)
            y_idx = sb("y_idx", [P, NT, TOP_K], U32, pb)
            t_idx = sb("t_idx", [P, NT, TOP_K], U32, pb)
            slot_tok = sb("slot_tok", [P, NP], U32, pb)
            rmax = sb("rmax", [P, NT], F32, pb)
            top8 = sb("top8", [P, NT, 8], F32, pb)
            top_i = sb("top_i", [P, NT, 8], U32, pb)
            top_e = sb("top_e", [P, NT, TOP_K], F32, pb)
            odd = sb("odd", [P, NT, TOP_K], F32, pb)
            pos = sb("pos", [P, NT, TOP_K], F32, pb)
            over = sb("over", [P, NT, TOP_K], F32, pb)
            idx_f = sb("idx_f", [P, NT, TOP_K], F32, pb)

            scr = egu[:, :, :, :, :].rearrange("p a w c f -> p (a w c f)")
            scd = ed[:, :, :, :].rearrange("p a c h -> p (a c h)")
            logits = scr[:, 0:NT * R].rearrange("p (i r) -> p i r", r=R)
            probs = scr[:, 544:544 + NT * E].rearrange("p (i e) -> p i e", e=E)
            onehot = scr[:, 1056:1056 + NT * TOP_K * E].rearrange("p (i k e) -> p i k e", k=TOP_K, e=E)
            picked = scr[:, 3104:3104 + NT * TOP_K * E].rearrange("p (i k e) -> p i k e", k=TOP_K, e=E)
            logT = scd[0:R, 0:NG * GW]
            mask = scd[:, 2048:2048 + NT * E].rearrange("p (i e) -> p i e", e=E)
            before = scd[:, 2560:2560 + NT * E].rearrange("p (i e) -> p i e", e=E)
            yg = scr[:, 0:2 * TOP_K * H].rearrange("p (n k h) -> p n k h", n=2, k=TOP_K)

            acc = (xg, ye)

            (rb_ok, rconst, lt_full, lt_ok, lg_full, shift_ok, ex_ok, pos_full, mask_ok, route_ok,
             tab_zero, scat, tab_in, whi_ok, wlo_ok, xhi_ok, xlo_ok, g_full, silu_ok, u_full,
             prod_ok, phi_ok, plo_ok, d_full0, d_full1, d_used0, d_used1, x_acc,
             xg_in, et_full, et_taken, eg_full, esilu_ok, eprod_ok, ey_full, ye_ok, ye_sent, ye_free,
             gu_in, dn_in, yg_zero, y_in0, y_in1, y_used, y_first, y_sum, out_done, dve_b, pool_b) = sems(
                 "rb_ok rconst lt_full lt_ok lg_full shift_ok ex_ok pos_full mask_ok route_ok "
                 "tab_zero scat tab_in whi_ok wlo_ok xhi_ok xlo_ok g_full silu_ok u_full "
                 "prod_ok phi_ok plo_ok d_full0 d_full1 d_used0 d_used1 x_acc "
                 "xg_in et_full et_taken eg_full esilu_ok eprod_ok ey_full ye_ok ye_sent ye_free "
                 "gu_in dn_in yg_zero y_in0 y_in1 y_used y_first y_sum out_done dve_b pool_b")
            d_full, d_used, y_in = (d_full0, d_full1), (d_used0, d_used1), (y_in0, y_in1)
            gB, uB, dB = bank[0], bank[1], bank[2:4]
            egB, euB, etB, eyB = bank[4:8]

            UNITS = [(p, g) for p in range(len(PARTS)) for g in range(NG)]

            def chunk(p, g, f):
                return NG * sum(PARTS[:p]) + (g * PARTS[p] + f)

            def tile(p, g, m):
                return p * NG * GT + (g * GT + m)

            def splits(p, k):
                return sum(PARTS[:p]) + p + k

            def pair(p, g, h):
                return (p - PAIR_PARTS[0]) * 2 * NG + (2 * g + h)

            with nc.Block() as block:

                @block.sync
                def _(sp):
                    def load_part(p):
                        sp.wait_ge(wlo_ok, splits(p, 0))
                        load_shared(sp, p)

                    def load_gate_up(j):
                        for e in range(2):
                            for w, src in enumerate((Wg, Wu)):
                                sp.dma_start(egu[:, e, w, :, :], src[2 * j + e, :, :].rearrange("(p c) f -> p c f", c=C)).then_inc(gu_in, 16)

                    def load_down(j):
                        for e in range(2):
                            sp.dma_start(ed[:, e, 0:2, :], Wd[2 * j + e, 0:2 * P, :].rearrange("(c p) h -> p c h", p=P)).then_inc(dn_in, 16)
                            sp.dma_start(ed[0:F - 2 * P, e, 2, :], Wd[2 * j + e, 2 * P:F, :]).then_inc(dn_in, 16)

                    sp.wait_ge(rconst, 1)
                    sp.dma_start(tok_dram.rearrange("(p j) a -> p (j a)", p=P), zero_u[:, :]).then_inc(tab_zero, 16)
                    sp.wait_ge(route_ok, 1)
                    load_gate_up(0)
                    load_down(0)
                    load_part(1)
                    sp.wait_ge(scat, 16 * NT * TOP_K)
                    sp.dma_start(slot_tok[:, :], tok_dram.rearrange("(p j) a -> p (j a)", p=P)).then_inc(tab_in, 16)
                    sp.sem_inc(ye_free, 1)
                    for p in PAIR_PARTS:
                        load_part(p + 1)
                        for g in range(NG):
                            for h in range(2):
                                j = pair(p, g, h)
                                if j + 1 < NP:
                                    sp.wait_ge(eg_full, j + 1)
                                    load_gate_up(j + 1)
                                    sp.wait_ge(ey_full, j + 1)
                                    load_down(j + 1)
                                sp.wait_ge(ye_ok, j + 1)
                                sp.dma_start(ye_dram[j * P:(j + 1) * P, :], ye[:, :]).then_inc(ye_sent, 16)
                                sp.wait_ge(ye_sent, 16 * (j + 1))
                                sp.sem_inc(ye_free, 1)
                    for g in range(NG):
                        for m in range(GT):
                            i = g * GT + m
                            sp.wait_ge(y_used, i + 3)
                            sp.dma_start(out_rows[:, i, :], xres[:, i, :]).then_inc(out_done, 16)
                    sp.wait_ge(out_done, 16 * NT)

                @block.gpsimd
                def _(pool):
                    gp = nc.gpsimd
                    own = Tally(pool_b)

                    def link(ins):
                        ins.then_inc(pool_b, 1)
                        pool.wait_ge(pool_b, own.tick())

                    gp.memset(zero_u[:, :], 0).then_inc(rconst, 1)
                    link(gp.memset(ones[:, :], 1.0))
                    link(gp.iota(iota_i[:, :], [[1, E]], base=0, channel_multiplier=0))
                    link(gp.tensor_copy(iota_e[:, :], iota_i[:, :]))
                    link(gp.iota(tok_id[:, :], [[P, NT]], base=0, channel_multiplier=1))
                    gp.affine_select(out=tri[:, :], in_=ones[:, :], compare_op=ALU.is_gt, fill=0.0, base=0,
                                     pattern=[[1, P]], channel_multiplier=-1).then_inc(rb_ok, 1)
                    pool.wait_ge(route_ok, 1)
                    pool.wait_ge(tab_zero, 16)
                    for i in range(NT):
                        for k in range(TOP_K):
                            gp.indirect_dma_start(tok_dram[:, :], bass.IndirectOffsetOnAxis(t_idx[:, i, k:k + 1], axis=0),
                                                  tok_id[:, i:i + 1], None,
                                                  bounds_check=E * CAP - 1, oob_is_err=False).then_inc(scat, 16)
                    pool.wait_ge(tab_in, 16)
                    for j in range(NP):
                        if j:
                            pool.wait_ge(et_full, 2 * j - 1)
                        gp.indirect_dma_start(xg[:, :], None, h2_dram[:, :],
                                              bass.IndirectOffsetOnAxis(slot_tok[:, j:j + 1], axis=0)).then_inc(xg_in, 16)
                    pool.wait_ge(eg_full, NP)
                    link(gp.memset(scr[:, 0:2 * TOP_K * H], 0.0))
                    pool.wait_ge(ye_free, NP + 1)
                    def close(i):
                        pool.wait_ge(y_sum, i + 1)
                        link(gp.tensor_tensor(acc[i % 2][:, :], acc[i % 2][:, :], gate_b[:, i // BT, :], ALU.mult))
                        pool.wait_ge(x_acc, tile(len(PARTS) - 1, 0, i) + 3)
                        gp.tensor_tensor(xres[:, i, :], xres[:, i, :], acc[i % 2][:, :], ALU.add).then_inc(y_used, 1)

                    pool.sem_inc(y_used, 2)
                    for i in range(NT):
                        if i > 1:
                            pool.wait_ge(y_sum, i - 1)
                        for k in range(TOP_K):
                            gp.indirect_dma_start(yg[:, i % 2, k, :], None, ye_dram[:, :],
                                                  bass.IndirectOffsetOnAxis(y_idx[:, i, k:k + 1], axis=0),
                                                  bounds_check=E * CAP - 1, oob_is_err=False).then_inc(y_in[i % 2], 16)
                        if i > 1:
                            close(i - 2)
                    close(NT - 2)
                    close(NT - 1)

                @block.scalar
                def _(act):
                    a = nc.scalar
                    act.sem_inc(u_full, 1)
                    act.sem_inc(prod_ok, 1)
                    for g in range(NG):
                        act.wait_ge(lt_full, g + 1)
                        a.activation(logT[:, g * GW:(g + 1) * GW], bank[4 + g][0:R, :], ACT.Copy).then_inc(lt_ok, 1)
                    act.wait_ge(shift_ok, 1)
                    a.activation(probs, probs, ACT.Exp).then_inc(ex_ok, 1)
                    a.activation(sigma[:, :], logits[:, :, E], ACT.Exp, scale=-1.0).then_inc(ex_ok, 1)

                    def split_weights(p, f):
                        act.wait_ge(w_in, 48 * (p + 1))
                        if p and f < PARTS[p - 1]:
                            act.wait_ge(u_full, chunk(p - 1, NG - 1, f) + 2)
                        at = slice(f * P, (f + 1) * P)
                        a.activation(wguH[:, :, :, at], wguN[:, :, :, at], ACT.Copy).then_inc(whi_ok, 1)

                    def split_down(p):
                        n = PARTS[p]
                        if p:
                            for q in range(2):
                                act.wait_ge(d_full[q], p * NG * GT // 2)
                        a.activation(wdH[:, 0:n, :], wdN[:, 0:n, :], ACT.Copy).then_inc(whi_ok, 1)

                    def split_group(p, g):
                        act.wait_ge(u_full, chunk(p, g, 0) + 1)
                        for c in range(C):
                            a.activation(xsH[:, c, :], h2T[:, c, g * GW:(g + 1) * GW], ACT.Copy).then_inc(xhi_ok, 1)

                    def gate_up(p, g, f):
                        n = chunk(p, g, f)
                        act.wait_ge(g_full, n + 1)
                        act.wait_ge(prod_ok, n + 1)
                        a.activation(silu[:, :], gB[:, :], ACT.Silu).then_inc(silu_ok, 1)
                        act.wait_ge(prod_ok, n + 2)
                        a.activation(prodH[:, f, :], prod[:, :], ACT.Copy).then_inc(phi_ok, 1)

                    def pair_rows(j):
                        act.wait_ge(et_full, 2 * j + 1)
                        a.activation(xeT[:, :, :], etB[:, :].rearrange("p (c m) -> p c m", c=C), ACT.Copy).then_inc(et_taken, 1)

                    def pair_silu(j):
                        act.wait_ge(eg_full, j + 1)
                        if j:
                            act.wait_ge(eprod_ok, j)
                        a.activation(esilu[:, :], egB[:, 0:F], ACT.Silu).then_inc(esilu_ok, 1)

                    def pair_turned(j):
                        act.wait_ge(et_full, 2 * j + 2)
                        for c, (lo, n) in enumerate(FC):
                            ins = a.activation(epT[0:n, c, :], etB[0:n, c * P:(c + 1) * P], ACT.Copy)
                        ins.then_inc(et_taken, 1)

                    def pair_out(j):
                        act.wait_ge(ey_full, j + 1)
                        act.wait_ge(ye_free, j + 1)
                        a.activation(ye[:, :], eyB[:, :], ACT.Copy).then_inc(ye_ok, 1)

                    def combine_front(g, m):
                        i = g * GT + m
                        act.wait_ge(y_in[i % 2], 16 * TOP_K * (i // 2 + 1))
                        act.wait_ge(y_used, i + 1)
                        a.activation(acc[i % 2][:, :], yg[:, i % 2, 0, :], ACT.Copy, scale=slotw[:, i, 0:1]).then_inc(y_first, 1)

                    for f in range(PARTS[0]):
                        split_weights(0, f)
                    split_group(0, 0)
                    for p, g in UNITS:
                        n, last = PARTS[p], g == NG - 1
                        if g == 0:
                            split_down(p)
                        pairs = [pair(p, g, h) for h in range(2)] if p in PAIR_PARTS else None
                        gate_up(p, g, 0)
                        if pairs:
                            pair_rows(pairs[0])
                        gate_up(p, g, 1)
                        if last and p + 1 < len(PARTS):
                            split_weights(p + 1, 0)
                        if pairs:
                            pair_silu(pairs[0])
                        if n > 2:
                            gate_up(p, g, 2)
                        if (p, g) != UNITS[-1]:
                            if last:
                                for f in range(1, PARTS[p + 1]):
                                    split_weights(p + 1, f)
                            split_group(*((p, g + 1) if not last else (p + 1, 0)))
                        if pairs:
                            pair_turned(pairs[0])
                            pair_out(pairs[0])
                            pair_rows(pairs[1])
                            pair_silu(pairs[1])
                            pair_turned(pairs[1])
                            pair_out(pairs[1])
                        if p == len(PARTS) - 1:
                            for m in range(GT):
                                combine_front(g, m)

                @block.vector
                def _(dve):
                    v = nc.vector
                    own = Tally(dve_b)
                    dve.sem_inc(silu_ok, 1)
                    dve.sem_inc(plo_ok, 1)
                    dve.sem_inc(x_acc, 2)

                    def link(ins):
                        ins.then_inc(dve_b, 1)
                        dve.wait_ge(dve_b, own.tick())

                    def over_e(ap):
                        return ap.rearrange("p (i a) -> p i a", a=1).to_broadcast([P, NT, E])

                    def over_k(ap):
                        return ap.rearrange("p i (a e) -> p i a e", a=1).to_broadcast([P, NT, TOP_K, E])

                    for n in range(2):
                        dve.wait_ge(lg_full, n + 1)
                        link(v.tensor_copy(logits[:, n * BT:(n + 1) * BT, :].rearrange("p i r -> p (i r)"), bank[4 + n][:, 0:BT * R]))
                    link(v.tensor_reduce(rmax[:, :], logits[:, :, 0:E], AX.X, ALU.max))
                    v.tensor_tensor(probs, logits[:, :, 0:E], over_e(rmax[:, :]), ALU.subtract).then_inc(shift_ok, 1)
                    dve.wait_ge(ex_ok, 2)
                    link(v.tensor_reduce(rmax[:, :], probs, AX.X, ALU.add))
                    link(v.reciprocal(rmax[:, :], rmax[:, :]))
                    link(v.tensor_tensor(probs, probs, over_e(rmax[:, :]), ALU.mult))
                    link(v.tensor_scalar(sigma[:, :], sigma[:, :], 1.0, None, ALU.add))
                    link(v.reciprocal(sigma[:, :], sigma[:, :]))
                    for i in range(NT):
                        v.max(top8[:, i, :], probs[:, i, :]).then_inc(dve_b, 1)
                        own.tick()
                    dve.wait_ge(dve_b, own.last())
                    for i in range(NT):
                        v.max_index(top_i[:, i, :], top8[:, i, :], probs[:, i, :]).then_inc(dve_b, 1)
                        own.tick()
                    dve.wait_ge(dve_b, own.last())
                    link(v.tensor_copy(top_e[:, :, :], top_i[:, :, 0:TOP_K]))
                    dve.wait_ge(rb_ok, 1)
                    for k in range(TOP_K):
                        v.tensor_tensor(onehot[:, :, k, :], top_e[:, :, k:k + 1].to_broadcast([P, NT, E]),
                                        iota_e[:, :].rearrange("p (a e) -> p a e", a=1).to_broadcast([P, NT, E]), ALU.is_equal).then_inc(dve_b, 1)
                        own.tick()
                    dve.wait_ge(dve_b, own.last())
                    link(v.tensor_reduce(mask, onehot.rearrange("p i k e -> p i e k"), AX.X, ALU.add))
                    link(v.memset(before[:, 0, :], 0.0))
                    for i in range(1, NT):
                        ins = v.tensor_tensor(before[:, i, :], before[:, i - 1, :], mask[:, i - 1, :], ALU.add)
                        if i < NT - 1:
                            link(ins)
                        else:
                            ins.then_inc(mask_ok, 1)
                    dve.wait_ge(pos_full, 1)
                    for k in range(TOP_K):
                        v.tensor_tensor(picked[:, :, k, :], bank[6][:, :].rearrange("p (i e) -> p i e", e=E), onehot[:, :, k, :], ALU.mult).then_inc(dve_b, 1)
                        own.tick()
                    dve.wait_ge(dve_b, own.last())
                    link(v.tensor_reduce(pos[:, :, :], picked, AX.X, ALU.add))
                    link(v.tensor_scalar(over[:, :, :], pos[:, :, :], float(CAP), None, ALU.is_ge))
                    link(v.scalar_tensor_tensor(idx_f[:, :, :], top_e[:, :, :], float(CAP), pos[:, :, :], ALU.mult, ALU.add))
                    link(v.scalar_tensor_tensor(idx_f[:, :, :], over[:, :, :], float(FAR), idx_f[:, :, :], ALU.mult, ALU.add))
                    link(v.tensor_copy(y_idx[:, :, :], idx_f[:, :, :]))
                    link(v.tensor_scalar(t_idx[:, :, :], top_i[:, :, 0:TOP_K], 1, None, ALU.bitwise_and))
                    link(v.tensor_copy(odd[:, :, :], t_idx[:, :, :]))
                    link(v.tensor_tensor(top_e[:, :, :], top_e[:, :, :], odd[:, :, :], ALU.subtract))
                    link(v.scalar_tensor_tensor(pos[:, :, :], odd[:, :, :], float(CAP), pos[:, :, :], ALU.mult, ALU.add))
                    link(v.tensor_scalar(pos[:, :, :], pos[:, :, :], float(NP), None, ALU.mult))
                    link(v.scalar_tensor_tensor(pos[:, :, :], top_e[:, :, :], 0.5, pos[:, :, :], ALU.mult, ALU.add))
                    link(v.scalar_tensor_tensor(pos[:, :, :], over[:, :, :], float(FAR), pos[:, :, :], ALU.mult, ALU.add))
                    link(v.tensor_copy(t_idx[:, :, :], pos[:, :, :]))
                    link(v.tensor_reduce(rmax[:, :], top8[:, :, 0:TOP_K], AX.X, ALU.add))
                    link(v.reciprocal(rmax[:, :], rmax[:, :]))
                    link(v.tensor_tensor(slotw[:, :, :], top8[:, :, 0:TOP_K],
                                         rmax[:, :].rearrange("p (i a) -> p i a", a=1).to_broadcast([P, NT, TOP_K]), ALU.mult))
                    link(v.tensor_scalar(over[:, :, :], over[:, :, :], -1.0, 1.0, ALU.mult, ALU.add))
                    v.tensor_tensor(slotw[:, :, :], slotw[:, :, :], over[:, :, :], ALU.mult).then_inc(route_ok, 1)

                    def lo_weights(p, f):
                        n, at = PARTS[p], slice(f * P, (f + 1) * P)
                        dve.wait_ge(whi_ok, splits(p, f + 1))
                        if f < n:
                            v.tensor_tensor(wguL[:, :, :, at], wguN[:, :, :, at],
                                            wguH[:, :, :, at].bitcast(F32), ALU.subtract).then_inc(wlo_ok, 1)
                        else:
                            v.tensor_tensor(wdL[:, 0:n, :], wdN[:, 0:n, :], wdH[:, 0:n, :].bitcast(F32), ALU.subtract).then_inc(wlo_ok, 1)

                    def lo_group(p, g):
                        for c in range(C):
                            dve.wait_ge(xhi_ok, (p * NG + g) * C + c + 1)
                            v.tensor_tensor(xsL[:, c, :], h2T[:, c, g * GW:(g + 1) * GW], xsH[:, c, :].bitcast(F32), ALU.subtract).then_inc(xlo_ok, 1)

                    def gate_up(p, g, f):
                        n = chunk(p, g, f)
                        dve.wait_ge(silu_ok, n + 2)
                        dve.wait_ge(u_full, n + 2)
                        dve.wait_ge(plo_ok, n + 1)
                        v.tensor_tensor(prod[:, :], uB[:, :], silu[:, :], ALU.mult).then_inc(prod_ok, 1)
                        dve.wait_ge(phi_ok, n + 1)
                        v.tensor_tensor(prodL[:, f, :], prod[:, :], prodH[:, f, :].bitcast(F32), ALU.subtract).then_inc(plo_ok, 1)

                    def down(p, g, m):
                        n, i = tile(p, g, m), g * GT + m
                        dve.wait_ge(d_full[m % 2], n // 2 + 1)
                        dve.wait_ge(x_acc, n + 1)
                        v.scalar_tensor_tensor(ytmp[:, m % 2, :], dB[m % 2][:, :], sigma[:, i:i + 1], gate_b[:, i // BT, :],
                                               ALU.mult, ALU.mult).then_inc(d_used[m % 2], 1)
                        dve.wait_ge(d_used[m % 2], n // 2 + 2)
                        v.tensor_tensor(xres[:, i, :], xres[:, i, :], ytmp[:, m % 2, :], ALU.add).then_inc(x_acc, 1)

                    def pair_prod(j):
                        dve.wait_ge(esilu_ok, j + 1)
                        if j:
                            dve.wait_ge(et_full, 2 * j)
                        v.tensor_tensor(eprod[:, :], euB[:, 0:F], esilu[:, :], ALU.mult).then_inc(eprod_ok, 1)

                    def combine(g, m):
                        i = g * GT + m
                        dve.wait_ge(y_in[i % 2], 16 * TOP_K * (i // 2 + 1))
                        dve.wait_ge(y_first, i + 1)
                        for k in range(1, TOP_K):
                            ins = v.scalar_tensor_tensor(acc[i % 2][:, :], yg[:, i % 2, k, :], slotw[:, i, k:k + 1], acc[i % 2][:, :], ALU.mult, ALU.add)
                            if k < TOP_K - 1:
                                link(ins)
                            else:
                                ins.then_inc(y_sum, 1)

                    for f in range(PARTS[0]):
                        lo_weights(0, f)
                    lo_group(0, 0)
                    for p, g in UNITS:
                        n, last = PARTS[p], g == NG - 1
                        if g == 0:
                            lo_weights(p, n)
                        pairs = [pair(p, g, h) for h in range(2)] if p in PAIR_PARTS else None
                        gate_up(p, g, 0)
                        gate_up(p, g, 1)
                        if last and p + 1 < len(PARTS):
                            lo_weights(p + 1, 0)
                        if pairs:
                            pair_prod(pairs[0])
                        if n > 2:
                            gate_up(p, g, 2)
                        if (p, g) != UNITS[-1]:
                            if last:
                                for f in range(1, PARTS[p + 1]):
                                    lo_weights(p + 1, f)
                            lo_group(*((p, g + 1) if not last else (p + 1, 0)))
                        final = p == len(PARTS) - 1
                        down(p, g, 0)
                        if final:
                            combine(g, 0)
                        down(p, g, 1)
                        if final:
                            combine(g, 1)
                        if pairs:
                            pair_prod(pairs[1])
                        down(p, g, 2)
                        if final:
                            combine(g, 2)
                        down(p, g, 3)
                        if final:
                            combine(g, 3)

                @block.tensor
                def _(pe):
                    mm = nc.tensor
                    for s_ in (d_used0, d_used1):
                        pe.sem_inc(s_, 1)
                    for g in range(NG):
                        for c in range(C):
                            ins = mm.matmul(bank[4 + g][0:R, :], wrN[:, c, :], h2T[:, c, g * GW:(g + 1) * GW], start=(c == 0), stop=(c == C - 1))
                        ins.then_inc(lt_full, 1)
                    pe.wait_ge(lt_ok, NG)
                    for n in range(2):
                        for i in range(BT):
                            t = n * BT + i
                            ins = mm.transpose(bank[4 + n][:, i * R:(i + 1) * R], logT[:, t * P:(t + 1) * P], ident[0:R, 0:R])
                        ins.then_inc(lg_full, 1)
                    pe.wait_ge(mask_ok, 1)
                    mm.matmul(bank[6][:, :], tri[:, :], mask.rearrange("p i e -> p (i e)"), start=True, stop=False)
                    mm.matmul(bank[6][:, :], ones[:, :], before.rearrange("p i e -> p (i e)"), start=False, stop=True).then_inc(pos_full, 1)

                    def gate_up(p, g, f):
                        n = chunk(p, g, f)
                        for w, (bk, free, full) in enumerate(((gB, silu_ok, g_full), (uB, prod_ok, u_full))):
                            pe.wait_ge(free, n + 1)
                            k = 0
                            for c in range(C):
                                if g == 0 and w == 0 and c == 0:
                                    pe.wait_ge(wlo_ok, splits(p, f + 1))
                                if f == 0 and w == 0:
                                    pe.wait_ge(xlo_ok, (p * NG + g) * C + c + 1)
                                at = slice(f * P, (f + 1) * P)
                                for l, r in ((wguH, xsH), (wguL, xsH), (wguH, xsL)):
                                    ins = mm.matmul(bk[:, :], l[:, w, c, at], r[:, c, :], start=(k == 0), stop=(k == 3 * C - 1))
                                    k += 1
                            ins.then_inc(full, 1)

                    def down(p, g, m):
                        n, nf = tile(p, g, m), PARTS[p]
                        pe.wait_ge(d_used[m % 2], n // 2 + 1)
                        if m == 0:
                            pe.wait_ge(plo_ok, chunk(p, g, nf) + 1)
                        k = 0
                        for f in range(nf):
                            for l, r in ((prodH, wdH), (prodH, wdL), (prodL, wdH)):
                                ins = mm.matmul(dB[m % 2][:, :], l[:, f, m * P:(m + 1) * P], r[:, f, :], start=(k == 0), stop=(k == 3 * nf - 1))
                                k += 1
                        ins.then_inc(d_full[m % 2], 1)

                    def pair_rows(j):
                        pe.wait_ge(xg_in, 16 * (j + 1))
                        if j:
                            pe.wait_ge(et_taken, 2 * j)
                        rows_v = xg[:, :].rearrange("s (p c) -> s c p", c=C)
                        for c in range(C):
                            ins = mm.transpose(etB[:, c * P:(c + 1) * P], rows_v[:, c, :], ident[:, :])
                        ins.then_inc(et_full, 1)

                    def pair_gate_up(j):
                        pe.wait_ge(gu_in, 64 * (j + 1))
                        pe.wait_ge(et_taken, 2 * j + 1)
                        if j:
                            pe.wait_ge(eprod_ok, j)
                        for c in range(C):
                            for w, bk in enumerate((egB, euB)):
                                for e in range(2):
                                    half = slice(e * CAP, (e + 1) * CAP)
                                    ins = mm.matmul(bk[half, 0:F], xeT[:, c, half], egu[:, e, w, c, :], start=(c == 0), stop=(c == C - 1))
                        ins.then_inc(eg_full, 1)

                    def pair_turned(j):
                        pe.wait_ge(eprod_ok, j + 1)
                        for c, (lo, n) in enumerate(FC):
                            ins = mm.transpose(etB[0:n, c * P:(c + 1) * P], eprod[:, lo:lo + n], ident[:, :])
                        ins.then_inc(et_full, 1)

                    def pair_down(j):
                        pe.wait_ge(dn_in, 64 * (j + 1))
                        pe.wait_ge(et_taken, 2 * j + 2)
                        if j:
                            pe.wait_ge(ye_ok, j)
                        for c, (lo, n) in enumerate(FC):
                            for e in range(2):
                                half = slice(e * CAP, (e + 1) * CAP)
                                ins = mm.matmul(eyB[half, :], epT[0:n, c, half], ed[0:n, e, c, :], start=(c == 0), stop=(c == len(FC) - 1))
                        ins.then_inc(ey_full, 1)

                    for p, n in enumerate(PARTS):
                        for g in range(NG):
                            pairs = [pair(p, g, h) for h in range(2)] if p in PAIR_PARTS else None
                            gate_up(p, g, 0)
                            if pairs:
                                pair_rows(pairs[0])
                            gate_up(p, g, 1)
                            if pairs:
                                pair_gate_up(pairs[0])
                            if n > 2:
                                gate_up(p, g, 2)
                            if pairs:
                                pair_turned(pairs[0])
                            if g == 0:
                                pe.wait_ge(wlo_ok, splits(p, n + 1))
                            down(p, g, 0)
                            if pairs:
                                pair_down(pairs[0])
                                pair_rows(pairs[1])
                            down(p, g, 1)
                            if pairs:
                                pair_gate_up(pairs[1])
                            down(p, g, 2)
                            if pairs:
                                pair_turned(pairs[1])
                                pair_down(pairs[1])
                            down(p, g, 3)


_INS = ['L0_attn_x', 'L0_attn_Wk', 'L0_attn_Wv', 'L0_attn_Wo', 'L0_attn_Wts', 'L0_attn_gate', 'L0_attn_time_decay',
        'L0_attn_time_first', 'L0_attn_ln_w', 'L0_attn_ln_b', 'L0_ffn_Wr', 'L0_ffn_Wg', 'L0_ffn_Wu', 'L0_ffn_Wd',
        'L0_ffn_Wsg', 'L0_ffn_Wsu', 'L0_ffn_Wsd', 'L0_ffn_Wse', 'L0_c', 'L0_wmod']
_OUTS = [((2, 1024, 512), 'float32')]


def kernel(**inputs):
    import numpy as _np
    import concourse.bacc as _bacc
    from concourse import mybir as _mybir
    from concourse.bass_utils import run_bass_kernel_spmd as _run

    nc = _bacc.Bacc("TRN2", target_bir_lowering=False, num_devices=1)
    arrays, args = {}, []
    for name in _INS:
        a = _np.ascontiguousarray(inputs[name])
        arrays[f"in_{name}_dram"] = a
        args.append(nc.dram_tensor(f"in_{name}_dram", a.shape, _mybir.dt.from_np(a.dtype), kind="ExternalInput").ap())
    for i, (shape, dtype) in enumerate(_OUTS):
        dt = _mybir.dt.from_np(_np.dtype(dtype))
        args.append(nc.dram_tensor(f"out_{i}_dram", shape, dt, kind="ExternalOutput").ap())
    build(nc, *args)
    r = _run(nc, [arrays], core_ids=[0])
    got = tuple(r.results[0][f"out_{i}_dram"] for i in range(len(_OUTS)))
    return got[0]
```

```python
from contextlib import ExitStack

import concourse.bass as bass
from concourse import mybir

F32 = mybir.dt.float32
F32R = mybir.dt.float32r
U32 = mybir.dt.uint32
ALU = mybir.AluOpType
ACT = mybir.ActivationFunctionType
AX = mybir.AxisListType

P = 128
LN_EPS = 1e-5
GATE_FLOOR = 0.25
TOP_K = 4
CAP = 64
FAR = 1 << 16


class Tally:

    def __init__(self):
        self.at = 0

    def tick(self):
        self.at += 1
        return self.at

    def last(self):
        return self.at


def build(nc, x, Wk, Wv, Wo, Wts, gate, time_decay, time_first, ln_w, ln_b,
          Wr, Wg, Wu, Wd, Wsg, Wsu, Wsd, Wse, c_in, wmod, out):
    B, T, H = x.shape
    S = Wk.shape[0]
    E, _, F = Wg.shape
    FS = Wsg.shape[1]
    C = H // P
    NT = B * T // P
    BT = T // P
    HB = BT // 2
    GT = 4
    GW = GT * P
    NG = NT // GT
    BG = BT // GT
    NP = E // 2
    FC = [(0, P), (P, P), (2 * P, F - 2 * P)]
    PC = 3
    PARTS = [FS // P - 3 * PC, PC, PC, PC]
    UNITS = [(p, g) for p in range(len(PARTS)) for g in range(NG)]
    PAIR_UNIT = NG + 1
    R = E + 2
    assert (H, S, C, CAP * 2, BT, NP, FS % P) == (512, 64, 4, P, 8, 16, 0)

    h2_dram = nc.dram_tensor("h2_rows", (B * T, H), F32, kind="Internal").ap()
    ye_dram = nc.dram_tensor("expert_rows", (E * CAP, H), F32, kind="Internal").ap()
    tok_dram = nc.dram_tensor("slot_tokens", (E * CAP, 1), U32, kind="Internal").ap()

    x_rows = x.rearrange("b (i p) h -> p (b i) h", p=P)
    out_rows = out.rearrange("b (i p) h -> p (b i) h", p=P)
    wmod_v = wmod.rearrange("(k p) n -> p k n", p=P)

    with ExitStack() as ctx:
        def sb(name, shape, dt=F32, scope=ctx):
            return scope.enter_context(nc.sbuf_tensor(name, shape, dt))

        def sems(names):
            return [ctx.enter_context(nc.semaphore(n)) for n in names.split()]

        xres = sb("xres", [P, NT, H])
        h2T = sb("h2T", [P, C, B * T])
        gate_b = sb("gate_b", [P, B, H])
        ident = sb("ident", [P, P])
        wrN = sb("wrN", [P, C, R])

        with ExitStack() as first_use:
            hT = sb("hT", [P, 2, C, T], F32R, first_use)
        wguN = sb("wguN", [P, 2, C, PC * P])
        wdN = sb("wdN", [P, PC, H])
        prodH = sb("prodH", [P, PC, GW], F32R)
        prodL = sb("prodL", [P, PC, GW], F32R)
        silu = sb("silu", [P, GW])
        assert 2 * C * T == 2 * C * PC * P + PC * H + 2 * PC * GW + GW
        with ExitStack() as first_use:
            xhat = sb("xhat", [P, BT, H], F32, first_use)
        with ExitStack() as first_use:
            logT = sb("logT", [R, B * T], F32, first_use)
        egu = sb("egu", [P, 2, 2, C, F])
        w_in = sems("w_in")[0]
        wsg_v = Wsg.rearrange("(c p) f -> p c f", p=P)
        wsu_v = Wsu.rearrange("(c p) f -> p c f", p=P)

        def load_shared(sp, p):
            lo, n = P * sum(PARTS[:p]), PARTS[p]
            sp.dma_start(wguN[:, 0, :, 0:n * P], wsg_v[:, :, lo:lo + n * P]).then_inc(w_in, 16)
            sp.dma_start(wguN[:, 1, :, 0:n * P], wsu_v[:, :, lo:lo + n * P]).then_inc(w_in, 16)
            sp.dma_start(wdN[:, 0:n, :], Wsd[lo:lo + n * P, :].rearrange("(f p) h -> p f h", p=P)).then_inc(w_in, 16)

        bank = [ctx.enter_context(nc.psum_tensor(f"bank{i}", [P, 512], F32)) for i in range(8)]

        with ExitStack() as pa:
            Q = P // C
            hTH, hTL = hT[:, 0, :, :], hT[:, 1, :, :]
            bc = sb("bc", [P, 4, B, H], F32, pa)
            wtsH = sb("wtsH", [P, C, H], F32R, pa)
            wtsL = sb("wtsL", [P, C, H], F32R, pa)
            xnTH = sb("xnTH", [P, C, GW], F32R, pa)
            xnTL = sb("xnTL", [P, C, GW], F32R, pa)
            mix = sb("mix", [P, 2, H], F32, pa)
            h2r = sb("h2r", [P, 2, H], F32, pa)
            xs = sb("xs", [P, 2, H], F32, pa)
            xn = sb("xn", [P, 2, H], F32, pa)
            kE = sb("kE", [S, GW], F32, pa)
            vV = sb("vV", [S, GW], F32, pa)
            states_all = sb("states", [P, T], F32, pa)
            states = states_all[0:S, :]
            partial = states_all[:, :].rearrange("p (n h) -> p n h", n=2)
            woT = sb("woT", [S, B, H], F32, pa)
            kvH = sb("kvH", [P, C, P], F32R, pa)
            kvL = sb("kvL", [P, C, P], F32R, pa)
            rows = sb("rows", [24, P], F32, pa)
            cols = sb("cols", [P, 24], F32, pa)
            cT = sb("cT", [P, C, Q], F32, pa)
            saT = sb("saT", [P, C, Q], F32, pa)
            pick = sb("pick", [P, B], F32, pa)
            gcol = sb("gcol", [P, 2, C], F32, pa)
            ecol = sb("ecol", [P, 12], F32, pa)
            wcol = sb("wcol", [S, 4], F32, pa)
            kvbias = sb("kvbias", [S, 2], F32, pa)
            modc = sb("modc", [P, 6, C, B], F32, pa)
            dcol = sb("dcol", [P, B, 8, C], F32, pa)
            tmpc = sb("tmpc", [P, 3, C, B], F32, pa)
            st6 = sb("st6", [P, 6], F32, pa)
            mv1 = sb("mv1", [P, BT, 2], F32, pa)
            mv2 = sb("mv2", [P, 2, 2], F32, pa)
            ve = sb("ve", [P, BT], F32, pa)
            ve2 = sb("ve2", [P, 2], F32, pa)
            neg_half = sb("neg_half", [P, BT], F32, pa)
            rs = sb("rs", [P, BT], F32, pa)
            rs2 = sb("rs2", [P, 2], F32, pa)
            stage = [h2T[:, :, k * H:(k + 1) * H] for k in range(3)]
            wtsT = h2T[:, :, 3 * H:4 * H]
            woN = h2r[:, 0, 0:C * S].rearrange("p (c s) -> p c s", c=C)
            woS = h2r[:, 1, 0:C * B * S].rearrange("p (c b s) -> p c b s", c=C, b=B)
            kvN = xn[:, 0, :]
            kvT = xs[:, 1, :].rearrange("p (c m) -> p c m", c=C)

            (rows_zero, const_ok, cols_in, kv_in, wo_in, wr_in, stage_in0, stage_in1, stage_in2,
             col_full, col_ok, exp_ok, silu_c_ok, wts_scaled, kvH_ok, kvL_ok, bias_full, kvb_ok,
             sa_ok, spread_ok, mod_ok, wo_scaled, wts_hi, wts_lo, part_full, part_ok, part_used, pick_ok,
             xhat_ok, hi_ok, h2_scaled, wr_zero, lt_full, lt_ok, s_full0, s_full1, s_taken0, s_taken1, mix_ok, normed, h2_ok,
             h2_sent0, h2_sent1, h2_free, kv_full, kv_read, e_tanh, e_fac, st_ok, ve_ok, rs_ok, dve_self, pool_self) = sems(
                 "rows_zero const_ok cols_in kv_in wo_in wr_in stage_in0 stage_in1 stage_in2 "
                 "col_full col_ok exp_ok silu_c_ok wts_scaled kvH_ok kvL_ok bias_full kvb_ok "
                 "sa_ok spread_ok mod_ok wo_scaled wts_hi wts_lo part_full part_ok part_used pick_ok "
                 "xhat_ok hi_ok h2_scaled wr_zero lt_full lt_ok s_full0 s_full1 s_taken0 s_taken1 mix_ok normed h2_ok "
                 "h2_sent0 h2_sent1 h2_free kv_full kv_read e_tanh e_fac st_ok ve_ok rs_ok dve_self pool_self")
            x_in = [sems(f"x_in{b}{h}")[0] for b in range(B) for h in range(2)]
            stage_in = (stage_in0, stage_in1, stage_in2)
            h2_sent = (h2_sent0, h2_sent1)
            NTB = 3
            t_full = [sems(f"t_full{k}")[0] for k in range(NTB)]
            t_taken = [sems(f"t_taken{k}")[0] for k in range(NTB)]
            s_full, s_taken = (s_full0, s_full1), (s_taken0, s_taken1)

            tb, sbk, kvb, modb, biasb = [bank[0], bank[1], bank[6]], bank[2:4], bank[4], bank[5], bank[7]
            ltb = (modb, biasb)
            partb = (kvb, biasb)
            GATE, LNW, LNB, CC, TD, TF = 0, 4, 8, 12, 20, 21
            M_CA, M_SA, M_SB, M_CB, M_GA, M_GB = range(6)
            BLOCK = [1, 0, 3, 4, 2, 5]
            STAGE = [1, 2, 1, 2, 0, 1]
            VECTORS = [M_CA, M_SA, "wsa", M_SB, M_CB, M_GA, M_GB]
            MOD_AT, WSA_AT, KVB_AT = 32, 96, 112
            K_1CA, K_A, K_B, K_1CB, K_SB, K_GB, K_GA = range(7)
            PLACE = {K_A: 0, K_B: 1, K_1CB: 2, K_SB: 3}
            FIRST = [(i + HB) % BT for i in range(BT)]

            TURNS = [("wts", q) for q in range(C)] + [("kv",)] + [("h", 0, i) for i in FIRST[0:HB]]
            LAG, LAG2 = 2, 2

            def mixer_turns(b, i):
                t = []
                if b and i < LAG2:
                    t.append(("h2", b - 1, BT - LAG2 + i))
                if b == 0 and i == 0:
                    t += [("spread", 0, K_A), ("spread", 0, K_B)]
                if b == 0 and i < HB:
                    t.append(("h", 0, FIRST[HB + i]))
                if i >= LAG:
                    t.append(("xn", b, i - LAG))
                if b == B - 1 and i < B:
                    t.append(("spread", i, K_GB))
                if b == 0 and i == BT - 2:
                    t += [("wo", 0), ("wo", 1)]
                if b == 0 and i == BT - 1:
                    t += [("spread", 0, K_1CB), ("spread", 0, K_SB), ("spread", 1, K_A), ("spread", 1, K_B)]
                return t

            def last_turns(b):
                before = [("xn", b, i) for i in range(BT - LAG, BT)]
                after = []
                if b + 1 < B:
                    after += [("h", b + 1, i) for i in FIRST[0:HB]]
                    after += [("spread", 1, k) for k in (K_1CB, K_SB)]
                return before, after

            def out_turns(b, i):
                t = []
                if b + 1 < B and 0 < i <= HB:
                    t.append(("h", b + 1, FIRST[HB + i - 1]))
                if i >= LAG2:
                    t.append(("h2", b, i - LAG2))
                return t

            for b in range(B):
                for i in range(BT):
                    TURNS += mixer_turns(b, i)
                TURNS += last_turns(b)[0] + last_turns(b)[1]
                for i in range(BT):
                    TURNS += out_turns(b, i)
            TURNS += [("h2", B - 1, i) for i in range(BT - LAG2, BT)]
            SPLITS = [t for t in TURNS if t[0] in ("h", "xn")]
            NORMS = [(k, b, i) for b in range(B) for k in ("xn", "h2") for i in range(BT)]
            RSTDS = [("h", 0, 1), ("h", 0, 0)]
            for b in range(B):
                RSTDS += [("xn", b, i) for i in range(BT)]
                if b + 1 < B:
                    RSTDS += [("h", b + 1, 1), ("h", b + 1, 0)]
                RSTDS += [("h2", b, i) for i in range(BT)]

            def used(eng, j):
                eng.wait_ge(part_used, VECTORS.index(j) + 1)

            def turn_full(eng, t):
                q = TURNS.index(t)
                eng.wait_ge(t_full[q % NTB], q // NTB + 1)

            def turn_taken(eng, t):
                q = TURNS.index(t)
                eng.wait_ge(t_taken[q % NTB], q // NTB + 1)

            def s_use(n, b):
                return b * BT + (n // 2 + 1)

            def mixers_done(eng, b):
                for i in (BT - 2, BT - 1):
                    eng.wait_ge(s_full[i % 2], s_use(i, b))

            with nc.Block() as block:

                @block.sync
                def _(sp):
                    sp.wait_ge(rows_zero, 1)
                    for src, r in ((gate, GATE), (ln_w, LNW), (ln_b, LNB)):
                        sp.dma_start(rows[r:r + C, :], src.rearrange("(c p) -> c p", p=P)).then_inc(cols_in, 16)
                    sp.dma_start(rows[CC:CC + B * C, :], c_in.rearrange("b (c p) -> (b c) p", p=P)).then_inc(cols_in, 16)
                    for src, r in ((time_decay, TD), (time_first, TF)):
                        sp.dma_start(rows[r:r + 1, 0:S], src.rearrange("(a s) -> a s", a=1)).then_inc(cols_in, 16)

                    def load_mod(j):
                        sp.dma_start(stage[STAGE[j]], wmod_v[:, :, BLOCK[j] * 512:(BLOCK[j] + 1) * 512]).then_inc(stage_in[STAGE[j]], 16)

                    def load_x(b, h):
                        lo = b * BT + h * HB
                        sp.dma_start(xres[:, lo:lo + HB, :], x_rows[:, lo:lo + HB, :]).then_inc(x_in[b * 2 + h], 16)

                    load_mod(0)
                    load_mod(1)
                    sp.dma_start(stage[0], Wts.rearrange("(c p) d -> p c d", p=P)).then_inc(stage_in0, 16)
                    sp.dma_start(kvN[0:S, :], Wk).then_inc(kv_in, 16)
                    sp.dma_start(kvN[S:2 * S, :], Wv).then_inc(kv_in, 16)
                    load_x(0, 1)
                    load_x(0, 0)
                    sp.dma_start(woN, Wo.rearrange("(c p) s -> p c s", p=P)).then_inc(wo_in, 16)
                    for j in (2, 3):
                        sp.wait_ge(part_full, VECTORS.index(j - 2) + 1)
                        load_mod(j)
                    turn_full(sp, ("wts", C - 1))
                    load_mod(4)
                    load_x(1, 1)
                    load_x(1, 0)
                    sp.wait_ge(part_full, VECTORS.index(M_SB) + 1)
                    load_mod(5)
                    sp.dma_start(wrN[:, :, 0:E], Wr.rearrange("(c p) e -> p c e", p=P)).then_inc(wr_in, 16)
                    with nc.allow_non_contiguous_dma(reason="one column"):
                        sp.dma_start(wrN[:, :, E:E + 1], Wse.rearrange("(c p) e -> p c e", p=P)).then_inc(wr_in, 16)
                    sp.wait_ge(wr_in, 32)
                    for b in range(B):
                        if b == B - 1:
                            mixers_done(sp, b)
                            load_shared(sp, 0)
                        for i in range(BT):
                            n = b * BT + i
                            sp.wait_ge(h2_ok, n + 1)
                            sp.dma_start(h2_dram[n * P:(n + 1) * P, :], h2r[:, i % 2, :]).then_inc(h2_sent[i % 2], 16)
                            if n:
                                sp.wait_ge(h2_sent[(n - 1) % 2], 16 * ((n - 1) // 2 + 1))
                                sp.sem_inc(h2_free, 1)
                    sp.wait_ge(h2_sent[(B * BT - 1) % 2], 16 * (B * BT // 2))

                @block.gpsimd
                def _(pool):
                    g = nc.gpsimd
                    own = Tally()
                    g.memset(rows[:, :], 0.0).then_inc(rows_zero, 1)
                    g.memset(ident[:, :], 0.0).then_inc(pool_self, 1)
                    g.memset(neg_half[:, :], -0.5).then_inc(pool_self, 1)
                    own.tick()
                    pool.wait_ge(pool_self, own.tick())
                    g.affine_select(out=ident[:, :], in_=ident[:, :], compare_op=ALU.not_equal, fill=1.0,
                                    base=0, pattern=[[-1, P]], channel_multiplier=1).then_inc(const_ok, 1)

                    def rstd(kind, b, i):
                        pool.wait_ge(ve_ok, RSTDS.index((kind, b, i)) + 1)
                        if kind == "h":
                            at = slice(i * HB, (i + 1) * HB)
                            g.tensor_tensor(rs[:, at], ve[:, at], neg_half[:, at], ALU.pow).then_inc(rs_ok, 1)
                        else:
                            at = slice(i % 2, i % 2 + 1)
                            n = NORMS.index((kind, b, i))
                            if n > 1 and NORMS[n - 2][0] == "h2":
                                pool.wait_ge(h2_scaled, NORMS[n - 2][1] * BT + NORMS[n - 2][2] + 1)
                            g.tensor_tensor(rs2[:, at], ve2[:, at], neg_half[:, 0:1], ALU.pow).then_inc(rs_ok, 1)

                    def mix_rows(b, i):
                        if i > 1:
                            pool.wait_ge(s_taken[i % 2], s_use(i - 2, b) + 1)
                        if i == 0:
                            turn_taken(pool, ("spread", b, K_A))
                        pool.wait_ge(xhat_ok, b * BT + FIRST.index(i) + 1)
                        g.tensor_tensor(mix[:, i % 2, :], xhat[:, i, :], bc[:, PLACE[K_A], b, :], ALU.mult).then_inc(pool_self, 1)
                        if i == 0:
                            turn_taken(pool, ("spread", b, K_B))
                        pool.wait_ge(pool_self, own.tick())
                        g.tensor_tensor(mix[:, i % 2, :], mix[:, i % 2, :], bc[:, PLACE[K_B], b, :], ALU.add).then_inc(mix_ok, 1)

                    def h2_rows(b, i):
                        n = b * BT + i
                        pool.wait_ge(h2_scaled, n + 1)
                        if n > 1:
                            pool.wait_ge(h2_free, n - 1)
                            turn_full(pool, ("h2", (n - 2) // BT, (n - 2) % BT))
                        if i == 0:
                            turn_taken(pool, ("spread", b, K_SB))
                        if n == 0:
                            turn_full(pool, ("wo", 1))
                        g.tensor_tensor(h2r[:, i % 2, :], xn[:, i % 2, :], bc[:, PLACE[K_SB], b, :], ALU.add).then_inc(h2_ok, 1)

                    def scale_weights(b):
                        assert b == B - 1
                        mixers_done(pool, b - 1)
                        for c in range(C):
                            pool.wait_ge(wts_hi, b * C + c + 1)
                            g.tensor_scalar(wtsT[:, c, :], wtsT[:, c, :], dcol[:, b, K_1CA, c:c + 1], None, ALU.mult).then_inc(pool_self, 1)
                            pool.wait_ge(pool_self, own.tick())
                            g.tensor_tensor(wtsL[:, c, :], wtsT[:, c, :], wtsH[:, c, :].bitcast(F32), ALU.subtract).then_inc(wts_lo, 1)

                    rstd("h", 0, 1)
                    rstd("h", 0, 0)
                    for b in range(B):
                        mix_rows(b, 0)
                        if b:
                            h2_rows(b - 1, BT - 1)
                        for i in range(BT):
                            if i + 1 < BT:
                                mix_rows(b, i + 1)
                            rstd("xn", b, i)
                        if b + 1 < B:
                            rstd("h", b + 1, 1)
                            rstd("h", b + 1, 0)
                            scale_weights(b + 1)
                        for i in range(BT):
                            rstd("h2", b, i)
                            if i:
                                h2_rows(b, i - 1)
                        if b == B - 1:
                            h2_rows(b, BT - 1)

                @block.scalar
                def _(act):
                    a = nc.scalar

                    def take(t):
                        q, kind = TURNS.index(t), t[0]
                        src = tb[q % NTB]
                        wide = src[:, :].rearrange("p (c m) -> p c m", c=C)
                        turn_full(act, t)
                        if kind == "wts":
                            a.activation(wtsT[:, t[1], :], src[:, :], ACT.Copy).then_inc(t_taken[q % NTB], 1)
                        elif kind == "kv":
                            a.activation(kvT, wide, ACT.Copy).then_inc(t_taken[q % NTB], 1)
                        elif kind == "wo":
                            a.activation(woT[:, t[1], :], src[0:S, :], ACT.Copy).then_inc(t_taken[q % NTB], 1)
                        elif kind == "spread":
                            dst = gate_b[:, t[1], :] if t[2] == K_GB else bc[:, PLACE[t[2]], t[1], :]
                            a.activation(dst, src[:, :], ACT.Copy).then_inc(t_taken[q % NTB], 1)
                        elif kind == "h":
                            _, b, i = t
                            if b and i == FIRST[0]:
                                mixers_done(act, b - 1)
                            a.activation(hTH[:, :, i * P:(i + 1) * P], wide, ACT.Copy).then_inc(hi_ok, 1)
                        elif kind == "xn":
                            _, b, i = t
                            k = b * BG + i // GT
                            if k and i % GT == 0:
                                act.wait_ge(kv_full, k)
                            at = (i % GT) * P
                            a.activation(xnTH[:, :, at:at + P], wide, ACT.Copy).then_inc(hi_ok, 1)
                        else:
                            n = t[1] * BT + t[2]
                            a.activation(h2T[:, :, n * P:(n + 1) * P], wide, ACT.Copy).then_inc(t_taken[q % NTB], 1)

                    def part_out(n):
                        act.wait_ge(part_full, n + 1)
                        if n > 1:
                            act.wait_ge(part_used, n - 1)
                        a.activation(partial[:, n % 2, :], partb[n % 2][:, :], ACT.Copy).then_inc(part_ok, 1)

                    def scale_weights(b):
                        if b:
                            mixers_done(act, b - 1)
                        act.wait_ge(sa_ok, 1)
                        for c in range(C):
                            a.activation(wtsH[:, c, :], wtsT[:, c, :], ACT.Copy, scale=dcol[:, b, K_1CA, c:c + 1]).then_inc(wts_hi, 1)

                    def decay_factor(b, n):
                        k = b * BG + n
                        act.wait_ge(kv_full, k + 1)
                        act.wait_ge(st_ok, k + 1)
                        a.activation(kE[:, :], kvb[0:S, :], ACT.Tanh, scale=0.5, bias=kvbias[:, 0:1]).then_inc(e_tanh, 1)
                        a.activation(vV[:, :], kvb[S:2 * S, :], ACT.Copy).then_inc(kv_read, 1)
                        act.wait_ge(e_tanh, k + 1)
                        a.activation(kE[:, :], kE[:, :], ACT.Exp, scale=wcol[:, 2:3], bias=wcol[:, 2:3]).then_inc(e_fac, 1)

                    def scale_row(b, i):
                        t = ("h2", b, i)
                        act.wait_ge(normed, NORMS.index(t) + 1)
                        act.wait_ge(rs_ok, RSTDS.index(t) + 1)
                        a.activation(xn[:, i % 2, :], xn[:, i % 2, :], ACT.Copy, scale=rs2[:, i % 2:i % 2 + 1]).then_inc(h2_scaled, 1)

                    def logits_out(g):
                        act.wait_ge(lt_full, g + 1)
                        a.activation(logT[:, g * GW:(g + 1) * GW], ltb[g % 2][0:R, :], ACT.Copy).then_inc(lt_ok, 1)

                    act.sem_inc(st_ok, 1)
                    act.wait_ge(col_ok, 1)
                    a.activation(ecol[:, 0:C], cols[:, GATE:GATE + C], ACT.Exp, scale=-1.0).then_inc(exp_ok, 1)
                    a.activation(ecol[:, C:C + B * C], cols[:, CC:CC + B * C], ACT.Exp, scale=-1.0).then_inc(exp_ok, 1)
                    a.activation(wcol[:, 0:2], cols[0:S, TD:TD + 2], ACT.Exp).then_inc(exp_ok, 1)
                    part_out(0)
                    part_out(1)
                    for q in range(C):
                        take(("wts", q))
                    take(("kv",))
                    part_out(2)
                    for q in range(C):
                        turn_taken(act, ("wts", q))
                    scale_weights(0)
                    for i in FIRST[0:HB]:
                        take(("h", 0, i))
                    turn_taken(act, ("kv",))
                    for c in range(C):
                        a.activation(kvH[:, c, :], kvT[:, c, :], ACT.Copy, scale=cols[:, LNW + c:LNW + c + 1]).then_inc(kvH_ok, 1)
                    act.wait_ge(kvb_ok, 1)

                    for b in range(B):
                        for i in range(BT):
                            if b == 0 and 0 < i < 5:
                                part_out(i + 2)
                            for t in mixer_turns(b, i):
                                take(t)
                            if i == BT - 2:
                                decay_factor(b, 0)
                        before, after = last_turns(b)
                        for t in before:
                            take(t)
                        if b + 1 < B:
                            scale_weights(b + 1)
                        decay_factor(b, 1)
                        for t in after:
                            take(t)
                        if not after:
                            logits_out(0)
                        for i in range(BT):
                            scale_row(b, i)
                            if b == B - 1 and i == 1:
                                logits_out(1)
                            for t in out_turns(b, i):
                                take(t)
                            if b == B - 1 and i == BT - 1:
                                logits_out(2)
                    for i in range(BT - LAG2, BT):
                        take(("h2", B - 1, i))
                    logits_out(3)

                @block.vector
                def _(dve):
                    v = nc.vector
                    own = Tally()

                    def link(ins):
                        ins.then_inc(dve_self, 1)
                        dve.wait_ge(dve_self, own.tick())

                    def xrow(b, i):
                        return xres[:, b * BT + i, :]

                    def first_stats(b, i):
                        dve.wait_ge(x_in[b * 2 + i // HB], 16)
                        link(v.bn_stats(st6[:, :], xrow(b, i)))
                        link(v.bn_aggr(mv1[:, i, :], st6[:, :]))

                    def first_var(b, h):
                        at = slice(h * HB, (h + 1) * HB)
                        v.tensor_scalar(ve[:, at], mv1[:, at, 1], LN_EPS, None, ALU.add).then_inc(ve_ok, 1)

                    def first_rows(b, i):
                        dve.wait_ge(rs_ok, RSTDS.index(("h", b, i // HB)) + 1)
                        if b:
                            dve.wait_ge(mix_ok, b * BT)
                        v.tensor_scalar(xhat[:, i, :], xrow(b, i), mv1[:, i, 0:1], rs[:, i:i + 1], ALU.subtract, ALU.mult).then_inc(xhat_ok, 1)

                    def lo(t):
                        (kind, b, i), q = t, TURNS.index(t)
                        dve.wait_ge(hi_ok, SPLITS.index(t) + 1)
                        dh, dl = (hTH, hTL) if kind == "h" else (xnTH, xnTL)
                        at = slice(i * P, (i + 1) * P) if kind == "h" else slice((i % GT) * P, (i % GT + 1) * P)
                        v.tensor_tensor(dl[:, :, at], tb[q % NTB][:, :].rearrange("p (c m) -> p c m", c=C),
                                        dh[:, :, at].bitcast(F32), ALU.subtract).then_inc(t_taken[q % NTB], 1)

                    def scale_weights():
                        for c in range(C):
                            dve.wait_ge(wts_hi, c + 1)
                            v.scalar_tensor_tensor(wtsL[:, c, :], wtsT[:, c, :], dcol[:, 0, K_1CA, c:c + 1],
                                                   wtsH[:, c, :].bitcast(F32), ALU.mult, ALU.subtract).then_inc(wts_lo, 1)

                    dk = lambda kind: dcol[:, :, kind, :].rearrange("p b c -> p c b")
                    g1 = gcol[:, 1, :].rearrange("p (c a) -> p c a", a=1).to_broadcast([P, C, B])
                    modp = lambda j, n: modb[:, MOD_AT + j * C * B:MOD_AT + (j + n) * C * B]

                    v.memset(wrN[:, :, E + 1:R], 0.0).then_inc(wr_zero, 1)
                    link(v.memset(cT[:, :, :], 0.0))
                    link(v.memset(saT[:, :, :], 0.0))
                    dve.wait_ge(const_ok, 1)
                    v.tensor_reduce(pick[:, :], ident[:, :].rearrange("p (k m) -> p m k", k=C)[:, 0:B, :], AX.X, ALU.add).then_inc(pick_ok, 1)
                    dve.wait_ge(col_full, 1)
                    v.tensor_copy(cols[:, :], modb[:, 0:24]).then_inc(col_ok, 1)
                    dve.wait_ge(col_ok, 1)
                    dve.wait_ge(exp_ok, 3)
                    link(v.tensor_scalar(ecol[:, :], ecol[:, :], 1.0, None, ALU.add))
                    link(v.reciprocal(ecol[:, :], ecol[:, :]))
                    link(v.tensor_copy(gcol[:, 0, :], ecol[:, 0:C]))
                    link(v.tensor_scalar(gcol[:, 1, :], ecol[:, 0:C], -1.0, 1.0, ALU.mult, ALU.add))
                    link(v.tensor_scalar(wcol[:, 2:3], wcol[:, 1:2], -0.5, None, ALU.mult))
                    v.tensor_tensor(cT[:, :, 0:B], cols[:, CC:CC + B * C].rearrange("p (b c) -> p c b", b=B),
                                    ecol[:, C:C + B * C].rearrange("p (b c) -> p c b", b=B), ALU.mult).then_inc(silu_c_ok, 1)
                    dve.wait_ge(stage_in0, 16)
                    for c in range(C):
                        v.tensor_scalar(stage[0][:, c, :], stage[0][:, c, :], gcol[:, 0, c:c + 1], None, ALU.mult).then_inc(wts_scaled, 1)
                    for i in FIRST[0:HB]:
                        first_stats(0, i)
                    first_var(0, 1)
                    used(dve, M_SA)
                    link(v.tensor_copy(modc[:, 0:2, :, :].rearrange("p j c b -> p (j c b)"), modp(0, 2)))
                    link(v.tensor_copy(saT[:, :, 0:B], modc[:, M_SA, :, :]))
                    v.tensor_scalar(dk(K_1CA), modc[:, M_CA, :, :], 1.0, None, ALU.add).then_inc(sa_ok, 1)
                    dve.wait_ge(sa_ok, 1)
                    link(v.tensor_tensor(dk(K_A), dk(K_1CA), g1, ALU.mult))
                    link(v.tensor_tensor(tmpc[:, 0, :, :], modc[:, M_SA, :, :], g1, ALU.mult))
                    for i in FIRST[0:HB]:
                        first_rows(0, i)
                    scale_weights()
                    for i in FIRST[0:HB]:
                        lo(("h", 0, i))
                    dve.wait_ge(bias_full, 1)
                    used(dve, "wsa")
                    v.tensor_tensor(dk(K_B), modb[:, WSA_AT:WSA_AT + C * B].rearrange("p (c b) -> p c b", c=C),
                                    tmpc[:, 0, :, :], ALU.add).then_inc(spread_ok, 1)
                    link(v.tensor_scalar(kvbias[:, 0:1], modb[0:S, KVB_AT:KVB_AT + 1], 0.5, None, ALU.mult))
                    v.tensor_copy(kvbias[:, 1:2], modb[0:S, KVB_AT + 1:KVB_AT + 2]).then_inc(kvb_ok, 1)
                    for i in FIRST[HB:BT]:
                        first_stats(0, i)
                    first_var(0, 0)
                    for c in range(C):
                        dve.wait_ge(kvH_ok, c + 1)
                        v.scalar_tensor_tensor(kvL[:, c, :], kvT[:, c, :], cols[:, LNW + c:LNW + c + 1],
                                               kvH[:, c, :].bitcast(F32), ALU.mult, ALU.subtract).then_inc(kvL_ok, 1)
                    for i in FIRST[HB:BT]:
                        first_rows(0, i)

                    def floored(src, kind):
                        link(v.tensor_scalar(tmpc[:, 0, :, :], modc[:, src, :, :], 0.0, 2.0, ALU.is_ge, ALU.mult))
                        link(v.tensor_scalar(tmpc[:, 1, :, :], tmpc[:, 0, :, :], -1.0, None, ALU.add))
                        link(v.tensor_scalar(tmpc[:, 2, :, :], modc[:, src, :, :], -1.0, GATE_FLOOR, ALU.mult, ALU.max))
                        link(v.tensor_tensor(tmpc[:, 2, :, :], tmpc[:, 2, :, :], modc[:, src, :, :], ALU.max))
                        return v.tensor_tensor(dk(kind), tmpc[:, 1, :, :], tmpc[:, 2, :, :], ALU.mult)

                    def derive_gb():
                        used(dve, M_GB)
                        link(v.tensor_copy(modc[:, 5, :, :].rearrange("p c b -> p (c b)"), modp(5, 1)))
                        floored(M_GB, K_GB).then_inc(mod_ok, 1)

                    def derive():
                        used(dve, M_GA)
                        link(v.tensor_copy(modc[:, 2:5, :, :].rearrange("p j c b -> p (j c b)"), modp(2, 3)))
                        link(v.tensor_scalar(dk(K_1CB), modc[:, M_CB, :, :], 1.0, None, ALU.add))
                        link(v.tensor_copy(dk(K_SB), modc[:, M_SB, :, :]))
                        floored(M_GA, K_GA).then_inc(mod_ok, 1)
                        dve.wait_ge(mod_ok, 1)
                        dve.wait_ge(wo_in, 16)
                        for b in range(B):
                            for c in range(C):
                                v.tensor_scalar(woS[:, c, b, :], woN[:, c, :], dcol[:, b, K_GA, c:c + 1], None, ALU.mult).then_inc(wo_scaled, 1)

                    def stats(t, src):
                        link(v.bn_stats(st6[:, :], src))
                        n = NORMS.index(t)
                        if n > 1:
                            dve.wait_ge(normed, n - 1)
                            dve.wait_ge(rs_ok, RSTDS.index(NORMS[n - 2]) + 1)
                        link(v.bn_aggr(mv2[:, n % 2, :], st6[:, :]))
                        v.tensor_scalar(ve2[:, n % 2:n % 2 + 1], mv2[:, n % 2, 1:2], LN_EPS, None, ALU.add).then_inc(ve_ok, 1)

                    def xn_free(n):
                        if n > 1:
                            before = NORMS[n - 2]
                            if before[0] == "xn":
                                turn_full(dve, before)
                            else:
                                dve.wait_ge(h2_ok, before[1] * BT + before[2] + 1)
                        else:
                            turn_full(dve, ("kv",))

                    def apply(t, src):
                        n = NORMS.index(t)
                        xn_free(n)
                        dve.wait_ge(rs_ok, RSTDS.index(t) + 1)
                        v.tensor_scalar(xn[:, n % 2, :], src, mv2[:, n % 2, 0:1], rs2[:, n % 2:n % 2 + 1],
                                        ALU.subtract, ALU.mult).then_inc(normed, 1)

                    def mix_front(b, i):
                        n = NORMS.index(("xn", b, i))
                        dve.wait_ge(s_full[i % 2], s_use(i, b))
                        dve.wait_ge(mix_ok, b * BT + (i + 1))
                        if n > 1:
                            dve.wait_ge(normed, n - 1)
                        v.tensor_tensor(xs[:, i % 2, :], sbk[i % 2][:, :], mix[:, i % 2, :], ALU.add).then_inc(s_taken[i % 2], 1)
                        dve.wait_ge(s_taken[i % 2], s_use(i, b) + 1)
                        stats(("xn", b, i), xs[:, i % 2, :])

                    def kv_scan(b, n):
                        k = b * BG + n
                        dve.wait_ge(e_fac, k + 1)
                        dve.wait_ge(kv_read, k + 2)
                        link(v.scalar_tensor_tensor(kE[:, :], vV[:, :], kvbias[:, 1:2], kE[:, :], ALU.add, ALU.mult))
                        dve.wait_ge(st_ok, k + 1)
                        v.tensor_tensor_scan(states[:, n * GW:(n + 1) * GW], wcol[:, 0:1].to_broadcast([S, GW]), kE[:, :],
                                             states[:, n * GW - 1:n * GW] if n else 0.0, ALU.mult, ALU.add).then_inc(st_ok, 1)

                    def residual(b, i):
                        dve.wait_ge(s_full[i % 2], s_use(BT + i, b))
                        v.tensor_tensor(xrow(b, i), sbk[i % 2][:, :], xrow(b, i), ALU.add).then_inc(s_taken[i % 2], 1)
                        dve.wait_ge(s_taken[i % 2], s_use(BT + i, b) + 1)
                        stats(("h2", b, i), xrow(b, i))
                        n = NORMS.index(("h2", b, i))
                        if i == 0:
                            turn_taken(dve, ("spread", b, K_1CB))
                        xn_free(n)
                        dve.wait_ge(ve_ok, RSTDS.index(("h2", b, i)) + 1)
                        v.scalar_tensor_tensor(xn[:, n % 2, :], xrow(b, i), mv2[:, n % 2, 0:1], bc[:, PLACE[K_1CB], b, :],
                                               ALU.subtract, ALU.mult).then_inc(normed, 1)

                    for b in range(B):
                        for i in range(BT):
                            mix_front(b, i)
                            if i:
                                apply(("xn", b, i - 1), xs[:, (i - 1) % 2, :])
                            if b == 0 and i < HB:
                                lo(("h", 0, FIRST[HB + i]))
                            if i >= LAG:
                                lo(("xn", b, i - LAG))
                            if b == 0 and i == BT - 3:
                                derive()
                            if b + 1 < B and i:
                                first_stats(b + 1, FIRST[i - 1])
                        apply(("xn", b, BT - 1), xs[:, (BT - 1) % 2, :])
                        lo(("xn", b, BT - 2))
                        kv_scan(b, 0)
                        lo(("xn", b, BT - 1))
                        if b + 1 < B:
                            first_stats(b + 1, FIRST[BT - 1])
                            first_var(b + 1, 1)
                            first_var(b + 1, 0)
                            for i in FIRST[0:HB]:
                                first_rows(b + 1, i)
                            for i in FIRST[0:2]:
                                lo(("h", b + 1, i))
                        kv_scan(b, 1)
                        if b + 1 < B:
                            for i in FIRST[2:HB]:
                                lo(("h", b + 1, i))
                        for i in range(BT):
                            residual(b, i)
                            if b + 1 < B and i < HB:
                                first_rows(b + 1, FIRST[HB + i])
                            if b + 1 < B and 0 < i <= HB:
                                lo(("h", b + 1, FIRST[HB + i - 1]))
                            if b == 0 and i == BT - 1:
                                derive_gb()

                @block.tensor
                def _(pe):
                    m = nc.tensor
                    for s_ in (s_taken0, s_taken1, kv_read):
                        pe.sem_inc(s_, 1)
                    pe.wait_ge(const_ok, 1)
                    pe.wait_ge(cols_in, 96)
                    m.transpose(modb[:, 0:24], rows[:, :], ident[0:24, 0:24]).then_inc(col_full, 1)

                    def turn(t):
                        q, kind = TURNS.index(t), t[0]
                        if q >= NTB:
                            pe.wait_ge(t_taken[q % NTB], q // NTB)
                        dst = tb[q % NTB]
                        if kind == "spread":
                            if t[2] in (K_A, K_B):
                                pe.wait_ge(spread_ok, 1)
                            else:
                                pe.wait_ge(mod_ok, 2 if t[2] == K_GB else 1)
                            for c in range(C):
                                ins = m.matmul(dst[:, c * P:(c + 1) * P], dcol[:, t[1], t[2], c:c + 1].to_broadcast([P, P]),
                                               ident[:, :], start=True, stop=True)
                            ins.then_inc(t_full[q % NTB], 1)
                            return
                        if kind == "wts":
                            pe.wait_ge(wts_scaled, C)
                            src = [stage[0][:, c, t[1] * P:(t[1] + 1) * P] for c in range(C)]
                        elif kind == "wo":
                            pe.wait_ge(wo_scaled, (t[1] + 1) * C)
                            src, dst = [woS[:, c, t[1], :] for c in range(C)], dst[0:S, :]
                        else:
                            if kind == "kv":
                                pe.wait_ge(kv_in, 32)
                                r = kvN
                            elif kind == "h":
                                pe.wait_ge(xhat_ok, t[1] * BT + FIRST.index(t[2]) + 1)
                                r = xhat[:, t[2], :]
                            elif kind == "xn":
                                pe.wait_ge(normed, NORMS.index(t) + 1)
                                r = xn[:, t[2] % 2, :]
                            else:
                                pe.wait_ge(h2_ok, t[1] * BT + t[2] + 1)
                                r = h2r[:, t[2] % 2, :]
                            src = [r[:, c * P:(c + 1) * P] for c in range(C)]
                        for c in range(C):
                            ins = m.transpose(dst[:, c * P:(c + 1) * P], src[c], ident[:, :])
                        ins.then_inc(t_full[q % NTB], 1)

                    def vector_product(n):
                        j = VECTORS[n]
                        if n == 0:
                            pe.wait_ge(silu_c_ok, 1)
                        if n > 1:
                            pe.wait_ge(part_ok, n - 1)
                        if j == "wsa":
                            pe.wait_ge(sa_ok, 1)
                            for q in range(C):
                                turn_taken(pe, ("wts", q))
                            vec, mat = saT, wtsT
                        else:
                            uses = [k for k in range(j + 1) if STAGE[k] == STAGE[j]]
                            pe.wait_ge(stage_in[STAGE[j]], 16 * (len(uses) + (STAGE[j] == 0)))
                            vec, mat = cT, stage[STAGE[j]]
                        for k in range(C):
                            ins = m.matmul(partb[n % 2][k * Q:(k + 1) * Q, :], vec[:, k, :], mat[:, k, :], start=True, stop=True)
                        ins.then_inc(part_full, 1)

                    def vector_columns(n):
                        j = VECTORS[n]
                        pe.wait_ge(part_ok, n + 1)
                        if n == 0:
                            pe.wait_ge(pick_ok, 1)
                            pe.wait_ge(col_ok, 1)
                        if n == 3:
                            pe.wait_ge(kvb_ok, 1)
                        for cc in range(C):
                            at = (WSA_AT if j == "wsa" else MOD_AT + j * C * B) + cc * B
                            ins = m.matmul(modb[:, at:at + B], partial[:, n % 2, cc * P:(cc + 1) * P], pick[:, :], start=True, stop=True)
                        ins.then_inc(part_used, 1)

                    def mixer(b, i):
                        s = FIRST[i]
                        pe.wait_ge(s_taken[i % 2], s_use(i, b))
                        turn_taken(pe, ("h", b, s))
                        if i == 0:
                            pe.wait_ge(wts_lo, (b + 1) * C)
                        k = 0
                        for c in range(C):
                            for l, r in ((hTH, wtsH), (hTH, wtsL), (hTL, wtsH)):
                                ins = m.matmul(sbk[i % 2][:, :], l[:, c, s * P:(s + 1) * P], r[:, c, :],
                                               start=(k == 0), stop=(k == 3 * C - 1))
                                k += 1
                        ins.then_inc(s_full[i % 2], 1)

                    def keys_values(b, n):
                        for i in range(n * GT, (n + 1) * GT):
                            turn_taken(pe, ("xn", b, i))
                        pe.wait_ge(kv_read, b * BG + (n + 1))
                        if b == 0 and n == 0:
                            pe.wait_ge(kvL_ok, C)
                            pe.wait_ge(part_ok, len(VECTORS))
                        k = 0
                        for c in range(C):
                            for l, r in ((kvH, xnTH), (kvH, xnTL), (kvL, xnTH)):
                                ins = m.matmul(kvb[:, :], l[:, c, :], r[:, c, :], start=(k == 0), stop=(k == 3 * C - 1))
                                k += 1
                        ins.then_inc(kv_full, 1)

                    def router(g):
                        for i in range(g * GT, (g + 1) * GT):
                            turn_taken(pe, ("h2", i // BT, i % BT))
                        if g == 0:
                            pe.wait_ge(mod_ok, 2)
                            pe.wait_ge(wr_in, 32)
                            pe.wait_ge(wr_zero, 1)
                            pe.wait_ge(mix_ok, B * BT)
                        if g > 1:
                            pe.wait_ge(lt_ok, g - 1)
                        for c in range(C):
                            ins = m.matmul(ltb[g % 2][0:R, :], wrN[:, c, :], h2T[:, c, g * GW:(g + 1) * GW], start=(c == 0), stop=(c == C - 1))
                        ins.then_inc(lt_full, 1)

                    def project(b, i):
                        pe.wait_ge(s_taken[i % 2], s_use(BT + i, b))
                        pe.wait_ge(st_ok, b * BG + (i // GT + 2))
                        if i == 0:
                            turn_taken(pe, ("wo", b))
                        m.matmul(sbk[i % 2][:, :], states[:, i * P:(i + 1) * P], woT[:, b, :],
                                 start=True, stop=True).then_inc(s_full[i % 2], 1)

                    vector_product(0)
                    vector_product(1)
                    vector_columns(0)
                    vector_columns(1)
                    for q in range(C):
                        turn(("wts", q))
                    turn(("kv",))
                    vector_product(2)
                    turn_taken(pe, ("kv",))
                    for w in range(2):
                        for c in range(C):
                            ins = m.matmul(modb[0:S, KVB_AT + w:KVB_AT + w + 1], kvT[:, c, w * S:(w + 1) * S], cols[:, LNB + c:LNB + c + 1],
                                           start=(c == 0), stop=(c == C - 1))
                    ins.then_inc(bias_full, 1)
                    vector_columns(2)
                    for i in FIRST[0:HB]:
                        turn(("h", 0, i))

                    for b in range(B):
                        for i in range(BT):
                            mixer(b, i)
                            if i == GT + LAG:
                                keys_values(b, 0)
                            if b == 0 and 0 < i < 5:
                                vector_product(i + 2)
                            for t in mixer_turns(b, i):
                                turn(t)
                            if b == 0 and 0 < i < 5:
                                vector_columns(i + 2)
                        before, after = last_turns(b)
                        for t in before:
                            turn(t)
                        keys_values(b, 1)
                        for t in after[0:HB]:
                            turn(t)
                        for t in after[HB:]:
                            turn(t)
                        if b == B - 1:
                            router(0)
                        for i in range(BT):
                            project(b, i)
                            if b == B - 1 and i == 1:
                                router(1)
                            for t in out_turns(b, i):
                                turn(t)
                        if b == B - 1:
                            router(2)
                    for i in range(BT - LAG2, BT):
                        turn(("h2", B - 1, i))
                    router(3)

        with ExitStack() as pb:
            xsH = sb("xsH", [P, C, GW], F32R, pb)
            xsL = sb("xsL", [P, C, GW], F32R, pb)
            wguH = sb("wguH", [P, 2, C, PC * P], F32R, pb)
            wguL = sb("wguL", [P, 2, C, PC * P], F32R, pb)
            wdH = sb("wdH", [P, PC, H], F32R, pb)
            wdL = sb("wdL", [P, PC, H], F32R, pb)
            prod = sb("prod", [P, GW], F32, pb)
            ytmp = sb("ytmp", [P, 2, H], F32, pb)
            ed = sb("ed", [P, 2, len(FC), H], F32, pb)
            xg = sb("xg", [P, H], F32, pb)
            xeT = sb("xeT", [P, C, P], F32, pb)
            esilu = sb("esilu", [P, F], F32, pb)
            eprod = sb("eprod", [P, F], F32, pb)
            epT = sb("epT", [P, len(FC), P], F32, pb)
            ye = sb("ye", [P, H], F32, pb)
            tri = sb("tri", [P, P], F32, pb)
            ones = sb("ones", [P, P], F32, pb)
            iota_e = sb("iota_e", [P, E], F32, pb)
            iota_i = sb("iota_i", [P, E], U32, pb)
            tok_id = sb("tok_id", [P, NT], U32, pb)
            zero_u = sb("zero_u", [P, NP], U32, pb)
            slotw = sb("slotw", [P, NT, TOP_K], F32, pb)
            sigma = sb("sigma", [P, NT], F32, pb)
            y_idx = sb("y_idx", [P, NT, TOP_K], U32, pb)
            t_idx = sb("t_idx", [P, NT, TOP_K], U32, pb)
            slot_tok = sb("slot_tok", [P, NP], U32, pb)
            rmax = sb("rmax", [P, NT], F32, pb)
            top8 = sb("top8", [P, NT, 8], F32, pb)
            top_i = sb("top_i", [P, NT, 8], U32, pb)
            top_e = sb("top_e", [P, NT, TOP_K], F32, pb)
            odd = sb("odd", [P, NT, TOP_K], F32, pb)
            pos = sb("pos", [P, NT, TOP_K], F32, pb)
            over = sb("over", [P, NT, TOP_K], F32, pb)
            idx_f = sb("idx_f", [P, NT, TOP_K], F32, pb)

            scr = egu[:, :, :, :, :].rearrange("p a w c f -> p (a w c f)")
            scd = ed[:, :, :, :].rearrange("p a c h -> p (a c h)")
            at = B * T
            logits = scr[:, at:at + NT * R].rearrange("p (i r) -> p i r", r=R)
            at += NT * R
            probs = scr[:, at:at + NT * E].rearrange("p (i e) -> p i e", e=E)
            at += NT * E
            onehot = scr[:, at:at + NT * TOP_K * E].rearrange("p (i k e) -> p i k e", k=TOP_K, e=E)
            picked = scd[:, 0:NT * TOP_K * E].rearrange("p (i k e) -> p i k e", k=TOP_K, e=E)
            mask = scd[:, 2048:2048 + NT * E].rearrange("p (e i) -> p e i", e=E)
            upto = scd[:, 2560:2560 + NT * E].rearrange("p (e i) -> p e i", e=E)
            keep = scd[:, 0:NT * E].rearrange("p (e i) -> p e i", e=E)
            YW = TOP_K * H
            yg = [w.rearrange("p (k h) -> p k h", k=TOP_K) for w in (scr[:, 0:YW], scr[:, YW:2 * YW], scd[:, 0:YW])]
            NY = len(yg)
            acc = (xg, ye, ytmp[:, 0, :], ytmp[:, 1, :])
            NACC = len(acc)
            MERGE = NG * (len(PARTS) - 1)


            (rb_ok, rconst, lg_full, shift_ok, ex_ok, pos_full, mask_ok, route_ok,
             tab_zero, scat, tab_in, whi_ok, wlo_ok, xhi_ok, xlo_ok, pool_lo, g_full, silu_ok, u_full,
             prod_ok, phi_ok, plo_ok, d_full0, d_full1, d_used0, d_used1, x_acc,
             xg_in, et_full, et_taken, eg_full, esilu_ok, eprod_ok, ey_full, ye_ok, ye_sent, ye_free,
             gu_in, dn_in, y_in0, y_in1, y_in2, y_used, y_first, y_read, y_sum, final_ok, out_done, dve_b, pool_b) = sems(
                 "rb_ok rconst lg_full shift_ok ex_ok pos_full mask_ok route_ok "
                 "tab_zero scat tab_in whi_ok wlo_ok xhi_ok xlo_ok pool_lo g_full silu_ok u_full "
                 "prod_ok phi_ok plo_ok d_full0 d_full1 d_used0 d_used1 x_acc "
                 "xg_in et_full et_taken eg_full esilu_ok eprod_ok ey_full ye_ok ye_sent ye_free "
                 "gu_in dn_in y_in0 y_in1 y_in2 y_used y_first y_read y_sum final_ok out_done dve_b pool_b")
            d_full, d_used, y_in = (d_full0, d_full1), (d_used0, d_used1), (y_in0, y_in1, y_in2)
            gB, uB, dB = bank[0], bank[1], bank[2:4]
            egB, euB, etB, eyB = bank[4:8]

            def chunk(p, g, f):
                return NG * sum(PARTS[:p]) + (g * PARTS[p] + f)

            def tile(p, g, m):
                return p * NG * GT + (g * GT + m)

            def splits(p, k):
                return sum(PARTS[:p]) + p + k

            def joins(u, place):
                if u < MERGE:
                    return []
                return ([[], [0], [1], [2], [3]] if u == MERGE else [[0], [1, 2], [], [3], []])[place]

            def weights_ahead(u):
                p, g = UNITS[u]
                return list(range(PARTS[p] - 2, PARTS[p + 1])) if g == NG - 1 and p + 1 < len(PARTS) else []

            def steps(p):
                return PARTS[p] + GT

            def stage_after(u, k):
                if u < PAIR_UNIT:
                    return None
                n = sum(steps(UNITS[w][0]) for w in range(PAIR_UNIT, u)) + k - 1
                j, stage = n // 3, n % 3
                return (j, stage) if j < NP else None

            assert stage_after(NG * (len(PARTS) - 1) - 1, steps(0) - 1) is not None
            assert stage_after(NG * (len(PARTS) - 1), 1) is None

            with nc.Block() as block:

                @block.sync
                def _(sp):
                    def load_part(p):
                        sp.wait_ge(wlo_ok, splits(p, 0) - 1)
                        sp.wait_ge(pool_lo, 1)
                        load_shared(sp, p)

                    def load_gate_up(j):
                        for e in range(2):
                            for w, src in enumerate((Wg, Wu)):
                                sp.dma_start(egu[:, e, w, :, :], src[2 * j + e, :, :].rearrange("(p c) f -> p c f", c=C)).then_inc(gu_in, 16)

                    def load_down(j):
                        for e in range(2):
                            sp.dma_start(ed[:, e, 0:2, :], Wd[2 * j + e, 0:2 * P, :].rearrange("(c p) h -> p c h", p=P)).then_inc(dn_in, 16)
                            sp.dma_start(ed[0:F - 2 * P, e, 2, :], Wd[2 * j + e, 2 * P:F, :]).then_inc(dn_in, 16)

                    sp.wait_ge(rconst, 1)
                    sp.dma_start(tok_dram.rearrange("(p j) a -> p (j a)", p=P), zero_u[:, :]).then_inc(tab_zero, 16)
                    load_part(1)
                    sp.wait_ge(route_ok, 1)
                    load_gate_up(0)
                    load_down(0)
                    sp.wait_ge(scat, 16 * NT * TOP_K)
                    sp.dma_start(slot_tok[:, :], tok_dram.rearrange("(p j) a -> p (j a)", p=P)).then_inc(tab_in, 16)
                    sp.sem_inc(ye_free, 1)
                    for j in range(NP):
                        if j == 0:
                            load_part(2)
                        if j == NP // 2 + 1:
                            load_part(3)
                        if j + 1 < NP:
                            sp.wait_ge(eg_full, j + 1)
                            load_gate_up(j + 1)
                            sp.wait_ge(ey_full, j + 1)
                            load_down(j + 1)
                        sp.wait_ge(ye_ok, j + 1)
                        sp.dma_start(ye_dram[j * P:(j + 1) * P, :], ye[:, :]).then_inc(ye_sent, 16)
                        sp.wait_ge(ye_sent, 16 * (j + 1))
                        sp.sem_inc(ye_free, 1)
                    for g in range(NG):
                        for m in range(GT):
                            i = g * GT + m
                            if g < NG - 1:
                                sp.wait_ge(y_used, i + 1 + NACC)
                            else:
                                sp.wait_ge(final_ok, m + 1)
                            sp.dma_start(out_rows[:, i, :], xres[:, i, :]).then_inc(out_done, 16)
                    sp.wait_ge(out_done, 16 * NT)

                @block.gpsimd
                def _(pool):
                    gp = nc.gpsimd
                    own = Tally()

                    def link(ins):
                        ins.then_inc(pool_b, 1)
                        pool.wait_ge(pool_b, own.tick())

                    gp.memset(zero_u[:, :], 0).then_inc(rconst, 1)
                    link(gp.memset(ones[:, :], 1.0))
                    link(gp.iota(iota_i[:, :], [[1, E]], base=0, channel_multiplier=0))
                    link(gp.tensor_copy(iota_e[:, :], iota_i[:, :]))
                    link(gp.iota(tok_id[:, :], [[P, NT]], base=0, channel_multiplier=1))
                    link(gp.memset(keep, 1.0))
                    link(gp.memset(keep[:, :, 0:1], 0.0))
                    link(gp.memset(tri[:, :], 0.0))
                    gp.affine_select(out=tri[:, :], in_=tri[:, :], compare_op=ALU.is_gt, fill=-1.0, base=0,
                                     pattern=[[1, P]], channel_multiplier=-1).then_inc(rb_ok, 1)
                    n = PARTS[0]
                    pool.wait_ge(whi_ok, splits(0, n + 1))
                    gp.tensor_tensor(wdL[:, 0:n, :], wdN[:, 0:n, :], wdH[:, 0:n, :].bitcast(F32), ALU.subtract).then_inc(pool_lo, 1)
                    for c in range(C):
                        pool.wait_ge(xhi_ok, C + c + 1)
                        gp.tensor_tensor(xsL[:, c, :], h2T[:, c, GW:2 * GW], xsH[:, c, :].bitcast(F32), ALU.subtract).then_inc(pool_lo, 1)
                    pool.wait_ge(route_ok, 1)
                    pool.wait_ge(tab_zero, 16)
                    for i in range(NT):
                        for k in range(TOP_K):
                            gp.indirect_dma_start(tok_dram[:, :], bass.IndirectOffsetOnAxis(t_idx[:, i, k:k + 1], axis=0),
                                                  tok_id[:, i:i + 1], None,
                                                  bounds_check=E * CAP - 1, oob_is_err=False).then_inc(scat, 16)
                    pool.wait_ge(tab_in, 16)
                    for j in range(NP):
                        if j:
                            pool.wait_ge(et_full, 2 * j - 1)
                        gp.indirect_dma_start(xg[:, :], None, h2_dram[:, :],
                                              bass.IndirectOffsetOnAxis(slot_tok[:, j:j + 1], axis=0)).then_inc(xg_in, 16)
                    pool.wait_ge(eg_full, NP)
                    link(gp.memset(scr[:, 0:2 * YW], 0.0))
                    pool.wait_ge(ye_free, NP + 1)
                    def close(i):
                        pool.wait_ge(y_sum, i + 1)
                        gp.tensor_tensor(xres[:, i, :], xres[:, i, :], acc[i % NACC][:, :], ALU.add).then_inc(y_used, 1)

                    pool.sem_inc(y_used, NACC)
                    for i in range(NT):
                        if i == 2:
                            link(gp.memset(scd[:, 0:YW], 0.0))
                        if i >= NY:
                            pool.wait_ge(y_read, i - NY + 1)
                        for k in range(TOP_K):
                            gp.indirect_dma_start(yg[i % NY][:, k, :], None, ye_dram[:, :],
                                                  bass.IndirectOffsetOnAxis(y_idx[:, i, k:k + 1], axis=0),
                                                  bounds_check=E * CAP - 1, oob_is_err=False).then_inc(y_in[i % NY], 16)
                        if i >= NACC:
                            close(i - NACC)

                @block.scalar
                def _(act):
                    a = nc.scalar
                    act.sem_inc(u_full, 1)
                    act.sem_inc(prod_ok, 1)
                    def split_weights(p, f):
                        act.wait_ge(w_in, 48 * (p + 1))
                        if p and f < PARTS[p - 1]:
                            act.wait_ge(u_full, chunk(p - 1, NG - 1, f) + 2)
                        at = slice(f * P, (f + 1) * P)
                        a.activation(wguH[:, :, :, at], wguN[:, :, :, at], ACT.Copy).then_inc(whi_ok, 1)

                    def split_down(p):
                        n = PARTS[p]
                        if p:
                            for q in range(2):
                                act.wait_ge(d_full[q], p * NG * GT // 2)
                        a.activation(wdH[:, 0:n, :], wdN[:, 0:n, :], ACT.Copy).then_inc(whi_ok, 1)

                    def split_group(p, g):
                        act.wait_ge(u_full, chunk(p, g, 0) + 1)
                        for c in range(C):
                            a.activation(xsH[:, c, :], h2T[:, c, g * GW:(g + 1) * GW], ACT.Copy).then_inc(xhi_ok, 1)

                    def gate_up(p, g, f):
                        n = chunk(p, g, f)
                        act.wait_ge(g_full, n + 1)
                        act.wait_ge(prod_ok, n + 1)
                        a.activation(silu[:, :], gB[:, :], ACT.Silu).then_inc(silu_ok, 1)
                        act.wait_ge(prod_ok, n + 2)
                        a.activation(prodH[:, f, :], prod[:, :], ACT.Copy).then_inc(phi_ok, 1)

                    def pair_rows(j):
                        act.wait_ge(et_full, 2 * j + 1)
                        a.activation(xeT[:, :, :], etB[:, :].rearrange("p (c m) -> p c m", c=C), ACT.Copy).then_inc(et_taken, 1)

                    def pair_silu(j):
                        act.wait_ge(eg_full, j + 1)
                        if j:
                            act.wait_ge(eprod_ok, j)
                        a.activation(esilu[:, :], egB[:, 0:F], ACT.Silu).then_inc(esilu_ok, 1)

                    def pair_turned(j):
                        act.wait_ge(et_full, 2 * j + 2)
                        for c, (lo, n) in enumerate(FC):
                            ins = a.activation(epT[0:n, c, :], etB[0:n, c * P:(c + 1) * P], ACT.Copy)
                        ins.then_inc(et_taken, 1)

                    def pair_out(j):
                        act.wait_ge(ey_full, j + 1)
                        act.wait_ge(ye_free, j + 1)
                        a.activation(ye[:, :], eyB[:, :], ACT.Copy).then_inc(ye_ok, 1)

                    def combine_front(g, m):
                        i = g * GT + m
                        act.wait_ge(y_in[i % NY], 16 * TOP_K * (i // NY + 1))
                        act.wait_ge(y_used, i + 1)
                        act.wait_ge(x_acc, tile(len(PARTS) - 1, 0, 0) + 2)
                        a.activation(acc[i % NACC][:, :], yg[i % NY][:, 0, :], ACT.Copy, scale=slotw[:, i, 0:1]).then_inc(y_first, 1)

                    def pair_stage(u, k):
                        at = stage_after(u, k)
                        if at is None:
                            return
                        j, stage = at
                        if stage == 0:
                            pair_silu(j)
                        elif stage == 1:
                            pair_turned(j)
                        else:
                            if j >= 0:
                                pair_out(j)
                            if j + 1 < NP:
                                pair_rows(j + 1)

                    split_weights(0, 0)
                    split_group(0, 0)
                    split_weights(0, 1)
                    split_down(0)
                    act.wait_ge(shift_ok, 1)
                    a.activation(probs, probs, ACT.Exp).then_inc(ex_ok, 1)
                    a.activation(sigma[:, :], logits[:, :, E], ACT.Exp, scale=-1.0).then_inc(ex_ok, 1)

                    for u, (p, g) in enumerate(UNITS):
                        n, last = PARTS[p], g == NG - 1
                        for f in range(n):
                            gate_up(p, g, f)
                            if f == 0 and g == 0 and p:
                                for k in weights_ahead(u - 1)[2:]:
                                    split_weights(p, k)
                                split_down(p)
                            pair_stage(u, f)
                            for m in joins(u, f):
                                combine_front(g, m)
                            if last and p + 1 < len(PARTS) and 0 < f < n - 1:
                                split_weights(p + 1, f - 1)
                        if u + 1 < len(UNITS):
                            split_group(*UNITS[u + 1])
                            for k in weights_ahead(u)[:2]:
                                split_weights(p + 1, k)
                        for m in range(GT):
                            pair_stage(u, n + m)
                        for m in joins(u, 3) + joins(u, 4):
                            combine_front(g, m)

                @block.vector
                def _(dve):
                    v = nc.vector
                    own = Tally()
                    dve.sem_inc(silu_ok, 1)
                    dve.sem_inc(plo_ok, 1)
                    dve.sem_inc(x_acc, 2)

                    def link(ins):
                        ins.then_inc(dve_b, 1)
                        dve.wait_ge(dve_b, own.tick())

                    def over_e(ap):
                        return ap.rearrange("p (i a) -> p i a", a=1).to_broadcast([P, NT, E])

                    def over_k(ap):
                        return ap.rearrange("p i (a e) -> p i a e", a=1).to_broadcast([P, NT, TOP_K, E])

                    def shifted_logits():
                        for n in range(2):
                            dve.wait_ge(lg_full, n + 1)
                            link(v.tensor_copy(logits[:, n * BT:(n + 1) * BT, :].rearrange("p i r -> p (i r)"), bank[4 + n][:, 0:BT * R]))
                        link(v.tensor_reduce(rmax[:, :], logits[:, :, 0:E], AX.X, ALU.max))
                        v.tensor_tensor(probs, logits[:, :, 0:E], over_e(rmax[:, :]), ALU.subtract).then_inc(shift_ok, 1)

                    def top_experts():
                        dve.wait_ge(ex_ok, 2)
                        link(v.tensor_reduce(rmax[:, :], probs, AX.X, ALU.add))
                        link(v.reciprocal(rmax[:, :], rmax[:, :]))
                        link(v.tensor_tensor(probs, probs, over_e(rmax[:, :]), ALU.mult))
                        link(v.tensor_scalar(sigma[:, :], sigma[:, :], 1.0, None, ALU.add))
                        link(v.reciprocal(sigma[:, :], sigma[:, :]))
                        for i in range(NT):
                            v.max(top8[:, i, :], probs[:, i, :]).then_inc(dve_b, 1)
                            own.tick()
                        dve.wait_ge(dve_b, own.last())
                        for i in range(NT):
                            v.max_index(top_i[:, i, :], top8[:, i, :], probs[:, i, :]).then_inc(dve_b, 1)
                            own.tick()
                        dve.wait_ge(dve_b, own.last())

                    def experts_mask():
                        link(v.tensor_copy(top_e[:, :, :], top_i[:, :, 0:TOP_K]))
                        dve.wait_ge(rb_ok, 1)
                        for k in range(TOP_K):
                            v.tensor_tensor(onehot[:, :, k, :], top_e[:, :, k:k + 1].to_broadcast([P, NT, E]),
                                            iota_e[:, :].rearrange("p (a e) -> p a e", a=1).to_broadcast([P, NT, E]), ALU.is_equal).then_inc(dve_b, 1)
                            own.tick()
                        dve.wait_ge(dve_b, own.last())
                        link(v.tensor_reduce(mask.rearrange("p e i -> p i e"), onehot.rearrange("p i k e -> p i e k"), AX.X, ALU.add))

                    def flat_ei(ap):
                        return ap.rearrange("p e i -> p (e i)")

                    def pairs_before():
                        v.tensor_tensor_scan(flat_ei(upto), flat_ei(keep), flat_ei(mask), 0.0, ALU.mult, ALU.add).then_inc(mask_ok, 1)

                    def slots():
                        dve.wait_ge(pos_full, 1)
                        for k in range(TOP_K):
                            v.tensor_tensor(picked[:, :, k, :], bank[6][:, :].rearrange("p (i e) -> p i e", e=E), onehot[:, :, k, :], ALU.mult).then_inc(dve_b, 1)
                            own.tick()
                        dve.wait_ge(dve_b, own.last())
                        link(v.tensor_reduce(pos[:, :, :], picked, AX.X, ALU.add))
                        link(v.tensor_scalar(over[:, :, :], pos[:, :, :], float(CAP), None, ALU.is_ge))
                        link(v.scalar_tensor_tensor(idx_f[:, :, :], top_e[:, :, :], float(CAP), pos[:, :, :], ALU.mult, ALU.add))
                        link(v.scalar_tensor_tensor(idx_f[:, :, :], over[:, :, :], float(FAR), idx_f[:, :, :], ALU.mult, ALU.add))
                        link(v.tensor_copy(y_idx[:, :, :], idx_f[:, :, :]))
                        link(v.tensor_scalar(t_idx[:, :, :], top_i[:, :, 0:TOP_K], 1, None, ALU.bitwise_and))
                        link(v.tensor_copy(odd[:, :, :], t_idx[:, :, :]))
                        link(v.tensor_tensor(top_e[:, :, :], top_e[:, :, :], odd[:, :, :], ALU.subtract))
                        link(v.scalar_tensor_tensor(pos[:, :, :], odd[:, :, :], float(CAP), pos[:, :, :], ALU.mult, ALU.add))
                        link(v.tensor_scalar(pos[:, :, :], pos[:, :, :], float(NP), None, ALU.mult))
                        link(v.scalar_tensor_tensor(pos[:, :, :], top_e[:, :, :], 0.5, pos[:, :, :], ALU.mult, ALU.add))
                        link(v.scalar_tensor_tensor(pos[:, :, :], over[:, :, :], float(FAR), pos[:, :, :], ALU.mult, ALU.add))
                        link(v.tensor_copy(t_idx[:, :, :], pos[:, :, :]))
                        link(v.tensor_reduce(rmax[:, :], top8[:, :, 0:TOP_K], AX.X, ALU.add))
                        link(v.reciprocal(rmax[:, :], rmax[:, :]))
                        link(v.tensor_tensor(slotw[:, :, :], top8[:, :, 0:TOP_K],
                                             rmax[:, :].rearrange("p (i a) -> p i a", a=1).to_broadcast([P, NT, TOP_K]), ALU.mult))
                        link(v.tensor_scalar(over[:, :, :], over[:, :, :], -1.0, 1.0, ALU.mult, ALU.add))
                        v.tensor_tensor(slotw[:, :, :], slotw[:, :, :], over[:, :, :], ALU.mult).then_inc(route_ok, 1)


                    def lo_weights(p, f):
                        n, at = PARTS[p], slice(f * P, (f + 1) * P)
                        dve.wait_ge(whi_ok, splits(p, f + 1))
                        if f < n:
                            v.tensor_tensor(wguL[:, :, :, at], wguN[:, :, :, at],
                                            wguH[:, :, :, at].bitcast(F32), ALU.subtract).then_inc(wlo_ok, 1)
                        else:
                            v.tensor_tensor(wdL[:, 0:n, :], wdN[:, 0:n, :], wdH[:, 0:n, :].bitcast(F32), ALU.subtract).then_inc(wlo_ok, 1)

                    def lo_group(p, g, chunks=range(C)):
                        for c in chunks:
                            dve.wait_ge(xhi_ok, (p * NG + g) * C + c + 1)
                            v.tensor_tensor(xsL[:, c, :], h2T[:, c, g * GW:(g + 1) * GW], xsH[:, c, :].bitcast(F32), ALU.subtract).then_inc(xlo_ok, 1)

                    def gate_up(p, g, f):
                        n = chunk(p, g, f)
                        dve.wait_ge(silu_ok, n + 2)
                        dve.wait_ge(u_full, n + 2)
                        dve.wait_ge(plo_ok, n + 1)
                        v.tensor_tensor(prod[:, :], uB[:, :], silu[:, :], ALU.mult).then_inc(prod_ok, 1)
                        dve.wait_ge(phi_ok, n + 1)
                        v.tensor_tensor(prodL[:, f, :], prod[:, :], prodH[:, f, :].bitcast(F32), ALU.subtract).then_inc(plo_ok, 1)

                    def down(p, g, m):
                        n, i = tile(p, g, m), g * GT + m
                        dve.wait_ge(d_full[m % 2], n // 2 + 1)
                        if p == len(PARTS) - 1:
                            dve.wait_ge(y_read, i + 1)
                            dve.wait_ge(x_acc, tile(p, 0, 0) + 2)
                            v.scalar_tensor_tensor(acc[i % NACC][:, :], dB[m % 2][:, :], sigma[:, i:i + 1], acc[i % NACC][:, :],
                                                   ALU.mult, ALU.add).then_inc(d_used[m % 2], 1)
                            dve.wait_ge(d_used[m % 2], n // 2 + 2)
                            v.tensor_tensor(acc[i % NACC][:, :], acc[i % NACC][:, :], gate_b[:, i // BT, :], ALU.mult).then_inc(y_sum, 1)
                            if g == NG - 1:
                                dve.wait_ge(y_sum, i + 1)
                                v.tensor_tensor(xres[:, i, :], xres[:, i, :], acc[i % NACC][:, :], ALU.add).then_inc(final_ok, 1)
                            return
                        dve.wait_ge(x_acc, n + 1)
                        v.scalar_tensor_tensor(ytmp[:, m % 2, :], dB[m % 2][:, :], sigma[:, i:i + 1], gate_b[:, i // BT, :],
                                               ALU.mult, ALU.mult).then_inc(d_used[m % 2], 1)
                        dve.wait_ge(d_used[m % 2], n // 2 + 2)
                        v.tensor_tensor(xres[:, i, :], xres[:, i, :], ytmp[:, m % 2, :], ALU.add).then_inc(x_acc, 1)

                    def pair_prod(j):
                        dve.wait_ge(esilu_ok, j + 1)
                        if j:
                            dve.wait_ge(et_full, 2 * j)
                        v.tensor_tensor(eprod[:, :], euB[:, 0:F], esilu[:, :], ALU.mult).then_inc(eprod_ok, 1)

                    def combine(g, m):
                        i = g * GT + m
                        dve.wait_ge(y_in[i % NY], 16 * TOP_K * (i // NY + 1))
                        dve.wait_ge(y_first, i + 1)
                        for k in range(1, TOP_K):
                            ins = v.scalar_tensor_tensor(acc[i % NACC][:, :], yg[i % NY][:, k, :], slotw[:, i, k:k + 1], acc[i % NACC][:, :], ALU.mult, ALU.add)
                            if k < TOP_K - 1:
                                link(ins)
                            else:
                                ins.then_inc(y_read, 1)

                    def pair_stage(u, k):
                        at = stage_after(u, k)
                        if at is not None and at[1] == 0:
                            pair_prod(at[0])

                    lo_weights(0, 0)
                    lo_group(0, 0)
                    shifted_logits()
                    lo_weights(0, 1)
                    gate_up(0, 0, 0)
                    top_experts()
                    gate_up(0, 0, 1)
                    experts_mask()
                    for u, (p, g) in enumerate(UNITS):
                        n, last = PARTS[p], g == NG - 1
                        if u:
                            for f in range(n):
                                gate_up(p, g, f)
                                if f == 0 and g == 0:
                                    for k in weights_ahead(u - 1)[2:]:
                                        lo_weights(p, k)
                                    lo_weights(p, n)
                                pair_stage(u, f)
                                for m in joins(u, f):
                                    combine(g, m)
                                if last and p + 1 < len(PARTS) and 0 < f < n - 1:
                                    lo_weights(p + 1, f - 1)
                        ahead = u > 0 and u + 1 < len(UNITS)
                        if ahead:
                            lo_group(*UNITS[u + 1], chunks=range(0, C // 2))
                        down(p, g, 0)
                        pair_stage(u, n)
                        down(p, g, 1)
                        pair_stage(u, n + 1)
                        if u == 0:
                            pairs_before()
                        if weights_ahead(u):
                            lo_weights(p + 1, weights_ahead(u)[0])
                        for m in joins(u, 3):
                            combine(g, m)
                        down(p, g, 2)
                        pair_stage(u, n + 2)
                        if ahead:
                            lo_group(*UNITS[u + 1], chunks=range(C // 2, C))
                        for m in joins(u, 4):
                            combine(g, m)
                        down(p, g, 3)
                        pair_stage(u, n + 3)
                        if weights_ahead(u):
                            lo_weights(p + 1, weights_ahead(u)[1])
                        if u == 0:
                            slots()

                @block.tensor
                def _(pe):
                    mm = nc.tensor
                    for s_ in (d_used0, d_used1):
                        pe.sem_inc(s_, 1)
                    for n in range(2):
                        for i in range(BT):
                            t = n * BT + i
                            ins = mm.transpose(bank[4 + n][:, i * R:(i + 1) * R], logT[:, t * P:(t + 1) * P], ident[0:R, 0:R])
                        ins.then_inc(lg_full, 1)
                    def gate_up(p, g, f):
                        n = chunk(p, g, f)
                        for w, (bk, free, full) in enumerate(((gB, silu_ok, g_full), (uB, prod_ok, u_full))):
                            pe.wait_ge(free, n + 1)
                            k = 0
                            for c in range(C):
                                if g == 0 and w == 0 and c == 0:
                                    pe.wait_ge(wlo_ok, splits(p, f + 1) - (p > 0))
                                if f == 0 and w == 0:
                                    u = p * NG + g
                                    if u == 1:
                                        pe.wait_ge(pool_lo, 1 + c + 1)
                                    else:
                                        pe.wait_ge(xlo_ok, (u - (u > 1)) * C + c + 1)
                                at = slice(f * P, (f + 1) * P)
                                for l, r in ((wguH, xsH), (wguL, xsH), (wguH, xsL)):
                                    ins = mm.matmul(bk[:, :], l[:, w, c, at], r[:, c, :], start=(k == 0), stop=(k == 3 * C - 1))
                                    k += 1
                            ins.then_inc(full, 1)

                    def down_chunks(p, g, m, fs):
                        n, nf = tile(p, g, m), PARTS[p]
                        for f in fs:
                            if f == 0:
                                pe.wait_ge(d_used[m % 2], n // 2 + 1)
                            if m < 2:
                                pe.wait_ge(plo_ok, chunk(p, g, f) + 2)
                            for k, (l, r) in enumerate(((prodH, wdH), (prodH, wdL), (prodL, wdH))):
                                ins = mm.matmul(dB[m % 2][:, :], l[:, f, m * P:(m + 1) * P], r[:, f, :],
                                                start=(f == 0 and k == 0), stop=(f == nf - 1 and k == 2))
                            if f == nf - 1:
                                ins.then_inc(d_full[m % 2], 1)

                    def down(p, g, m):
                        last = PARTS[p] - 1
                        if m == 0:
                            down_chunks(p, g, 0, range(last))
                            down_chunks(p, g, 1, range(last))
                        down_chunks(p, g, m, [last] if m < 2 else range(last + 1))

                    def pair_rows(j):
                        pe.wait_ge(xg_in, 16 * (j + 1))
                        if j:
                            pe.wait_ge(et_taken, 2 * j)
                        rows_v = xg[:, :].rearrange("s (p c) -> s c p", c=C)
                        for c in range(C):
                            ins = mm.transpose(etB[:, c * P:(c + 1) * P], rows_v[:, c, :], ident[:, :])
                        ins.then_inc(et_full, 1)

                    def pair_gate_up(j):
                        pe.wait_ge(gu_in, 64 * (j + 1))
                        pe.wait_ge(et_taken, 2 * j + 1)
                        if j:
                            pe.wait_ge(eprod_ok, j)
                        for c in range(C):
                            for w, bk in enumerate((egB, euB)):
                                for e in range(2):
                                    half = slice(e * CAP, (e + 1) * CAP)
                                    ins = mm.matmul(bk[half, 0:F], xeT[:, c, half], egu[:, e, w, c, :], start=(c == 0), stop=(c == C - 1))
                        ins.then_inc(eg_full, 1)

                    def pair_turned(j):
                        pe.wait_ge(eprod_ok, j + 1)
                        for c, (lo, n) in enumerate(FC):
                            ins = mm.transpose(etB[0:n, c * P:(c + 1) * P], eprod[:, lo:lo + n], ident[:, :])
                        ins.then_inc(et_full, 1)

                    def pair_down(j):
                        pe.wait_ge(dn_in, 64 * (j + 1))
                        pe.wait_ge(et_taken, 2 * j + 2)
                        if j:
                            pe.wait_ge(ye_ok, j)
                        for c, (lo, n) in enumerate(FC):
                            for e in range(2):
                                half = slice(e * CAP, (e + 1) * CAP)
                                ins = mm.matmul(eyB[half, :], epT[0:n, c, half], ed[0:n, e, c, :], start=(c == 0), stop=(c == len(FC) - 1))
                        ins.then_inc(ey_full, 1)

                    def pair_stage(u, k):
                        at = stage_after(u, k)
                        if at is None:
                            return
                        j, stage = at
                        if stage == 0:
                            pair_gate_up(j)
                        elif stage == 1:
                            pair_turned(j)
                        else:
                            if j >= 0:
                                pair_down(j)
                            if j + 1 < NP:
                                pair_rows(j + 1)

                    def positions():
                        pe.wait_ge(mask_ok, 1)
                        counts = bank[6][:, :].rearrange("p (i e) -> p i e", e=E)
                        mm.matmul(counts, tri[:, :], mask.rearrange("p e i -> p i e"), start=True, stop=False)
                        mm.matmul(counts, ones[:, :], upto.rearrange("p e i -> p i e"), start=False, stop=True).then_inc(pos_full, 1)

                    for u, (p, g) in enumerate(UNITS):
                        n = PARTS[p]
                        for f in range(n):
                            gate_up(p, g, f)
                            pair_stage(u, f)
                        if g == 0:
                            if p == 0:
                                pe.wait_ge(pool_lo, 1)
                            else:
                                pe.wait_ge(wlo_ok, splits(p, n + 1) - 1)
                        for m in range(GT):
                            down(p, g, m)
                            pair_stage(u, n + m)
                        if u == 0:
                            positions()


_INS = ['L0_attn_x', 'L0_attn_Wk', 'L0_attn_Wv', 'L0_attn_Wo', 'L0_attn_Wts', 'L0_attn_gate', 'L0_attn_time_decay',
        'L0_attn_time_first', 'L0_attn_ln_w', 'L0_attn_ln_b', 'L0_ffn_Wr', 'L0_ffn_Wg', 'L0_ffn_Wu', 'L0_ffn_Wd',
        'L0_ffn_Wsg', 'L0_ffn_Wsu', 'L0_ffn_Wsd', 'L0_ffn_Wse', 'L0_c', 'L0_wmod']
_OUTS = [((2, 1024, 512), 'float32')]


def kernel(**inputs):
    import numpy as _np
    import concourse.bacc as _bacc
    from concourse import mybir as _mybir
    from concourse.bass_utils import run_bass_kernel_spmd as _run

    nc = _bacc.Bacc("TRN2", target_bir_lowering=False, num_devices=1)
    arrays, args = {}, []
    for name in _INS:
        a = _np.ascontiguousarray(inputs[name])
        arrays[f"in_{name}_dram"] = a
        args.append(nc.dram_tensor(f"in_{name}_dram", a.shape, _mybir.dt.from_np(a.dtype), kind="ExternalInput").ap())
    for i, (shape, dtype) in enumerate(_OUTS):
        dt = _mybir.dt.from_np(_np.dtype(dtype))
        args.append(nc.dram_tensor(f"out_{i}_dram", shape, dt, kind="ExternalOutput").ap())
    build(nc, *args)
    r = _run(nc, [arrays], core_ids=[0])
    got = tuple(r.results[0][f"out_{i}_dram"] for i in range(len(_OUTS)))
    return got[0]
```
